# Optimizing a Trainium2 kernel written in Bass

```python
import numpy as np
import jax
import jax.numpy as jnp

def _softmax(x, axis=-1):
    return jax.nn.softmax(x, axis=axis)

def _gelu(x):
    return jax.nn.gelu(x, approximate=True)

def _silu(x):
    return jax.nn.silu(x)

def _sigmoid(x):
    return jax.nn.sigmoid(x)

def _layernorm(x, axis=-1, eps=1e-05):
    m = jnp.mean(x, axis=axis, keepdims=True)
    v = jnp.var(x, axis=axis, keepdims=True)
    return (x - m) / jnp.sqrt(v + eps)

def _scatter_add(tgt, idx, src, axis=0):
    return tgt.at[idx].add(src)

def _segment_sum(src, seg, n):
    return jax.ops.segment_sum(src, seg, n)
kernel_name = 'mk_cond_seq_d2_seqx_r4_937145'

def setup_inputs(seed: int=0):
    np.random.seed(seed)
    _w = jnp.asarray

    def _rec_inputs():
        import jax
        import jax.numpy as jnp
        _rk = jax.random.key(seed)
        x = -0.0003482 + 1 * jax.random.normal(jax.random.fold_in(_rk, 1), (2, 1024, 288), jnp.float32)
        _lenS = 1024 - jax.random.randint(jax.random.fold_in(_rk, 7), (2,), 0, max(1, 1024 // 4) + 1, jnp.int32)
        _lenS2 = 1024 - jax.random.randint(jax.random.fold_in(_rk, 8), (2,), 0, max(1, 1024 // 4) + 1, jnp.int32)
        cond_1152 = 0.00257642 + 1.0011 * jax.random.normal(jax.random.fold_in(_rk, 11), (2, 288), jnp.float32)
        return (x, cond_1152)
    x, cond_1152 = _rec_inputs()

    def _L0_cond_setup():
        import jax, jax.numpy as jnp
        import numpy as np
        from jax.scipy.linalg import expm
        N, D, COND_DIM = (288, 64, 288)
        B, T = (16, 256)

        def _rotation(cond, W, b):
            v = jax.nn.silu(cond) @ W.T + b
            iu, ju = jnp.triu_indices(D, k=1)
            A = jnp.zeros((cond.shape[0], D, D), dtype=v.dtype)
            A = A.at[:, iu, ju].set(v).at[:, ju, iu].set(-v)
            return expm(A)
        key = jax.random.key(seed)
        k1, k2, k3, k4, k5 = jax.random.split(key, 5)
        x = jax.random.normal(k1, (B, T, N), dtype=jnp.float32)
        cond = jax.random.normal(k2, (B, COND_DIM), dtype=jnp.float32)
        P = jax.random.normal(k3, (N, D), dtype=jnp.float32)
        n_skew = D * (D - 1) // 2
        bound = 1.0 / np.sqrt(COND_DIM)
        W = jax.random.uniform(k4, (n_skew, COND_DIM), minval=-bound, maxval=bound, dtype=jnp.float32)
        b = jax.random.uniform(k5, (n_skew,), minval=-bound, maxval=bound, dtype=jnp.float32)
        return {'x': x, 'cond': cond, 'P': P, 'W': W, 'b': b}
    _L0_cond_all = _L0_cond_setup()
    _L0_cond_in = {k: v for k, v in _L0_cond_all.items() if k in ('P', 'W', 'b')}
    del _L0_cond_all

    def _L1_cond_setup():
        import jax, jax.numpy as jnp
        import numpy as np
        H = 288
        NH = 16
        HD = H // NH
        MLP = int(H * 4.0)
        EPS = 1e-06

        def _ln(z, scale=None):
            m = jnp.mean(z, axis=-1, keepdims=True)
            v = jnp.mean(jnp.square(z - m), axis=-1, keepdims=True)
            y = (z - m) * jax.lax.rsqrt(v + EPS)
            if scale is not None:
                y = y * scale
            return y
        key = jax.random.key(seed)
        ks = jax.random.split(key, 16)
        B, N = (16, 256)
        x = jax.random.normal(ks[0], (B, N, H), dtype=jnp.float32)
        c = jax.random.normal(ks[1], (B, H), dtype=jnp.float32)

        def xav(k, fan_in, fan_out):
            lim = np.sqrt(6.0 / (fan_in + fan_out))
            return jax.random.uniform(k, (fan_in, fan_out), jnp.float32, -lim, lim)
        w_mod = 0.02 * jax.random.normal(ks[2], (H, 6 * H), dtype=jnp.float32)
        b_mod = 0.02 * jax.random.normal(ks[3], (6 * H,), dtype=jnp.float32)
        w_qkv = xav(ks[4], H, 3 * H)
        b_qkv = jnp.zeros((3 * H,), jnp.float32)
        g_q = jnp.ones((HD,), jnp.float32)
        g_k = jnp.ones((HD,), jnp.float32)
        w_proj = xav(ks[5], H, H)
        b_proj = jnp.zeros((H,), jnp.float32)
        w1 = xav(ks[6], H, MLP)
        b1 = jnp.zeros((MLP,), jnp.float32)
        w2 = xav(ks[7], MLP, H)
        b2 = jnp.zeros((H,), jnp.float32)
        return dict(x=x, c=c, w_mod=w_mod, b_mod=b_mod, w_qkv=w_qkv, b_qkv=b_qkv, g_q=g_q, g_k=g_k, w_proj=w_proj, b_proj=b_proj, w1=w1, b1=b1, w2=w2, b2=b2)
    _L1_cond_all = _L1_cond_setup()
    _L1_cond_in = {k: v for k, v in _L1_cond_all.items() if k in ('w_mod', 'b_mod', 'w_qkv', 'b_qkv', 'g_q', 'g_k', 'w_proj', 'b_proj', 'w1', 'b1', 'w2', 'b2')}
    del _L1_cond_all
    return {'x': x, 'cond_1152': cond_1152, 'L0_cond_P': _L0_cond_in['P'], 'L0_cond_W': _L0_cond_in['W'], 'L0_cond_b': _L0_cond_in['b'], 'L1_cond_w_mod': _L1_cond_in['w_mod'], 'L1_cond_b_mod': _L1_cond_in['b_mod'], 'L1_cond_w_qkv': _L1_cond_in['w_qkv'], 'L1_cond_b_qkv': _L1_cond_in['b_qkv'], 'L1_cond_g_q': _L1_cond_in['g_q'], 'L1_cond_g_k': _L1_cond_in['g_k'], 'L1_cond_w_proj': _L1_cond_in['w_proj'], 'L1_cond_b_proj': _L1_cond_in['b_proj'], 'L1_cond_w1': _L1_cond_in['w1'], 'L1_cond_b1': _L1_cond_in['b1'], 'L1_cond_w2': _L1_cond_in['w2'], 'L1_cond_b2': _L1_cond_in['b2']}

def reference(x, cond_1152, L0_cond_P, L0_cond_W, L0_cond_b, L1_cond_w_mod, L1_cond_b_mod, L1_cond_w_qkv, L1_cond_b_qkv, L1_cond_g_q, L1_cond_g_k, L1_cond_w_proj, L1_cond_b_proj, L1_cond_w1, L1_cond_b1, L1_cond_w2, L1_cond_b2):
    import jax
    import jax.numpy as jnp

    def _L0_cond_ref(x, cond, P, W, b):
        import jax, jax.numpy as jnp
        import numpy as np
        from jax.scipy.linalg import expm
        N, D, COND_DIM = (288, 64, 288)
        B, T = (16, 256)

        def _rotation(cond, W, b):
            v = jax.nn.silu(cond) @ W.T + b
            iu, ju = jnp.triu_indices(D, k=1)
            A = jnp.zeros((cond.shape[0], D, D), dtype=v.dtype)
            A = A.at[:, iu, ju].set(v).at[:, ju, iu].set(-v)
            return expm(A)
        U, _ = jnp.linalg.qr(P)
        R = _rotation(cond, W, b)
        z = jnp.einsum('btn,nd->btd', x, U)
        z_rot = jnp.einsum('btd,bde->bte', z, R)
        x_rot = x + jnp.einsum('btd,nd->btn', z_rot - z, U)
        return x_rot

    def _L1_cond_ref(x, c, w_mod, b_mod, w_qkv, b_qkv, g_q, g_k, w_proj, b_proj, w1, b1, w2, b2):
        import jax, jax.numpy as jnp
        import numpy as np
        H = 288
        NH = 16
        HD = H // NH
        MLP = int(H * 4.0)
        EPS = 1e-06

        def _ln(z, scale=None):
            m = jnp.mean(z, axis=-1, keepdims=True)
            v = jnp.mean(jnp.square(z - m), axis=-1, keepdims=True)
            y = (z - m) * jax.lax.rsqrt(v + EPS)
            if scale is not None:
                y = y * scale
            return y
        B, N, _ = x.shape
        mod = jax.nn.swish(c) @ w_mod + b_mod
        sh_msa, sc_msa, g_msa, sh_mlp, sc_mlp, g_mlp = jnp.split(mod, 6, axis=1)
        xn = _ln(x) * (1 + sc_msa[:, None, :]) + sh_msa[:, None, :]
        qkv = xn @ w_qkv + b_qkv
        qkv = qkv.reshape(B, N, 3, NH, HD).transpose(2, 0, 3, 1, 4)
        q, k, v = (qkv[0], qkv[1], qkv[2])
        q = _ln(q, g_q)
        k = _ln(k, g_k)
        attn = jax.nn.softmax(jnp.einsum('bhqd,bhkd->bhqk', q, k) * HD ** (-0.5), axis=-1)
        o = jnp.einsum('bhqk,bhkd->bhqd', attn, v)
        o = o.transpose(0, 2, 1, 3).reshape(B, N, H) @ w_proj + b_proj
        x = x + g_msa[:, None, :] * o
        xn2 = _ln(x) * (1 + sc_mlp[:, None, :]) + sh_mlp[:, None, :]
        h = jax.nn.gelu(xn2 @ w1 + b1, approximate=True)
        x = x + g_mlp[:, None, :] * (h @ w2 + b2)
        return x
    x = _L0_cond_ref(x, cond_1152, L0_cond_P, L0_cond_W, L0_cond_b)
    x = _L1_cond_ref(x, cond_1152, L1_cond_w_mod, L1_cond_b_mod, L1_cond_w_qkv, L1_cond_b_qkv, L1_cond_g_q, L1_cond_g_k, L1_cond_w_proj, L1_cond_b_proj, L1_cond_w1, L1_cond_b1, L1_cond_w2, L1_cond_b2)
    return x

_drawn_inputs = setup_inputs


def setup_inputs(seed=0):
    import zlib

    import numpy as np

    out = dict(_drawn_inputs(seed))
    spreads = {'L1_cond_b_qkv': (0.0, 0.395),
     'L1_cond_g_q': (1.0, 0.6),
     'L1_cond_g_k': (1.0, 0.6),
     'L1_cond_b_proj': (0.0, 0.408),
     'L1_cond_b1': (0.0, 0.489),
     'L1_cond_b2': (0.0, 0.412)}
    factors = {'L1_cond_b_mod': 5.236}
    for name, (base, spread) in spreads.items():
        noise = np.random.default_rng([zlib.crc32(name.encode()), seed]).standard_normal(out[name].shape)
        drawn = base * np.exp(spread * noise) if base else spread * noise
        out[name] = jnp.asarray(drawn.astype(out[name].dtype))
    for name, factor in factors.items():
        out[name] = (out[name] * factor).astype(out[name].dtype)
    return out
```

```python
from contextlib import ExitStack

import numpy as np

import concourse.bass as bass
from concourse import mybir

F32 = mybir.dt.float32
F16 = mybir.dt.float16
ALU = mybir.AluOpType
ACT = mybir.ActivationFunctionType
AX = mybir.AxisListType

B, T, H = 2, 1024, 288
D = 64
NH, HD = 16, 18
MLP = 4 * H
P128 = 128
TILES = T // P128
NT = B * TILES
KC = 96
NC = H // KC
HG = 4
GROUPS = B * NH // HG
GW = HG * HD
PARTS = 4
EPS = 1e-6
LAG = 8
SQUARINGS = 8
TAYLOR = 6
ROUNDS = SQUARINGS + TAYLOR
FF = MLP // P128
CH = 256
CHUNKS = B * T // CH
SH_MSA, SC_MSA, G_MSA, SH_MLP, SC_MLP, G_MLP = range(6)

T_AFTER = {7: 0, 9: 1, 11: 2, 13: 3}
O_AFTER = 3


def ring_units():
    at, pairs = 0, []
    for v in range(16):
        units = [("S", 2 * v, at), ("S", 2 * v + 1, at + 1)]
        at += 2
        if v == O_AFTER:
            units.append(("O", 0, at))
            at += 1
        if v in T_AFTER:
            units.append(("T", T_AFTER[v], at))
            at += 1
        pairs.append(units)
    return pairs, -(-at // 3) * 3


RING_PAIRS, RING_LEN = ring_units()
RING_AT = {p: (kind, n) for pair in RING_PAIRS for kind, n, p in pair}


def build(nc, x, cond_t, P, P_t, W_fold, b_fold, w_mod, b_mod_cols, b_mod, w_qkv, b_qkv, g_q, g_k,
          w_proj, b_proj, w1, b1_cols, w2, b2, out):
    with ExitStack() as ctx:
        def sb(name, shape, dt=F32):
            return ctx.enter_context(nc.sbuf_tensor(name, shape, dt))

        def sem(name):
            return ctx.enter_context(nc.semaphore(name))

        ps = ctx.enter_context(nc.psum_tensor("ps", [P128, 8, 512], F32))

        ident = sb("ident", [P128, P128])
        ident16 = sb("ident16", [P128, P128], F16)
        neg_half = sb("neg_half", [P128, 32])
        x_sb = sb("x_sb", [P128, NT, H])
        o_tok = sb("o_tok", [P128, GROUPS, TILES, GW])
        w_proj_sb = sb("w_proj_sb", [KC, NC, H])
        mod_col = sb("mod_col", [KC, 6, NC, B])
        gate = sb("gate", [P128, 2, B, H])
        gate_bias = sb("gate_bias", [P128, 2, B, H])
        b1_sb = sb("b1_sb", [P128, FF])
        stats = sb("stats", [P128, 6])
        mean_var = sb("mean_var", [P128, 2, 2])
        var_eps = sb("var_eps", [P128, 2])
        rstd = sb("rstd", [P128, 2])
        xn = sb("xn", [P128, H])
        x_cur = sb("x_cur", [P128, 2, H])
        eps_layer = sb("eps_layer", [P128, 1])
        eps_head = sb("eps_head", [P128, 32])
        bias_row = sb("bias_row", [P128, 3 * H])
        g_row = sb("g_row", [P128, H])
        qkn = sb("qkn", [P128, GROUPS, TILES, 2, HG, HD])
        v_all = sb("v_all", [P128, GROUPS, TILES, HG, HD])

        arena1 = sb("arena1", [P128, 8192])
        w_qkv_sb = arena1[0:KC, 0:NC * 3 * H].rearrange("p (c n) -> p c n", c=NC)
        z0_all = arena1[0:D, 2592:2592 + NT * P128].rearrange("p (t k) -> p t k", t=NT)
        xT = arena1[0:KC, 4640:4640 + 2 * NC * P128].rearrange("p (j c k) -> p j c k", j=2, c=NC)
        qk_c = arena1[:, 5408:5408 + 2 * H].rearrange("p (a f) -> p a f", a=2)
        qk_sq = arena1[:, 5984:5984 + 2 * H].rearrange("p (a f) -> p a f", a=2)
        k_g = arena1[:, 6560:6560 + H]
        head_ssq = arena1[:, 6848:6848 + 32]
        head_var = arena1[:, 6880:6880 + 32]
        head_rstd = arena1[:, 6912:6912 + 32]
        z_slot = arena1[0:D, 6944:6944 + 2 * P128].rearrange("p (j k) -> p j k", j=2)
        Y = arena1[0:D, 7200:7200 + B * H].rearrange("p (b f) -> p b f", b=B)
        prob = arena1[:, :].rearrange("p (s q) -> p s q", s=8)

        arena2 = sb("arena2", [P128, 11328])
        Wf = arena2[0:KC, 0:NC * 2048].rearrange("p (c n) -> p c n", c=NC)
        w_mod_sb = arena2[0:KC, 6144:6144 + NC * 6 * H].rearrange("p (c n) -> p c n", c=NC)
        qk_op = arena2[0:PARTS * HD, 0:8192].bitcast(F16).rearrange("p (s a h t) -> p s a h t", s=2, a=2, h=HG)
        qk_split = arena2[:, 8192:10496].bitcast(F16).rearrange("p (t a h r d) -> p t a h r d", t=TILES, a=2, h=HG, r=PARTS)
        hid = arena2[:, 0:FF * CH].rearrange("p (m t) -> p m t", m=FF)
        xn2T = arena2[0:KC, 2304:2304 + NC * CH].rearrange("p (c t) -> p c t", c=NC)
        oT2 = arena2[0:KC, 3072:3072 + 2 * NC * P128].rearrange("p (j c t) -> p j c t", j=2, c=NC)
        o_row = arena2[:, 3840:3840 + 2 * H].rearrange("p (j f) -> p j f", j=2)
        x_gb = arena2[:, 4416:4416 + 2 * H].rearrange("p (j f) -> p j f", j=2)
        x_gb2 = arena2[:, 4992:4992 + 2 * H].rearrange("p (j f) -> p j f", j=2)
        gated = arena2[:, 5568:5568 + H]
        gated2 = arena2[:, 5856:5856 + 2 * H].rearrange("p (j f) -> p j f", j=2)
        y_out = arena2[:, 6720:6720 + 2 * H].rearrange("p (j f) -> p j f", j=2)
        qk_mem = qkn[:, :, :, :, :, :].rearrange("p g t a h d -> p (g t a h d)")
        half_qk = GROUPS // 2 * TILES * 2 * GW
        w1_sb = qk_mem[0:KC, 0:NC * MLP].rearrange("p (c n) -> p c n", c=NC)
        w2_sb = qk_mem[:, half_qk:half_qk + FF * H].rearrange("p (m n) -> p m n", m=FF)

        v_op = sb("v_op", [P128, 2, TILES, HG, 32])
        o_acc = sb("o_acc", [P128, T])
        den_inv = sb("den_inv", [P128, TILES, HG])

        arena3 = o_tok[0:D, :, :, :].rearrange("p g t f -> p (g t f)")
        elim_mask = arena3[:, 0:D * D].rearrange("p (k i) -> p k i", k=D)
        flip = sb("flip", [D, D])
        neg_i = sb("neg_i", [32, 32])
        scaled_i = v_op[0:D, 0, 0:5, :, :].rearrange("p j a b -> p (j a b)")[:, 0:5 * D].rearrange("p (j i) -> p j i", j=5)
        ident4 = v_op[0:D, 1, 0:2, :, :].rearrange("p j a b -> p (j a b)").rearrange("p (j i) -> p j i", j=4)
        fold_up = sb("fold_up", [32, D])
        fold_low = sb("fold_low", [32, D])
        P_sb = sb("P_sb", [KC, NC, D])
        P_top = sb("P_top", [D, D])
        Pt_sb = sb("Pt_sb", [D, H])
        cond_sb = sb("cond_sb", [KC, NC, B])
        ex = sb("ex", [KC, NC, B])
        silu = sb("silu", [KC, NC, 32])
        bf = sb("bf", [32, D])
        z_row = sb("z_row", [D, P128])
        z_col = sb("z_col", [D, D])
        z_rcp = sb("z_rcp", [D, 1])
        diag = sb("diag", [D, 1])
        diag_rs = sb("diag_rs", [D, 1])
        junk = sb("junk", [D, D])
        R_half = sb("R_half", [D, D])
        pivot_half = sb("pivot_half", [D, 1])
        pivot_rcp = sb("pivot_rcp", [D, 1])
        signs = sb("signs", [D, D])
        w_row = sb("w_row", [D, 2, D])
        m_col = sb("m_col", [D, 2, D])
        sign_of = sb("sign_of", [D, 1])
        Winv = sb("Winv", [D, D])
        head_mem = o_acc[:, :]
        v_sb = head_mem[:, 0:512]
        fold = head_mem[0:32, 512:640].rearrange("p (b j) -> p b j", b=B)
        fold_b = head_mem[0:32, 640:768].rearrange("p (b j) -> p b j", b=B)
        v_up = head_mem[0:32, 768:896].rearrange("p (b j) -> p b j", b=B)
        v_low = head_mem[0:32, 896:1024].rearrange("p (b j) -> p b j", b=B)
        lowT = arena3[:, 4096:4224].rearrange("p (b j) -> p b j", b=B)
        neg_lowT = arena3[:, 4224:4288].rearrange("p (b j) -> p b j", b=B)
        skew = qk_mem[0:D, 0:256].rearrange("p (m j) -> p m j", m=4)
        X = qk_mem[0:D, 256:768].rearrange("p (s m j) -> p s m j", s=2, m=4)
        FW = qk_mem[0:D, 768:896].rearrange("p (b j) -> p b j", b=B)
        Kt = qk_mem[0:D, 896:1024].rearrange("p (b j) -> p b j", b=B)
        mod_row = qk_mem[:, 1024:1024 + 2 * H].rearrange("p (r f) -> p r f", r=2)
        bm_col = qk_mem[0:KC, 1600:1618].rearrange("p (s c) -> p s c", s=6)
        bm_row = qk_mem[:, 1632:1632 + 2 * H].rearrange("p (r f) -> p r f", r=2)
        bo_row = qk_mem[:, 2208:2208 + 2 * H].rearrange("p (r f) -> p r f", r=2)
        gq_row = qk_mem[:, 2784:2784 + H]
        gk_row = qk_mem[:, 3072:3072 + H]
        w_sum = qk_mem[0:KC, 3360:3360 + NC * 32].rearrange("p (c h) -> p c h", c=NC)
        b_sum = qk_mem[:, 3456:3456 + 32]
        xT_head = qk_mem[0:KC, 3584:3584 + 2 * NC * P128].rearrange("p (s c k) -> p s c k", s=2, c=NC)
        v_dram = nc.dram_tensor("v_scratch", [B, 4, 512], F32).ap()

        p_loaded, cond_loaded, x_loaded, wf_loaded = sem("p_loaded"), sem("cond_loaded"), sem("x_loaded"), sem("wf_loaded")
        wqkv_loaded, mod_loaded, row_loaded, proj_loaded = sem("wqkv_loaded"), sem("mod_loaded"), sem("row_loaded"), sem("proj_loaded")
        w1_loaded, w2_loaded = sem("w1_loaded"), sem("w2_loaded")
        v_stored, fold_loaded = sem("v_stored"), sem("fold_loaded")
        const_step, ident_ready, mask_ready, const_ready = sem("const_step"), sem("ident_ready"), sem("mask_ready"), sem("const_ready")
        z_ready, m_ready, n_ready = sem("z_ready"), sem("m_ready"), sem("n_ready")
        zrcp_ready, zrow_ready, zcol_ready = sem("zrcp_ready"), sem("zrow_ready"), sem("zcol_ready")
        diag_ready, diagrs_ready, r_ready = sem("diag_ready"), sem("diagrs_ready"), sem("r_ready")
        sign_step, pivot_ready, prcp_ready = sem("sign_step"), sem("pivot_ready"), sem("prcp_ready")
        w_ready, c_ready, sign_ready, winv_ready = sem("w_ready"), sem("c_ready"), sem("sign_ready"), sem("winv_ready")
        silu_step, silu_ready = sem("silu_step"), sem("silu_ready")
        v_ready, vsb_ready, foldb_ready, vparts_ready = sem("v_ready"), sem("vsb_ready"), sem("foldb_ready"), sem("vparts_ready")
        lowT_psum, lowT_ready, skew_psum, skew_ready = sem("lowT_psum"), sem("lowT_ready"), sem("skew_psum"), sem("skew_ready")
        xp_ready, x_ready, k_psum, k_ready = sem("xp_ready"), sem("x_ready"), sem("k_psum"), sem("k_ready")
        hx_psum, hx_ready, z0_psum, z0_ready = sem("hx_psum"), sem("hx_ready"), sem("z0_psum"), sem("z0_ready")
        mod_psum, modrow_ready, modT_psum, modcol_ready = sem("mod_psum"), sem("modrow_ready"), sem("modT_psum"), sem("modcol_ready")
        gate_psum, gate_ready, wsum_ready, wscale, wcen_ready, rows_ready = (
            sem("gate_psum"), sem("gate_ready"), sem("wsum_ready"), sem("wscale"), sem("wcen_ready"), sem("rows_ready"))
        zslot_ready = [sem(f"zslot_ready{j}") for j in range(2)]
        xkept = [sem(f"xkept{j}") for j in range(2)]
        rot_ready, xrot_ready, stats_ready, mv_ready = sem("rot_ready"), sem("xrot_ready"), sem("stats_ready"), sem("mv_ready")
        vareps_ready, rstd_ready, xn_ready, xT_psum, xT_ready = sem("vareps_ready"), sem("rstd_ready"), sem("xn_ready"), sem("xT_psum"), sem("xT_ready")
        qkv_psum = [sem(f"qkv_psum{j}") for j in range(2)]
        qkv_used = [sem(f"qkv_used{j}") for j in range(2)]
        qkc_ready, sq_ready, ssq_ready, kg_ready, hvar_ready, hrstd_ready, qkn_ready = (
            sem("qkc_ready"), sem("sq_ready"), sem("ssq_ready"), sem("kg_ready"), sem("hvar_ready"), sem("hrstd_ready"), sem("qkn_ready"))
        split_h, split_l, split_ready = sem("split_h"), sem("split_l"), sem("split_ready")
        t_psum, op_ready, s_ready, exp_done, pv_done = sem("t_psum"), sem("op_ready"), sem("s_ready"), sem("exp_done"), sem("pv_done")
        vop_set, vop_ready, oacc_ready, oT_psum, den_ready, o_ready = (
            sem("vop_set"), sem("vop_ready"), sem("oacc_ready"), sem("oT_psum"), sem("den_ready"), sem("o_ready"))
        orow_ready, xgb_ready, oT2_psum, oT2_ready = sem("orow_ready"), sem("xgb_ready"), sem("oT2_psum"), sem("oT2_ready")
        proj_ready, gated_ready, x2_ready, stats2_ready, mv2_ready = (
            sem("proj_ready"), sem("gated_ready"), sem("x2_ready"), sem("stats2_ready"), sem("mv2_ready"))
        vareps2_ready, rstd2_ready, xn2_ready, xT2_psum, xT2_ready = (
            sem("vareps2_ready"), sem("rstd2_ready"), sem("xn2_ready"), sem("xT2_psum"), sem("xT2_ready"))
        h_psum, h_ready, y_psum = (
            sem("h_psum"), sem("h_ready"), sem("y_psum"))
        xgb2_ready = [sem(f"xgb2_ready{j}") for j in range(2)]
        gated2_ready = [sem(f"gated2_ready{j}") for j in range(2)]
        y_ready = [sem(f"y_ready{j}") for j in range(2)]
        y_stored = [sem(f"y_stored{j}") for j in range(2)]

        block = ctx.enter_context(nc.Block())

        def wait(eng, s, value):
            if not isinstance(value, int) or value > 0:
                eng.wait_ge(s, value)

        def pairs_of(eng, body):
            half = TILES // 2
            for b in range(B):
                with eng.Fori(0, half - 1) as i:
                    body(half * b + i, TILES * b + 2 * i, b, b)
                body(half * (b + 1) - 1, TILES * (b + 1) - 2, b, b + 1 if b + 1 < B else None)

        @block.sync
        def _(sp):
            sp.dma_start(P_sb[:, :, :], P.rearrange("(c p) d -> p c d", p=KC)).then_inc(p_loaded, 16)
            sp.dma_start(P_top[:, :], P[0:D, :]).then_inc(p_loaded, 16)
            sp.dma_start(cond_sb[:, :, :], cond_t.rearrange("(c p) b -> p c b", p=KC)).then_inc(cond_loaded, 16)
            for b in range(B):
                sp.dma_start(x_sb[:, TILES * b:TILES * b + TILES, :],
                             x[b].rearrange("(t p) f -> p t f", p=P128)).then_inc(x_loaded, 16)
            sp.dma_start(Wf, W_fold.rearrange("(c p) n -> p c n", p=KC)).then_inc(wf_loaded, 16)
            sp.dma_start(bf[:, :], b_fold).then_inc(wf_loaded, 16)
            sp.dma_start(Pt_sb[:, :], P_t).then_inc(wf_loaded, 16)
            sp.dma_start(w_qkv_sb, w_qkv.rearrange("(c p) n -> p c n", p=KC)).then_inc(wqkv_loaded, 16)
            sp.dma_start(bias_row[:, :], b_qkv.partition_broadcast(P128)).then_inc(wqkv_loaded, 16)
            sp.dma_start(w_mod_sb, w_mod.rearrange("(c p) n -> p c n", p=KC)).then_inc(mod_loaded, 16)
            sp.dma_start(bm_col, b_mod_cols).then_inc(mod_loaded, 16)
            for row, g in ((gq_row, g_q), (gk_row, g_k)):
                sp.dma_start(row.rearrange("p (h d) -> p h d", d=HD),
                             g.partition_broadcast(NH).partition_broadcast(P128)).then_inc(row_loaded, 16)
            for r, blk in enumerate((G_MSA, G_MLP)):
                sp.dma_start(bm_row[:, r, :], b_mod[H * blk:H * blk + H].partition_broadcast(P128)).then_inc(row_loaded, 16)
            for r, bias in enumerate((b_proj, b2)):
                sp.dma_start(bo_row[:, r, :], bias.partition_broadcast(P128)).then_inc(row_loaded, 16)
            sp.dma_start(w_proj_sb[:, :, :], w_proj.rearrange("(c p) n -> p c n", p=KC)).then_inc(proj_loaded, 16)
            sp.dma_start(b1_sb[:, :], b1_cols).then_inc(proj_loaded, 16)
            sp.wait_ge(vsb_ready, 1)
            for b in range(B):
                sp.dma_start(v_dram[b], v_sb[b:b + 97:32, :]).then_inc(v_stored, 16)
            sp.wait_ge(v_stored, 16 * B)
            sp.dma_start(fold, v_dram.rearrange("b g (r j) -> (g r) b j", j=D)).then_inc(fold_loaded, 16)
            sp.wait_ge(split_ready, 4 * (GROUPS // 2))
            sp.dma_start(w1_sb, w1.rearrange("(c p) n -> p c n", p=KC)).then_inc(w1_loaded, 16)
            sp.wait_ge(split_ready, 4 * GROUPS)
            sp.dma_start(w2_sb, w2.rearrange("(m p) n -> p m n", p=P128)).then_inc(w2_loaded, 16)
            out_t = out.rearrange("b (c j p) f -> (b c) p j f", p=P128, j=2)
            with sp.Fori(0, CHUNKS) as c:
                for j in range(2):
                    sp.wait_ge(y_ready[j], c + 1)
                    sp.dma_start(out_t[bass.ds(c, 1), :, j, :].rearrange("c p f -> p (c f)"), y_out[:, j, :]).then_inc(y_stored[j], 16)
            for j in range(2):
                sp.wait_ge(y_stored[j], 16 * CHUNKS)

        @block.gpsimd
        def _(pool):
            n_const = 0

            def step(ins):
                nonlocal n_const
                n_const += 1
                ins.then_inc(const_step, 1)
                pool.wait_ge(const_step, n_const)

            def select(ap, op, fill, base, pattern, mult):
                return pool.affine_select(out=ap, in_=ap, compare_op=op, fill=fill, base=base, pattern=pattern,
                                          channel_multiplier=mult)

            step(pool.memset(ident[:, :], 0.0))
            select(ident[:, :], ALU.not_equal, 1.0, 0, [[-1, P128]], 1).then_inc(ident_ready, 1)
            pool.memset(neg_half[:, :], -0.5).then_inc(const_step, 1)
            n_const += 1
            pool.memset(eps_layer[:, :], EPS).then_inc(const_step, 1)
            pool.memset(eps_head[:, :], HD * EPS).then_inc(const_step, 1)
            n_const += 2
            for c in range(8):
                part = elim_mask[:, 8 * c:8 * c + 8, :]
                step(pool.memset(part, -1.0))
                step(select(part, ALU.is_equal, 0.0, -8 * c, [[-1, 8], [0, D]], 1))
                select(part, ALU.is_gt, 0.0, -8 * c, [[-1, 8], [1, D]], 0).then_inc(mask_ready, 1)
                if c == 0:
                    pool.memset(silu[:, :, :], 0.0).then_inc(silu_step, 1)
                    pool.wait_ge(silu_step, 2)
                    pool.tensor_scalar(ex[:, :, :], ex[:, :, :], 1.0, None, ALU.add).then_inc(silu_step, 1)
            step(pool.memset(flip[:, :], 0.0))
            step(select(flip[:, :], ALU.not_equal, 1.0, -(D - 1), [[1, D]], 1))
            step(pool.memset(neg_i[:, :], 0.0))
            step(select(neg_i[:, :], ALU.not_equal, -1.0, 0, [[-1, 32]], 1))
            for m, sign in ((fold_up, 1), (fold_low, -1)):
                step(pool.memset(m[:, :], 1.0))
                step(select(m[:, :], ALU.is_gt, 0.0, 0, [[sign, D]], -sign))
            for j in range(5):
                step(pool.memset(scaled_i[:, j, :], 0.0))
                step(select(scaled_i[:, j, :], ALU.not_equal, float(j + 2), 0, [[-1, D]], 1))
            for j in range(4):
                step(pool.memset(ident4[:, j, :], 0.0))
                step(select(ident4[:, j, :], ALU.not_equal, 1.0, 0, [[-1, D]], 1))
            step(pool.memset(ident16[:, :], 0.0))
            step(select(ident16[:, :], ALU.not_equal, 1.0, 0, [[-1, P128]], 1))
            pool.memset(lowT, 0.0).then_inc(const_ready, 1)

            n_rs = 0

            def diagonal_rsqrt():
                nonlocal n_rs
                n_rs += 1
                pool.wait_ge(diag_ready, n_rs)
                pool.tensor_tensor(diag_rs[:, :], diag[:, :], neg_half[0:D, 0:1], ALU.pow).then_inc(diagrs_ready, 1)

            for _ in range(2):
                diagonal_rsqrt()
            for c in range(NC + 1):
                s = w_sum[:, c, :] if c < NC else b_sum
                w = (w_qkv_sb[:, c, 0:2 * H] if c < NC else bias_row[:, 0:2 * H]).rearrange("p (h d) -> p h d", d=HD)
                pool.wait_ge(wsum_ready, c + 1)
                pool.tensor_scalar(s, s, -1.0 / HD, None, ALU.mult).then_inc(wscale, 1)
                pool.wait_ge(wscale, c + 1)
                pool.tensor_tensor(w, w, s.unsqueeze(2).broadcast_to([s.shape[0], 32, HD]), ALU.add).then_inc(wcen_ready, 1)
                if c == 1:
                    diagonal_rsqrt()
            diagonal_rsqrt()
            pool.wait_ge(fold_loaded, 16)
            pool.wait_ge(wf_loaded, 48)
            pool.tensor_tensor(fold_b, fold, bf[:, :].unsqueeze(1).broadcast_to([32, B, D]), ALU.add).then_inc(foldb_ready, 1)
            pool.wait_ge(foldb_ready, 1)
            for part, mask in ((v_up, fold_up), (v_low, fold_low)):
                pool.tensor_tensor(part, fold_b, mask[:, :].unsqueeze(1).broadcast_to([32, B, D]), ALU.mult).then_inc(vparts_ready, 1)
            pool.wait_ge(row_loaded, 16 * 6)
            pool.tensor_tensor(g_row[:, :], gq_row, gk_row, ALU.mult).then_inc(rows_ready, 1)
            pool.wait_ge(rows_ready, 1)
            pool.tensor_scalar(g_row[:, :], g_row[:, :], float(HD), None, ALU.mult).then_inc(rows_ready, 1)
            for _ in range(4):
                diagonal_rsqrt()
            pool.wait_ge(gate_ready, 4)
            for r in range(2):
                for b in range(B):
                    pool.tensor_tensor(gate_bias[:, r, b, :], gate[:, r, b, :], bo_row[:, r, :], ALU.mult).then_inc(rows_ready, 1)

            def layer_rstd(n, j):
                pool.wait_ge(mv_ready, n + 1)
                pool.tensor_tensor(var_eps[:, 0:1], mean_var[:, 0, 1:2], eps_layer[:, :], ALU.add).then_inc(vareps_ready, 1)
                pool.wait_ge(vareps_ready, n + 1)
                pool.tensor_tensor(rstd[:, 0:1], var_eps[:, 0:1], neg_half[:, 0:1], ALU.pow).then_inc(rstd_ready, 1)
                pool.tensor_copy(x_sb[:, bass.ds(n, 1), :].rearrange("p t f -> p (t f)"), x_cur[:, j, :]).then_inc(xkept[j], 1)

            def heads(n):
                pool.wait_ge(qkc_ready, 2 * n + 2)
                wait(pool, qkn_ready, 2 * n)
                pool.tensor_tensor(k_g, qk_c[:, 1, :], g_row[:, :], ALU.mult).then_inc(kg_ready, 1)
                pool.wait_ge(ssq_ready, n + 1)
                pool.tensor_tensor(head_var, head_ssq, eps_head[:, :], ALU.add).then_inc(hvar_ready, 1)
                pool.wait_ge(hvar_ready, n + 1)
                pool.tensor_tensor(head_rstd, head_var, neg_half[:, :], ALU.pow).then_inc(hrstd_ready, 1)

            layer_rstd(0, 0)

            def pair_a(pair, n0, b, b_next):
                layer_rstd(n0 + 1, 1)
                heads(n0)
                if b_next is not None:
                    layer_rstd(n0 + 2, 0)
                heads(n0 + 1)

            pairs_of(pool, pair_a)

            pool.memset(v_op[:, :, :, :, HD:HD + 1], 1.0).then_inc(vop_set, 1)
            pool.memset(v_op[:, :, :, :, HD + 1:32], 0.0).then_inc(vop_set, 1)

            def copy_v(g, par):
                wait(pool, pv_done, 16 * g)
                pool.tensor_copy(v_op[:, par, :, :, 0:HD].rearrange("p t h d -> p (t h) d"),
                                 v_all[:, bass.ds(g, 1), :, :, :].rearrange("p g t h d -> p (g t h) d")).then_inc(vop_ready, 1)

            pool.wait_ge(qkn_ready, 2 * NT)
            pool.wait_ge(qkv_used[1], NT // 2)
            copy_v(0, 0)
            copy_v(1, 1)
            with pool.Fori(0, GROUPS // 2 - 1) as i:
                pool.wait_ge(pv_done, 16 * (2 * i + 2))
                copy_v(2 * i + 2, 0)
                pool.wait_ge(pv_done, 16 * (2 * i + 3))
                copy_v(2 * i + 3, 1)

            def c_inputs(n, j, b):
                t = n - TILES * b
                wait(pool, oT2_psum, n - 1)
                pool.tensor_copy(o_row[:, j, :].rearrange("p (g f) -> p g f", g=4),
                                 o_tok[:, 4 * b:4 * b + 4, bass.ds(t, 1), :].rearrange("p g t f -> p g (t f)")).then_inc(orow_ready, 1)
                wait(pool, x2_ready, n - 1)
                pool.tensor_tensor(x_gb[:, j, :], x_sb[:, bass.ds(n, 1), :].rearrange("p t f -> p (t f)"),
                                   gate_bias[:, 0, b, :], ALU.add).then_inc(xgb_ready, 1)

            def c_rstd(n, j):
                pool.wait_ge(mv2_ready, n + 1)
                pool.tensor_tensor(var_eps[:, j:j + 1], mean_var[:, j, 1:2], eps_layer[:, :], ALU.add).then_inc(vareps2_ready, 1)
                pool.wait_ge(vareps2_ready, n + 1)
                pool.tensor_tensor(rstd[:, j:j + 1], var_eps[:, j:j + 1], neg_half[:, 0:1], ALU.pow).then_inc(rstd2_ready, 1)

            def c_out_residual(c_no, n, j, b):
                wait(pool, y_ready[j], c_no)
                pool.tensor_tensor(x_gb2[:, j, :], x_cur[:, j, :],
                                   gate_bias[:, 1, b, :], ALU.add).then_inc(xgb2_ready[j], 1)

            def c_front(n0, b):
                for j in range(2):
                    c_inputs(n0 + j, j, b)
                for j in range(2):
                    c_rstd(n0 + j, j)

            pool.wait_ge(o_ready, GROUPS)
            c_front(0, 0)

            def chunk_c(c_no, n0, b, b_next):
                for j in range(2):
                    c_out_residual(c_no, n0 + j, j, b)
                if b_next is not None:
                    c_front(n0 + 2, b_next)

            pairs_of(pool, chunk_c)

        @block.scalar
        def _(act):
            act.wait_ge(cond_loaded, 16)
            act.activation(ex[:, :, :], cond_sb[:, :, :], ACT.Exp, scale=-1.0).then_inc(silu_step, 1)

            def head_tile(n):
                act.wait_ge(hx_psum, n + 1)
                act.activation(xT_head[:, n % 2, :, :], ps[0:KC, 5, 0:NC * P128].rearrange("p (c k) -> p c k", c=NC),
                               ACT.Copy).then_inc(hx_ready, 1)
                act.wait_ge(z0_psum, n + 1)
                act.activation(z0_all[:, n, :], ps[0:D, 6, 0:P128], ACT.Copy).then_inc(z0_ready, 1)

            for n in range(NT):
                head_tile(n)
            act.wait_ge(v_ready, 1)
            act.activation(v_sb, ps[:, 3, :], ACT.Copy).then_inc(vsb_ready, 1)
            act.wait_ge(lowT_psum, 1)
            act.wait_ge(const_ready, 1)
            low = ps[0:D, 4, 0:B * 32].rearrange("p (b r) -> p b r", b=B)
            act.activation(lowT[:, :, 32:D], low, ACT.Copy).then_inc(lowT_ready, 1)
            act.activation(neg_lowT, low, ACT.Copy, scale=-1.0).then_inc(lowT_ready, 1)
            act.wait_ge(skew_psum, 1)
            sk = ps[0:D, 3, 0:B * D].rearrange("p (b j) -> p b j", b=B)
            act.activation(skew[:, 0:2, :], sk, ACT.Copy, scale=2.0 ** -SQUARINGS).then_inc(skew_ready, 1)
            act.activation(skew[:, 2:4, :], sk, ACT.Copy, scale=-2.0 ** -SQUARINGS).then_inc(skew_ready, 1)

            def expm_round(n):
                j = TAYLOR - n
                act.wait_ge(xp_ready, n + 1)
                act.activation(X[:, n % 2, :, :], ps[0:D, 3 + (n + 1) % 2, 0:4 * D].rearrange("p (m j) -> p m j", m=4),
                               ACT.Copy, scale=1.0 / j if j > 1 else 1.0).then_inc(x_ready, 1)

            for n in range(4):
                expm_round(n)
            act.wait_ge(mod_psum, 1)
            act.activation(mod_row[:, 0, :], ps[:, 5, 0:H], ACT.Copy).then_inc(modrow_ready, 1)
            act.activation(mod_row[0:64, 1, :], ps[0:64, 6, 0:H], ACT.Copy).then_inc(modrow_ready, 1)
            for n in range(4, ROUNDS):
                expm_round(n)
            act.wait_ge(k_psum, 1)
            act.activation(FW, ps[0:D, 3, 0:B * D].rearrange("p (b j) -> p b j", b=B), ACT.Copy).then_inc(k_ready, 1)
            act.wait_ge(k_psum, 2)
            act.activation(Kt, ps[0:D, 4, 0:B * D].rearrange("p (b j) -> p b j", b=B), ACT.Copy).then_inc(k_ready, 1)
            for b in range(B):
                act.wait_ge(k_psum, 3 + b)
                act.activation(Y[:, b, :], ps[0:D, 5 + b, 0:H], ACT.Copy).then_inc(k_ready, 1)

            def fill_z(n, j):
                wait(act, rot_ready, n - 1)
                act.activation(z_slot[:, j, :], z0_all[:, bass.ds(n, 1), :].rearrange("p t k -> p (t k)"),
                               ACT.Copy).then_inc(zslot_ready[j], 1)

            act.wait_ge(z0_ready, NT)
            fill_z(0, 0)
            fill_z(1, 1)

            def tile_a(pair, n, j, b, fill):
                act.wait_ge(xT_psum, n + 1)
                wait(act, qkv_psum[j], 3 * pair)
                for c in range(NC):
                    ins = act.activation(xT[:, j, c, :], ps[0:KC, 1, P128 * c:P128 * c + P128], ACT.Identity,
                                         scale=mod_col[:, SC_MSA, c, b:b + 1], bias=mod_col[:, SH_MSA, c, b:b + 1])
                ins.then_inc(xT_ready, 1)
                if fill:
                    fill_z(n + 2, j)
                act.wait_ge(qkc_ready, 2 * n + 2)
                wait(act, ssq_ready, n)
                act.activation(qk_sq, qk_c, ACT.Square).then_inc(sq_ready, 1)

            act.wait_ge(modcol_ready, 3)

            def pair_a(pair, n0, b, b_next):
                for j in range(2):
                    tile_a(pair, n0 + j, j, b, b_next is not None)

            pairs_of(act, pair_a)

            def exp_unit(g, u):
                act.wait_ge(s_ready, 32 * g + u + 1)
                kt = u // 4
                wait(act, pv_done, 16 * g + 2 * kt - 2)
                act.activation(prob[:, u % 8, :], ps[:, 2 * slot_of(u):2 * slot_of(u) + 2, :].rearrange("p a q -> p (a q)"),
                               ACT.Exp, scale=HD ** -0.5).then_inc(exp_done, 1)

            def slot_of(u):
                return next(p for pair in RING_PAIRS for kind, n, p in pair if (kind, n) == ("S", u)) % 3

            def group_b(g):
                for u in range(32):
                    exp_unit(g, u)

            group_b(0)
            with act.Fori(0, GROUPS // 2 - 1) as i:
                group_b(2 * i + 1)
                group_b(2 * i + 2)
            group_b(GROUPS - 1)

            def c_turn_o(n, j):
                act.wait_ge(oT2_psum, n + 1)
                wait(act, proj_ready, n - 1)
                act.activation(oT2[:, j, :, :], ps[0:KC, 0, 0:NC * P128].rearrange("p (c k) -> p c k", c=NC),
                               ACT.Copy).then_inc(oT2_ready, 1)

            def c_turn_x(n, j, b):
                act.wait_ge(xT2_psum, n + 1)
                for c in range(NC):
                    ins = act.activation(xn2T[:, c, P128 * j:P128 * j + P128], ps[0:KC, 2, P128 * c:P128 * c + P128], ACT.Identity,
                                         scale=mod_col[:, SC_MLP, c, b:b + 1], bias=mod_col[:, SH_MLP, c, b:b + 1])
                ins.then_inc(xT2_ready, 1)

            for j in range(2):
                c_turn_o(j, j)
            for j in range(2):
                c_turn_x(j, j, 0)

            def chunk_c(c_no, n0, b, b_next):
                for m in range(FF):
                    act.wait_ge(h_psum, FF * c_no + m + 1)
                    act.activation(hid[:, m, :], ps[:, 3 + m % 3, 0:CH], ACT.Gelu_apprx_tanh, bias=b1_sb[:, m:m + 1]).then_inc(h_ready, 1)
                    if b_next is not None and m in (1, 4):
                        c_turn_o(n0 + 2 + (m == 4), int(m == 4))
                if b_next is not None:
                    for j in range(2):
                        c_turn_x(n0 + 2 + j, j, b_next)

            pairs_of(act, chunk_c)

        @block.tensor
        def _(pe):
            Z, M, N = ps[:, 0, :], ps[:, 1, :], ps[:, 2, :]
            pe.wait_ge(p_loaded, 32)
            for c in range(NC):
                pe.matmul(Z[0:D, 0:D], P_sb[:, c, :], P_sb[:, c, :], start=(c == 0), stop=(c == NC - 1))
            pe.wait_ge(ident_ready, 1)
            pe.matmul(Z[0:D, D:2 * D], ident[0:D, 0:D], ident[0:D, 0:D], start=False, stop=False,
                      skip_group_check=True).then_inc(z_ready, 1)
            pe.matmul(M[0:D, 0:D], ident[0:D, 0:D], P_top[:, :], start=True, stop=False, skip_group_check=True).then_inc(m_ready, 1)
            pe.matmul(N[0:D, 0:D], P_top[:, :], ident[0:D, 0:D], start=True, stop=False, skip_group_check=True).then_inc(n_ready, 1)

            def update_z(k):
                pe.wait_ge(zrow_ready, k + 1)
                pe.wait_ge(zcol_ready, k + 1)
                pe.matmul(Z[0:D, k + 1:k + 1 + D], z_col[:, :], z_row[:, k + 1:k + 1 + D], start=False, stop=False,
                          skip_group_check=True).then_inc(z_ready, 1)

            def update_mn(k):
                pe.wait_ge(w_ready, k + 1)
                pe.wait_ge(c_ready, k + 1)
                pe.matmul(M[0:D, k + 1:D], m_col[:, k % 2, :], w_row[:, k % 2, k + 1:D], start=False, stop=False,
                          skip_group_check=True).then_inc(m_ready, 1)
                pe.matmul(N[0:D, k + 1:D], w_row[:, k % 2, :], m_col[:, k % 2, k + 1:D], start=False, stop=False,
                          skip_group_check=True).then_inc(n_ready, 1)

            def head_turn(n):
                if n == 0:
                    pe.wait_ge(x_loaded, 32)
                wait(pe, hx_ready, n)
                for c in range(NC):
                    mm = pe.transpose(ps[0:KC, 5, P128 * c:P128 * c + P128], x_sb[:, n, KC * c:KC * c + KC], ident[:, :])
                mm.then_inc(hx_psum, 1)

            def head_z0(n):
                pe.wait_ge(hx_ready, n + 1)
                wait(pe, z0_ready, n)
                for c in range(NC):
                    mm = pe.matmul(ps[0:D, 6, 0:P128], P_sb[:, c, :], xT_head[:, n % 2, c, :], start=(c == 0), stop=(c == NC - 1))
                mm.then_inc(z0_psum, 1)

            def angles():
                pe.wait_ge(wf_loaded, 48)
                pe.wait_ge(silu_ready, 1)
                for c in range(NC):
                    for g in range(4):
                        mm = pe.matmul(ps[32 * g:32 * g + 32, 3, :], silu[:, c, :], Wf[:, c, 512 * g:512 * g + 512],
                                       start=(c == 0), stop=(c == NC - 1), tile_position=(0, 32 * g))
                mm.then_inc(v_ready, 1)

            def lower_half():
                pe.wait_ge(vparts_ready, 2)
                for b in range(B):
                    mm = pe.matmul(ps[0:D, 4, 32 * b:32 * b + 32], v_low[:, b, :], flip[0:32, 32:64], start=True, stop=True)
                mm.then_inc(lowT_psum, 1)

            def skew_matrix():
                pe.wait_ge(lowT_ready, 2)
                for b in range(B):
                    a = ps[0:D, 3, D * b:D * b + D]
                    pe.matmul(a, ident[0:32, 0:D], v_up[:, b, :], start=True, stop=False, skip_group_check=True)
                    pe.matmul(a[:, 0:32], v_up[:, b, :], neg_i[:, :], start=False, stop=False, skip_group_check=True)
                    pe.matmul(a, lowT[:, b, :], flip[:, :], start=False, stop=False, skip_group_check=True)
                    mm = pe.matmul(a[:, 32:64], flip[:, :], neg_lowT[:, b, :], start=False, stop=True, skip_group_check=True)
                mm.then_inc(skew_psum, 1)

            def expm_round(n):
                to, j = 3 + (n + 1) % 2, TAYLOR - n
                if n == 0:
                    pe.wait_ge(skew_ready, 2)
                    pe.wait_ge(const_ready, 1)
                else:
                    pe.wait_ge(x_ready, n)
                old = ident4 if n == 0 else X[:, (n - 1) % 2, :, :]
                if j > 1:
                    pe.matmul(ps[0:D, to, 0:4 * D], scaled_i[:, j - 2, :], ident4, start=True, stop=False, skip_group_check=True)
                elif j < 1:
                    pe.matmul(ps[0:D, to, 0:4 * D], scaled_i[:, 0, :], old, start=True, stop=False, skip_group_check=True)
                for m in range(4):
                    left = skew if j >= 1 else old
                    mm = pe.matmul(ps[0:D, to, D * m:D * m + D], left[:, m ^ 2, :], old[:, m, :], start=(j == 1), stop=True,
                                   skip_group_check=True)
                mm.then_inc(xp_ready, 1)

            def modulation():
                pe.wait_ge(mod_loaded, 32)
                for r, blocks in ((0, range(4)), (1, range(4, 6))):
                    for c in range(NC):
                        for g, blk in enumerate(blocks):
                            mm = pe.matmul(ps[32 * g:32 * g + 32, 5 + r, 0:H], silu[:, c, :], w_mod_sb[:, c, H * blk:H * blk + H],
                                           start=(c == 0), stop=(c == NC - 1), tile_position=(0, 32 * g))
                mm.then_inc(mod_psum, 1)

            def modulation_columns():
                pe.wait_ge(modrow_ready, 2)
                for c in range(NC):
                    pe.transpose(ps[0:KC, 7, P128 * c:P128 * c + P128], mod_row[:, 0, KC * c:KC * c + KC], ident[:, :])
                    mm = pe.transpose(ps[0:KC, 6, P128 * c:P128 * c + 64], mod_row[0:64, 1, KC * c:KC * c + KC], ident[0:64, 0:64])
                mm.then_inc(modT_psum, 1)

            def gate_rows(r, b):
                wait(pe, gate_ready, 2 * r + b)
                if r == 0:
                    mm = pe.matmul(ps[:, 5, 0:H], ident[:, 64 + b:65 + b].broadcast_to([P128, P128]), mod_row[:, 0, :], start=True, stop=True)
                else:
                    mm = pe.matmul(ps[:, 5, 0:H], ident[0:64, 32 + b:33 + b].broadcast_to([64, P128]), mod_row[0:64, 1, :], start=True, stop=True)
                mm.then_inc(gate_psum, 1)

            for it in range(D + LAG):
                if it < D - 1:
                    update_z(it)
                if LAG <= it < D - 1 + LAG:
                    update_mn(it - LAG)
                if 8 <= it < 8 + NT:
                    head_turn(it - 8)
                if 9 <= it < 9 + NT:
                    head_z0(it - 9)
                if it == 26:
                    angles()
                if it == 32:
                    lower_half()
                if it == 34:
                    skew_matrix()
                if 36 <= it < 36 + 2 * ROUNDS and it % 2 == 0:
                    expm_round((it - 36) // 2)
                if it == 43:
                    modulation()
                if it == 47:
                    modulation_columns()
                if it in (51, 55, 59, 63):
                    gate_rows((it - 51) // 8, (it - 51) // 4 % 2)
            E = X[:, (ROUNDS - 1) % 2, :, :]
            pe.wait_ge(x_ready, ROUNDS)
            pe.wait_ge(winv_ready, 1)
            for b in range(B):
                mm = pe.matmul(ps[0:D, 3, D * b:D * b + D], E[:, b, :], Winv[:, :], start=True, stop=True)
            mm.then_inc(k_psum, 1)
            pe.wait_ge(k_ready, 1)
            pe.matmul(ps[0:D, 4, 0:B * D], Winv[:, :], FW, start=True, stop=True).then_inc(k_psum, 1)
            pe.wait_ge(k_ready, 2)
            pe.wait_ge(gate_ready, 4)
            for b in range(B):
                pe.matmul(ps[0:D, 5 + b, 0:H], Kt[:, b, :], Pt_sb[:, :], start=True, stop=True).then_inc(k_psum, 1)
            pe.wait_ge(k_ready, 4)

            def rotate(n, j, b, uses):
                pe.wait_ge(zslot_ready[j], uses + 1)
                wait(pe, xrot_ready, n)
                pe.matmul(ps[:, 0, 0:H], z_slot[:, j, :], Y[:, b, :], start=True, stop=True).then_inc(rot_ready, 1)

            def turn(n):
                pe.wait_ge(xn_ready, n + 1)
                wait(pe, xT_ready, n)
                for c in range(NC):
                    mm = pe.transpose(ps[0:KC, 1, P128 * c:P128 * c + P128], xn[:, KC * c:KC * c + KC], ident[:, :])
                mm.then_inc(xT_psum, 1)

            def qkv(n, j, uses):
                pe.wait_ge(xT_ready, n + 1)
                wait(pe, qkv_used[j], uses)
                for a in range(3):
                    for c in range(NC):
                        mm = pe.matmul(ps[:, 2 + 3 * j + a, 0:H], xT[:, j, c, :], w_qkv_sb[:, c, H * a:H * a + H],
                                       start=(c == 0), stop=(c == NC - 1))
                    mm.then_inc(qkv_psum[j], 1)

            pe.wait_ge(wcen_ready, NC)
            pe.wait_ge(modcol_ready, 3)
            rotate(0, 0, 0, 0)

            def pair_a(pair, n0, b, b_next):
                turn(n0)
                rotate(n0 + 1, 1, b, pair)
                qkv(n0, 0, pair)
                turn(n0 + 1)
                if b_next is not None:
                    rotate(n0 + 2, 0, b_next, pair + 1)
                qkv(n0 + 1, 1, pair)

            pairs_of(pe, pair_a)

            def bank(slot, a):
                return ps[:, 2 * slot + a, :]

            def slot_free(g, p, before, after):
                back = (p - 3) % RING_LEN
                while back not in RING_AT or back < p and (
                        RING_AT[back][0] == "O" and not before or RING_AT[back][0] == "T" and not after):
                    back = (back - 3) % RING_LEN
                kind, n = RING_AT[back]
                of = g if back < p else g - 1
                if kind == "S":
                    wait(pe, exp_done, 32 * of + n + 1)
                elif kind == "T":
                    wait(pe, op_ready, 4 * of + 4 + n + 1)
                else:
                    wait(pe, o_ready, of)

            def turn_qk(g_next, h, slot):
                pe.wait_ge(split_ready, 4 * g_next + 4)
                for a in range(2):
                    to = bank(slot, a)[0:PARTS * HD, :].bitcast(F16)
                    for t in range(TILES):
                        mm = pe.transpose(to[:, P128 * t:P128 * t + P128],
                                          qk_split[:, t, a, h, :, :].rearrange("p r d -> p (r d)"), ident16[:, :])
                mm.then_inc(t_psum, 1)

            def scores(g, u, par, slot):
                kt, h = u // 4, u % 4
                if kt == 0:
                    pe.wait_ge(op_ready, 4 * g + h + 1)
                for a in range(2):
                    mm = pe.matmul(bank(slot, a), qk_op[:, par, 1, h, P128 * kt:P128 * kt + P128],
                                   qk_op[:, par, 0, h, 512 * a:512 * a + 512], start=True, stop=True)
                mm.then_inc(s_ready, 1)

            def weigh_v(g, w, par):
                kt, a = w // 2, w % 2
                pe.wait_ge(exp_done, 32 * g + 4 * kt + 4)
                if w < 2:
                    pe.wait_ge(vop_ready, g + 1)
                    wait(pe, oacc_ready, 2 * g + a - 1)
                for h in range(HG):
                    mm = pe.matmul(ps[32 * h:32 * h + 32, 6 + a, :], v_op[:, par, kt, h, :],
                                   prob[:, (4 * kt + h) % 8, 512 * a:512 * a + 512], start=(kt == 0), stop=(kt == TILES - 1),
                                   tile_position=(0, 32 * h))
                mm.then_inc(pv_done, 1)

            def turn_o(g, slot):
                pe.wait_ge(oacc_ready, 2 * g + 2)
                for t in range(TILES):
                    mm = pe.transpose(bank(slot, t // 4)[:, P128 * (t % 4):P128 * (t % 4) + P128], o_acc[:, P128 * t:P128 * t + P128],
                                      ident[:, :])
                mm.then_inc(oT_psum, 1)

            def group_b(g, par, before, after):
                for v in range(16):
                    for kind, n, p in RING_PAIRS[v]:
                        if kind == "S":
                            slot_free(g, p, before, after)
                            scores(g, n, par, p % 3)
                        elif kind == "T" and after:
                            slot_free(g, p, before, after)
                            turn_qk(g + 1, n, p % 3)
                        elif kind == "O" and before:
                            slot_free(g, p, before, after)
                            turn_o(g - 1, p % 3)
                        if kind == "S" and n % 2 == 1:
                            if v >= 3:
                                weigh_v(g, v - 3, par)
                            elif before:
                                weigh_v(g - 1, 13 + v, 1 - par)

            for h in range(HG):
                if h == 3:
                    pe.wait_ge(op_ready, 1)
                turn_qk(0, h, h % 3)
            pe.wait_ge(op_ready, HG)
            group_b(0, 0, False, True)
            with pe.Fori(0, GROUPS // 2 - 1) as i:
                group_b(2 * i + 1, 1, True, True)
                group_b(2 * i + 2, 0, True, True)
            group_b(GROUPS - 1, 1, True, False)
            for w in range(13, 16):
                weigh_v(GROUPS - 1, w, 1)
            pe.wait_ge(exp_done, 32 * GROUPS)
            turn_o(GROUPS - 1, 0)
            pe.wait_ge(o_ready, GROUPS)

            def c_turn_o(n, j):
                pe.wait_ge(orow_ready, n + 1)
                wait(pe, oT2_ready, n)
                for c in range(NC):
                    mm = pe.transpose(ps[0:KC, 0, P128 * c:P128 * c + P128], o_row[:, j, KC * c:KC * c + KC], ident[:, :])
                mm.then_inc(oT2_psum, 1)

            def c_project(n, j):
                pe.wait_ge(oT2_ready, n + 1)
                wait(pe, gated_ready, n)
                for c in range(NC):
                    mm = pe.matmul(ps[:, 1, 0:H], oT2[:, j, c, :], w_proj_sb[:, c, :], start=(c == 0), stop=(c == NC - 1))
                mm.then_inc(proj_ready, 1)

            def c_turn_x(n):
                pe.wait_ge(xn2_ready, n + 1)
                wait(pe, xT2_ready, n)
                for c in range(NC):
                    mm = pe.transpose(ps[0:KC, 2, P128 * c:P128 * c + P128], xn[:, KC * c:KC * c + KC], ident[:, :])
                mm.then_inc(xT2_psum, 1)

            def c_up(c_no, n0, m):
                pe.wait_ge(xT2_ready, n0 + 2)
                if m >= 3:
                    pe.wait_ge(h_ready, FF * c_no + m - 2)
                for c in range(NC):
                    mm = pe.matmul(ps[:, 3 + m % 3, 0:CH], w1_sb[:, c, P128 * m:P128 * m + P128], xn2T[:, c, :],
                                   start=(c == 0), stop=(c == NC - 1))
                mm.then_inc(h_psum, 1)

            def c_down(c_no, n0):
                pe.wait_ge(h_ready, FF * c_no + FF)
                for j in range(2):
                    wait(pe, gated2_ready[j], c_no)
                    for m in range(FF):
                        mm = pe.matmul(ps[:, 6 + j, 0:H], hid[:, m, P128 * j:P128 * j + P128], w2_sb[:, m, :],
                                       start=(m == 0), stop=(m == FF - 1))
                    mm.then_inc(y_psum, 1)

            pe.wait_ge(proj_loaded, 32)
            c_turn_o(0, 0)
            c_project(0, 0)
            c_turn_o(1, 1)
            c_project(1, 1)
            c_turn_x(0)
            c_turn_x(1)
            pe.wait_ge(w1_loaded, 16)
            pe.wait_ge(w2_loaded, 16)

            def chunk_c(c_no, n0, b, b_next):
                for m in range(FF):
                    c_up(c_no, n0, m)
                    if b_next is not None:
                        if m == 0:
                            c_turn_o(n0 + 2, 0)
                        if m == 2:
                            c_project(n0 + 2, 0)
                        if m == 3:
                            c_turn_o(n0 + 3, 1)
                        if m == 6:
                            c_project(n0 + 3, 1)
                if b_next is not None:
                    c_turn_x(n0 + 2)
                    c_turn_x(n0 + 3)
                c_down(c_no, n0)

            pairs_of(pe, chunk_c)

        @block.vector
        def _(dve):
            Z, M, N = ps[:, 0, :], ps[:, 1, :], ps[:, 2, :]
            dve.wait_ge(silu_step, 3)
            dve.reciprocal(ex[:, :, :], ex[:, :, :]).then_inc(silu_step, 1)
            dve.wait_ge(silu_step, 4)
            dve.tensor_tensor(silu[:, :, 0:B], ex[:, :, :], cond_sb[:, :, :], ALU.mult).then_inc(silu_ready, 1)

            def read_diagonal():
                dve.tensor_tensor_reduce(out=junk[:, :], in0=Z[0:D, 0:D], in1=ident[0:D, 0:D], scale=1.0, scalar=0.0,
                                         op0=ALU.mult, op1=ALU.add, accum_out=diag[:, :]).then_inc(diag_ready, 1)

            def scale_r(j):
                dve.wait_ge(diagrs_ready, j + 1)
                wait(dve, w_ready, LAG * j)
                dve.tensor_scalar(R_half[:, :], Z[0:D, 0:D], diag_rs[:, 0:1], 0.5, ALU.mult, ALU.mult).then_inc(r_ready, 1)

            def z_step(k):
                dve.wait_ge(z_ready, k + 1)
                if k % LAG == LAG - 1:
                    read_diagonal()
                if k % LAG == 0 and k > 0:
                    scale_r(k // LAG - 1)
                if k == D - 1:
                    return
                if k % 8 == 0:
                    dve.wait_ge(mask_ready, k // 8 + 1)
                dve.reciprocal(z_rcp[:, :], Z[0:D, k:k + 1]).then_inc(zrcp_ready, 1)
                dve.tensor_copy(z_row[:, k + 1:k + 1 + D], Z[0:D, k + 1:k + 1 + D]).then_inc(zrow_ready, 1)
                dve.wait_ge(zrcp_ready, k + 1)
                dve.scalar_tensor_tensor(out=z_col[:, :], in0=Z[0:D, 0:D], scalar=z_rcp[:, 0:1], in1=elim_mask[:, k, :],
                                         op0=ALU.mult, op1=ALU.mult).then_inc(zcol_ready, 1)

            def m_step(k):
                dve.wait_ge(m_ready, k + 1)
                if k % LAG == 0:
                    dve.wait_ge(r_ready, k // LAG + 1)
                dve.tensor_scalar(signs[:, k:k + 1], M[0:D, k:k + 1], 0.0, -0.5, ALU.is_ge, ALU.add).then_inc(sign_step, 1)
                if k == D - 1:
                    return
                dve.wait_ge(sign_step, k + 1)
                dve.scalar_tensor_tensor(out=pivot_half[:, :], in0=M[0:D, k:k + 1], scalar=signs[:, k:k + 1],
                                         in1=R_half[:, k:k + 1], op0=ALU.mult, op1=ALU.add).then_inc(pivot_ready, 1)
                dve.scalar_tensor_tensor(out=w_row[:, k % 2, :], in0=M[0:D, 0:D], scalar=signs[:, k:k + 1], in1=R_half[:, :],
                                         op0=ALU.mult, op1=ALU.add).then_inc(w_ready, 1)
                dve.wait_ge(pivot_ready, k + 1)
                dve.reciprocal(pivot_rcp[:, :], pivot_half[:, :]).then_inc(prcp_ready, 1)
                dve.wait_ge(n_ready, k + 1)
                dve.wait_ge(prcp_ready, k + 1)
                dve.scalar_tensor_tensor(out=m_col[:, k % 2, :], in0=N[0:D, 0:D], scalar=pivot_rcp[:, 0:1],
                                         in1=elim_mask[:, k, :], op0=ALU.mult, op1=ALU.mult).then_inc(c_ready, 1)

            def weight_sum(c):
                if c == 0:
                    dve.wait_ge(wqkv_loaded, 32)
                w = w_qkv_sb[:, c, 0:2 * H] if c < NC else bias_row[:, 0:2 * H]
                dve.tensor_reduce(w_sum[:, c, :] if c < NC else b_sum, w.rearrange("p (h d) -> p h d", d=HD), AX.X,
                                  ALU.add).then_inc(wsum_ready, 1)

            def modulation_columns():
                dve.wait_ge(modT_psum, 1)
                for r, blocks in ((0, 4), (1, 2)):
                    src = ps[0:KC, 7 - r, 0:NC * P128].rearrange("p (c g q) -> p g c q", c=NC, g=4)[:, 0:blocks, :, 0:B]
                    for b in range(B):
                        ins = dve.tensor_tensor(mod_col[:, 4 * r:4 * r + blocks, :, b], src[:, :, :, b],
                                                bm_col[:, 4 * r:4 * r + blocks, :], ALU.add)
                    ins.then_inc(modcol_ready, 1)
                dve.wait_ge(modcol_ready, 2)
                scales = mod_col[:, SC_MSA:SC_MLP + 1:SC_MLP - SC_MSA, :, :].rearrange("p s c b -> p s (c b)")
                dve.tensor_scalar(scales, scales, 1.0, None, ALU.add).then_inc(modcol_ready, 1)

            def gate_rows(r, b):
                dve.wait_ge(gate_psum, 2 * r + b + 1)
                if r == b == 0:
                    dve.wait_ge(row_loaded, 16 * 6)
                dve.tensor_tensor(gate[:, r, b, :], ps[:, 5, 0:H], bm_row[:, r, :], ALU.add).then_inc(gate_ready, 1)

            for it in range(D + LAG):
                if it < D:
                    z_step(it)
                if it == D:
                    scale_r(D // LAG - 1)
                if it >= LAG:
                    m_step(it - LAG)
                if it in (17, 19, 21, 23):
                    weight_sum((it - 17) // 2)
                if it == 49:
                    modulation_columns()
                if it in (52, 56, 60, 64):
                    gate_rows((it - 52) // 8, (it - 52) // 4 % 2)
            dve.wait_ge(sign_step, D)
            dve.tensor_tensor_reduce(out=junk[:, :], in0=signs[:, :], in1=ident[0:D, 0:D], scale=-2.0, scalar=0.0,
                                     op0=ALU.mult, op1=ALU.add, accum_out=sign_of[:, :]).then_inc(sign_ready, 1)
            dve.wait_ge(sign_ready, 1)
            dve.tensor_scalar(Winv[:, :], Z[0:D, D:2 * D], diag_rs[:, 0:1], sign_of[:, 0:1], ALU.mult, ALU.mult).then_inc(winv_ready, 1)

            def tile_of(n):
                return x_sb[:, bass.ds(n, 1), :].rearrange("p t f -> p (t f)")

            def layer_stats(n, j, uses):
                dve.wait_ge(rot_ready, n + 1)
                wait(dve, xkept[j], uses)
                dve.tensor_tensor(x_cur[:, j, :], ps[:, 0, 0:H], tile_of(n), ALU.add).then_inc(xrot_ready, 1)
                dve.wait_ge(xrot_ready, n + 1)
                dve.bn_stats(stats[:, :], x_cur[:, j, :]).then_inc(stats_ready, 1)

            def mean_and_variance():
                dve.bn_aggr(mean_var[:, 0, :], stats[:, :]).then_inc(mv_ready, 1)

            def normalise(n, j):
                dve.wait_ge(rstd_ready, n + 1)
                wait(dve, xT_psum, n)
                dve.tensor_scalar(xn[:, :], x_cur[:, j, :], mean_var[:, 0, 0:1], rstd[:, 0:1], ALU.subtract, ALU.mult).then_inc(xn_ready, 1)

            def biases(n, t, j, b, uses, stats_of):
                wait(dve, sq_ready, n)
                wait(dve, kg_ready, n)
                wait(dve, qkn_ready, 2 * n)
                for a in range(2):
                    if a == 0 and stats_of is not None:
                        dve.wait_ge(stats_ready, stats_of + 1)
                    dve.wait_ge(qkv_psum[j], 3 * uses + a + 1)
                    dve.tensor_tensor(qk_c[:, a, :], ps[:, 2 + 3 * j + a, 0:H], bias_row[:, H * a:H * a + H], ALU.add).then_inc(qkc_ready, 1)
                    if a == 0 and stats_of is not None:
                        mean_and_variance()
                dve.wait_ge(qkv_psum[j], 3 * uses + 3)
                dve.tensor_tensor(v_all[:, 4 * b:4 * b + 4, bass.ds(t, 1), :, :].rearrange("p g t h d -> p g (t h d)"),
                                  ps[:, 4 + 3 * j, 0:H].rearrange("p (g f) -> p g f", g=4),
                                  bias_row[:, 2 * H:3 * H].rearrange("p (g f) -> p g f", g=4), ALU.add).then_inc(qkv_used[j], 1)

            def head_norms(n, t, b):
                dve.wait_ge(sq_ready, n + 1)
                dve.tensor_reduce(head_ssq, qk_sq.rearrange("p a (h d) -> p (a h) d", d=HD), AX.X, ALU.add).then_inc(ssq_ready, 1)
                dve.wait_ge(hrstd_ready, n + 1)
                dve.wait_ge(kg_ready, n + 1)
                for a, src in ((0, qk_c[:, 0, :]), (1, k_g)):
                    dve.tensor_tensor(qkn[:, 4 * b:4 * b + 4, bass.ds(t, 1), a, :, :].rearrange("p g t h d -> p g (t h) d"),
                                      src.rearrange("p (g h d) -> p g h d", g=4, h=HG),
                                      head_rstd[:, 16 * a:16 * a + 16].rearrange("p (g h) -> p g h", g=4).unsqueeze(3)
                                      .broadcast_to([P128, 4, HG, HD]), ALU.mult).then_inc(qkn_ready, 1)

            layer_stats(0, 0, 0)
            dve.wait_ge(stats_ready, 1)
            mean_and_variance()
            normalise(0, 0)
            dve.wait_ge(wcen_ready, NC + 1)

            def pair_a(pair, n0, b, b_next):
                t0 = n0 - TILES * b
                layer_stats(n0 + 1, 1, pair)
                biases(n0, t0, 0, b, pair, n0 + 1)
                normalise(n0 + 1, 1)
                head_norms(n0, t0, b)
                if b_next is not None:
                    layer_stats(n0 + 2, 0, pair + 1)
                biases(n0 + 1, t0 + 1, 1, b, pair, n0 + 2 if b_next is not None else None)
                if b_next is not None:
                    normalise(n0 + 2, 0)
                head_norms(n0 + 1, t0 + 1, b)

            pairs_of(dve, pair_a)

            def split_qk(g):
                src = qkn[:, bass.ds(g, 1), :, :, :, :].rearrange("p g t a h d -> p (g t a h) d")
                to = qk_split.rearrange("p t a h r d -> p (t a h) r d")
                wait(dve, t_psum, 4 * g)
                dve.tensor_copy(to[:, :, 0, :], src).then_inc(split_h, 1)
                dve.wait_ge(split_h, g + 1)
                dve.tensor_tensor(to[:, :, 3, :], src, to[:, :, 0, :], ALU.subtract).then_inc(split_l, 1)
                dve.tensor_copy(qk_split[:, :, 0, :, 1, :], qk_split[:, :, 0, :, 0, :]).then_inc(split_ready, 1)
                dve.tensor_copy(qk_split[:, :, 1, :, 2, :], qk_split[:, :, 1, :, 0, :]).then_inc(split_ready, 1)
                dve.wait_ge(split_l, g + 1)
                dve.tensor_copy(qk_split[:, :, 0, :, 2, :], qk_split[:, :, 0, :, 3, :]).then_inc(split_ready, 1)
                dve.tensor_copy(qk_split[:, :, 1, :, 1, :], qk_split[:, :, 1, :, 3, :]).then_inc(split_ready, 1)

            def read_operands(g, par, h, slot):
                dve.wait_ge(t_psum, 4 * g + h + 1)
                for a in range(2):
                    ins = dve.tensor_copy(qk_op[:, par, a, h, :], ps[0:PARTS * HD, 2 * slot + a, :].bitcast(F16))
                ins.then_inc(op_ready, 1)

            def read_output(g):
                for a in range(2):
                    dve.wait_ge(pv_done, 16 * g + 15 + a)
                    if a == 0:
                        wait(dve, oT_psum, g)
                    dve.tensor_copy(o_acc[:, 512 * a:512 * a + 512], ps[:, 6 + a, :]).then_inc(oacc_ready, 1)

            def divide_output(g, slot):
                dve.wait_ge(oT_psum, g + 1)
                src = ps[:, 2 * slot:2 * slot + 2, :].rearrange("p a (t h d) -> p (a t) h d", h=HG, d=32)
                dve.reciprocal(den_inv[:, :, :].unsqueeze(3), src[:, :, :, HD:HD + 1]).then_inc(den_ready, 1)
                dve.wait_ge(den_ready, g + 1)
                dve.tensor_tensor(o_tok[:, bass.ds(g, 1), :, :].rearrange("p g t (h d) -> p (g t) h d", d=HD), src[:, :, :, 0:HD],
                                  den_inv[:, :, :].unsqueeze(3).broadcast_to([P128, TILES, HG, HD]), ALU.mult).then_inc(o_ready, 1)

            units = [(kind, n, p % 3) for pair in RING_PAIRS for kind, n, p in pair if kind != "S"]

            def group_b(g, par, before, after):
                if before:
                    read_output(g - 1)
                for kind, n, slot in units:
                    if kind == "T" and after:
                        if n == 0:
                            split_qk(g + 1)
                        read_operands(g + 1, 1 - par, n, slot)
                    if kind == "O" and before:
                        divide_output(g - 1, slot)

            dve.wait_ge(qkn_ready, 2 * NT)
            split_qk(0)
            for h in range(HG):
                read_operands(0, 0, h, h % 3)
            group_b(0, 0, False, True)
            with dve.Fori(0, GROUPS // 2 - 1) as i:
                group_b(2 * i + 1, 1, True, True)
                group_b(2 * i + 2, 0, True, True)
            group_b(GROUPS - 1, 1, True, False)
            read_output(GROUPS - 1)
            divide_output(GROUPS - 1, 0)

            def c_gate(n, b, stats_of):
                dve.wait_ge(proj_ready, n + 1)
                wait(dve, x2_ready, n)
                if stats_of is not None:
                    dve.wait_ge(stats2_ready, stats_of + 1)
                dve.tensor_tensor(gated, ps[:, 1, 0:H], gate[:, 0, b, :], ALU.mult).then_inc(gated_ready, 1)

            def c_add(n, j, uses):
                dve.wait_ge(gated_ready, n + 1)
                dve.wait_ge(xgb_ready, n + 1)
                wait(dve, xgb2_ready[j], uses)
                dve.tensor_tensor(x_cur[:, j, :], gated, x_gb[:, j, :], ALU.add).then_inc(x2_ready, 1)
                dve.wait_ge(x2_ready, n + 1)
                dve.bn_stats(stats[:, :], x_cur[:, j, :]).then_inc(stats2_ready, 1)

            def c_mean_and_variance(j):
                dve.bn_aggr(mean_var[:, j, :], stats[:, :]).then_inc(mv2_ready, 1)

            def c_normalise(n, j, stats_of):
                dve.wait_ge(rstd2_ready, n + 1)
                wait(dve, xT2_psum, n)
                if stats_of is not None:
                    dve.wait_ge(stats2_ready, stats_of + 1)
                dve.tensor_scalar(xn[:, :], x_cur[:, j, :], mean_var[:, j, 0:1], rstd[:, j:j + 1], ALU.subtract, ALU.mult).then_inc(xn2_ready, 1)

            def c_front(n0, b, uses):
                c_gate(n0, b, None)
                c_add(n0, 0, uses)
                c_gate(n0 + 1, b, n0)
                c_mean_and_variance(0)
                c_add(n0 + 1, 1, uses)
                c_normalise(n0, 0, n0 + 1)
                c_mean_and_variance(1)
                c_normalise(n0 + 1, 1, None)

            def c_result(n, j, b, c_no):
                dve.wait_ge(y_psum, n + 1)
                dve.tensor_tensor(gated2[:, j, :], ps[:, 6 + j, 0:H], gate[:, 1, b, :], ALU.mult).then_inc(gated2_ready[j], 1)
                dve.wait_ge(gated2_ready[j], c_no + 1)
                dve.wait_ge(xgb2_ready[j], c_no + 1)
                wait(dve, y_stored[j], 16 * c_no)
                dve.tensor_tensor(y_out[:, j, :], gated2[:, j, :], x_gb2[:, j, :], ALU.add).then_inc(y_ready[j], 1)

            c_front(0, 0, 0)

            def chunk_c(c_no, n0, b, b_next):
                if b_next is not None:
                    c_front(n0 + 2, b_next, c_no + 1)
                for j in range(2):
                    c_result(n0 + j, j, b, c_no)

            pairs_of(dve, chunk_c)


def fold_index():
    place = np.full((D, D), -1)
    rows, cols = np.triu_indices(D, 1)
    place[rows, cols] = np.arange(len(rows))
    index = np.full((D // 2, D), len(rows))
    for r in range(D // 2):
        index[r, r + 1:] = place[r, r + 1:]
        index[r, :r] = place[D - 1 - r, D - 1 - np.arange(r)]
    return index


def kernel(**inputs):
    import concourse.bacc as bacc
    from concourse.bass_utils import run_bass_kernel_spmd

    a = {k: np.asarray(v) for k, v in inputs.items()}
    index = fold_index()
    W = np.concatenate([a["L0_cond_W"], np.zeros((1, H), a["L0_cond_W"].dtype)])
    b = np.concatenate([a["L0_cond_b"], np.zeros(1, a["L0_cond_b"].dtype)])
    arrays = {
        "x": a["x"],
        "cond_t": a["cond_1152"].T,
        "P": a["L0_cond_P"],
        "P_t": a["L0_cond_P"].T,
        "W_fold": W[index.ravel()].T,
        "b_fold": b[index],
        "w_mod": a["L1_cond_w_mod"],
        "b_mod_cols": a["L1_cond_b_mod"].reshape(6, NC, KC).transpose(2, 0, 1),
        "b_mod": a["L1_cond_b_mod"],
        "w_qkv": a["L1_cond_w_qkv"],
        "b_qkv": a["L1_cond_b_qkv"],
        "g_q": a["L1_cond_g_q"],
        "g_k": a["L1_cond_g_k"],
        "w_proj": a["L1_cond_w_proj"],
        "b_proj": a["L1_cond_b_proj"],
        "w1": a["L1_cond_w1"],
        "b1_cols": a["L1_cond_b1"].reshape(FF, P128).T,
        "w2": a["L1_cond_w2"],
        "b2": a["L1_cond_b2"],
    }
    arrays = {f"in_{k}": np.ascontiguousarray(v) for k, v in arrays.items()}
    nc = bacc.Bacc("TRN2", target_bir_lowering=False, num_devices=1)
    args = [nc.dram_tensor(k, v.shape, mybir.dt.from_np(v.dtype), kind="ExternalInput").ap() for k, v in arrays.items()]
    out = nc.dram_tensor("out", (B, T, H), F32, kind="ExternalOutput").ap()
    build(nc, *args, out)
    r = run_bass_kernel_spmd(nc, [arrays], core_ids=[0])
    return r.results[0]["out"]
```

```python
from contextlib import ExitStack

import numpy as np

import concourse.bass as bass
from concourse import mybir

F32 = mybir.dt.float32
F16 = mybir.dt.float16
ALU = mybir.AluOpType
ACT = mybir.ActivationFunctionType
AX = mybir.AxisListType

B, T, H = 2, 1024, 288
D = 64
NH, HD = 16, 18
MLP = 4 * H
P128 = 128
TILES = T // P128
NT = B * TILES
KC = 96
NC = H // KC
HG = 4
GROUPS = B * NH // HG
GW = HG * HD
PARTS = 3
ROWS = 64
HP = HG // 2
PV_LAG = 2
EPS = 1e-6
SCORE_BOUND = 60.0
LAG = 8
SQUARINGS = 8
TAYLOR = 6
ROUNDS = SQUARINGS + TAYLOR
FF = MLP // P128
CH = 256
REM = H - 2 * P128
W_SCALE = 64.0
CHUNKS = B * T // CH
SH_MSA, SC_MSA, G_MSA, SH_MLP, SC_MLP, G_MLP = range(6)

T_AFTER = {9: 0, 12: 1}
O_AFTER = 3


def ring_units():
    at, pairs = 0, []
    for v in range(16):
        units = [("S", 2 * v, at), ("S", 2 * v + 1, at + 1)]
        at += 2
        if v == O_AFTER:
            units.append(("O", 0, at))
            at += 1
        if v in T_AFTER:
            units.append(("T", T_AFTER[v], at))
            at += 1
        pairs.append(units)
    return pairs, -(-at // 3) * 3


RING_PAIRS, RING_LEN = ring_units()
RING_AT = {p: (kind, n) for pair in RING_PAIRS for kind, n, p in pair}


def build(nc, x, x_t, cond_t, P, P_t, W_fold, b_fold, w_mod, b_mod_cols, b_mod, w_qkv, b_qkv, g_q, g_k,
          w_proj, b_proj, w1, b1_cols, w2, b2, b_mlp_cols, out):
    with ExitStack() as ctx:
        def sb(name, shape, dt=F32):
            return ctx.enter_context(nc.sbuf_tensor(name, shape, dt))

        def sem(name):
            return ctx.enter_context(nc.semaphore(name))

        ps = ctx.enter_context(nc.psum_tensor("ps", [P128, 8, 512], F32))

        ident = sb("ident", [P128, P128])
        ident16 = sb("ident16", [P128, P128], F16)
        neg_half = sb("neg_half", [P128, 1])
        x_sb = sb("x_sb", [P128, NT, H])
        o_tok = sb("o_tok", [P128, GROUPS, TILES, GW])
        w_proj_sb = sb("w_proj_sb", [KC, NC, H])
        mod_col = sb("mod_col", [KC, 6, NC, B])
        mod_mlp = sb("mod_mlp", [P128, 2, 3, B])
        gate = sb("gate", [P128, 2, B, H])
        gate_bias = sb("gate_bias", [P128, 2, B, H])
        b1_sb = sb("b1_sb", [P128, FF])
        stats = sb("stats", [P128, 6])
        mean_var = sb("mean_var", [P128, 2, 2])
        var_eps = sb("var_eps", [P128, 2])
        rstd = sb("rstd", [P128, 2])
        xn = sb("xn", [P128, H])
        x_cur = sb("x_cur", [P128, 2, H])
        eps_layer = sb("eps_layer", [P128, 1])
        eps_head = sb("eps_head", [P128, 1])
        bias_row = sb("bias_row", [P128, 3 * H])
        g_row = sb("g_row", [P128, H])
        qkn = sb("qkn", [P128, GROUPS, TILES, 2, HG, HD])
        v_all = sb("v_all", [P128, GROUPS, TILES, HG, HD])

        arena1 = sb("arena1", [P128, 8192])
        w_qkv_sb = arena1[0:KC, 0:NC * 3 * H].rearrange("p (c n) -> p c n", c=NC)
        z0_all = arena1[0:D, 2592:2592 + NT * P128].rearrange("p (t k) -> p t k", t=NT)
        xT = arena1[0:KC, 4640:4640 + 2 * NC * P128].rearrange("p (j c k) -> p j c k", j=2, c=NC)
        qk_sq = arena1[:, 5984:5984 + 2 * H].rearrange("p (a f) -> p a f", a=2)
        k_g = arena1[:, 6560:6560 + H]
        head_ssq = arena1[:, 6848:6848 + 32]
        head_sd = arena1[:, 6880:6880 + 32]
        head_rstd = arena1[:, 6912:6912 + 32]
        z_slot = arena1[0:D, 6944:6944 + 2 * P128].rearrange("p (j k) -> p j k", j=2)
        Y = arena1[0:D, 7200:7200 + B * H].rearrange("p (b f) -> p b f", b=B)
        prob = arena1[:, :].rearrange("p (s q) -> p s q", s=8)

        arena2 = sb("arena2", [P128, 11328])
        Wf = arena2[0:KC, 0:NC * 2048].rearrange("p (c n) -> p c n", c=NC)
        w_mod_sb = arena2[0:KC, 6144:6144 + NC * 6 * H].rearrange("p (c n) -> p c n", c=NC)
        qk_c = arena2[:, 0:4 * H].rearrange("p (j a f) -> p j a f", j=2, a=2)
        qk_op = arena2[:, 0:4096].bitcast(F16).rearrange("p (s a h t) -> p s a h t", s=2, a=2, h=HP)
        qk_split = arena2[:, 4096:6144].bitcast(F16).rearrange("p (t a h r) -> p t a h r", t=TILES, a=2, h=HG)
        c_at = 0

        def c_mem(*shape):
            nonlocal c_at
            n = int(np.prod(shape))
            c_at += n
            names = "abc"[:len(shape)]
            return arena1[:, c_at - n:c_at].rearrange(
                f"p ({' '.join(names)}) -> p {' '.join(names)}", **dict(zip(names, shape)))

        hid = c_mem(FF, CH)
        xn2T = c_mem(3, CH)
        oT2 = c_mem(2, NC, P128)[0:KC]
        o_row, x_gb, x_gb2, gated2, y_out = (c_mem(2, H) for _ in range(5))
        gated = c_mem(H)
        hid_h = arena2[:, 0:1152].bitcast(F16).rearrange("p (m t) -> p m t", m=FF)
        hid_l = arena2[:, 1152:2304].bitcast(F16).rearrange("p (m t) -> p m t", m=FF)
        xn2_h = arena2[:, 2304:2688].bitcast(F16).rearrange("p (c t) -> p c t", c=3)
        xn2_l = arena2[:, 2688:2944].bitcast(F16).rearrange("p (c t) -> p c t", c=2)
        qk_mem = qkn[:, :, :, :, :, :].rearrange("p g t a h d -> p (g t a h d)")
        half_qk = GROUPS // 2 * TILES * 2 * GW
        w1_sb = qk_mem[:, 0:3 * MLP].rearrange("p (c n) -> p c n", c=3)
        w2_sb = qk_mem[:, half_qk:half_qk + FF * H].rearrange("p (m n) -> p m n", m=FF)
        w1_h = arena2[:, 6144:7872].bitcast(F16).rearrange("p (c n) -> p c n", c=3)
        w1_l = arena2[:, 7872:9024].bitcast(F16).rearrange("p (c n) -> p c n", c=2)
        w2_h = arena2[:, 9024:10320].bitcast(F16).rearrange("p (m n) -> p m n", m=FF)
        w2_l = v_all[:, :, :, :, :].rearrange("p g t h d -> p (g t h d)")[:, 0:1296].bitcast(F16).rearrange("p (m n) -> p m n", m=FF)

        v_op = sb("v_op", [P128, 2, TILES, HG, 32])
        o_acc = sb("o_acc", [P128, T])
        den_inv = sb("den_inv", [P128, TILES, HG])

        q_factor = sb("q_factor", [P128, 1])
        unshifted_ok = sb("unshifted_ok", [1, 1], mybir.dt.int32)
        row_p = arena1[:, 0:T]
        row_pT = arena1[:, 1024:1024 + T]
        row_ops = arena1[0:HD, 2048:2048 + 2 * T].rearrange("p (a t) -> p a t", a=2)
        row_q = arena1[0:HD, 4096:4096 + P128]
        row_qk = arena1[:, 4224:4224 + 2 * TILES * HD].rearrange("p (a t d) -> p a t d", a=2, t=TILES)
        row_v = arena1[:, 4512:4512 + TILES * HD].rearrange("p (t d) -> p t d", t=TILES)
        row_max, row_shift, row_den, row_rcp = (arena1[:, 4656 + i:4657 + i] for i in range(4))

        arena3 = o_tok[0:D, :, :, :].rearrange("p g t f -> p (g t f)")
        elim_mask = arena3[:, 0:D * D].rearrange("p (k i) -> p k i", k=D)
        flip = sb("flip", [D, D])
        neg_i = sb("neg_i", [32, 32])
        scaled_i = v_op[0:D, 0, 0:5, :, :].rearrange("p j a b -> p (j a b)")[:, 0:5 * D].rearrange("p (j i) -> p j i", j=5)
        ident4 = v_op[0:D, 1, 0:2, :, :].rearrange("p j a b -> p (j a b)").rearrange("p (j i) -> p j i", j=4)
        fold_up = sb("fold_up", [32, D])
        fold_low = sb("fold_low", [32, D])
        P_sb = sb("P_sb", [KC, NC, D])
        P_top = sb("P_top", [D, D])
        Pt_sb = sb("Pt_sb", [D, H])
        cond_sb = sb("cond_sb", [KC, NC, B])
        ex = sb("ex", [KC, NC, B])
        silu = sb("silu", [KC, NC, 32])
        bf = sb("bf", [32, D])
        z_row = sb("z_row", [D, P128])
        z_col = sb("z_col", [D, D])
        z_rcp = sb("z_rcp", [D, 1])
        diag = sb("diag", [D, 1])
        diag_rs = sb("diag_rs", [D, 1])
        junk = sb("junk", [D, D])
        R_half = sb("R_half", [D, D])
        pivot_half = sb("pivot_half", [D, 1])
        pivot_rcp = sb("pivot_rcp", [D, 1])
        signs = sb("signs", [D, D])
        w_row = sb("w_row", [D, 2, D])
        m_col = sb("m_col", [D, 2, D])
        sign_of = sb("sign_of", [D, 1])
        Winv = sb("Winv", [D, D])
        head_mem = o_acc[:, :]
        v_sb = head_mem[:, 0:512]
        fold = head_mem[0:32, 512:640].rearrange("p (b j) -> p b j", b=B)
        fold_b = head_mem[0:32, 640:768].rearrange("p (b j) -> p b j", b=B)
        v_up = head_mem[0:32, 768:896].rearrange("p (b j) -> p b j", b=B)
        v_low = head_mem[0:32, 896:1024].rearrange("p (b j) -> p b j", b=B)
        lowT = arena3[:, 4096:4224].rearrange("p (b j) -> p b j", b=B)
        neg_lowT = arena3[:, 4224:4288].rearrange("p (b j) -> p b j", b=B)
        skew = qk_mem[0:D, 0:256].rearrange("p (m j) -> p m j", m=4)
        X = qk_mem[0:D, 256:768].rearrange("p (s m j) -> p s m j", s=2, m=4)
        FW = qk_mem[0:D, 768:896].rearrange("p (b j) -> p b j", b=B)
        Kt = qk_mem[0:D, 896:1024].rearrange("p (b j) -> p b j", b=B)
        bm_mlp = qk_mem[:, 4288:4294].rearrange("p (s c) -> p s c", s=2)
        mod_row = qk_mem[:, 1024:1024 + 2 * H].rearrange("p (r f) -> p r f", r=2)
        bm_col = qk_mem[0:KC, 1600:1618].rearrange("p (s c) -> p s c", s=6)
        bm_row = qk_mem[:, 1632:1632 + 2 * H].rearrange("p (r f) -> p r f", r=2)
        bo_row = qk_mem[:, 2208:2208 + 2 * H].rearrange("p (r f) -> p r f", r=2)
        gq_row = qk_mem[:, 2784:2784 + H]
        gk_row = qk_mem[:, 3072:3072 + H]
        w_sum = qk_mem[0:KC, 3360:3360 + NC * 32].rearrange("p (c h) -> p c h", c=NC)
        b_sum = qk_mem[:, 3456:3456 + 32]
        xT_head = [qk_mem[0:KC, 4352:4352 + NC * T].rearrange("p (c t) -> p c t", c=NC),
                   v_all[0:KC, :, :, :, :].rearrange("p g t h d -> p (g t h d)")[:, 0:NC * T].rearrange("p (c t) -> p c t", c=NC)]
        v_dram = nc.dram_tensor("v_scratch", [B, 4, 512], F32).ap()

        xt_loaded = [sem(f"xt_loaded{b}") for b in range(B)]
        p_loaded, cond_loaded, x_loaded, wf_loaded = sem("p_loaded"), sem("cond_loaded"), sem("x_loaded"), sem("wf_loaded")
        wqkv_loaded, mod_loaded, row_loaded, proj_loaded = sem("wqkv_loaded"), sem("mod_loaded"), sem("row_loaded"), sem("proj_loaded")
        w1_loaded, w2_loaded = sem("w1_loaded"), sem("w2_loaded")
        v_stored, fold_loaded = sem("v_stored"), sem("fold_loaded")
        const_step, ident_ready, mask_ready, const_ready = sem("const_step"), sem("ident_ready"), sem("mask_ready"), sem("const_ready")
        z_ready, m_ready, n_ready = sem("z_ready"), sem("m_ready"), sem("n_ready")
        zrcp_ready, zrow_ready, zcol_ready = sem("zrcp_ready"), sem("zrow_ready"), sem("zcol_ready")
        diag_ready, diagrs_ready, r_ready = sem("diag_ready"), sem("diagrs_ready"), sem("r_ready")
        sign_step, pivot_ready, prcp_ready = sem("sign_step"), sem("pivot_ready"), sem("prcp_ready")
        w_ready, c_ready, sign_ready, winv_ready = sem("w_ready"), sem("c_ready"), sem("sign_ready"), sem("winv_ready")
        silu_step, silu_ready = sem("silu_step"), sem("silu_ready")
        v_ready, vsb_ready, foldb_ready, vparts_ready = sem("v_ready"), sem("vsb_ready"), sem("foldb_ready"), sem("vparts_ready")
        lowT_psum, lowT_ready, skew_psum, skew_ready = sem("lowT_psum"), sem("lowT_ready"), sem("skew_psum"), sem("skew_ready")
        xp_ready, x_ready, k_psum, k_ready = sem("xp_ready"), sem("x_ready"), sem("k_psum"), sem("k_ready")
        z0_psum, z0_ready = sem("z0_psum"), sem("z0_ready")
        mod_psum, modrow_ready, modT_psum, modcol_ready = sem("mod_psum"), sem("modrow_ready"), sem("modT_psum"), sem("modcol_ready")
        mlpT_psum, modmlp_ready, w_half, w_split, hh_ready, hl_ready, xh_ready, xsplit_ready = (
            sem("mlpT_psum"), sem("modmlp_ready"), sem("w_half"), sem("w_split"), sem("hh_ready"), sem("hl_ready"),
            sem("xh_ready"), sem("xsplit_ready"))
        gate_psum, gate_ready, wsum_ready, wscale, wcen_ready, rows_ready = (
            sem("gate_psum"), sem("gate_ready"), sem("wsum_ready"), sem("wscale"), sem("wcen_ready"), sem("rows_ready"))
        zslot_ready, xkept, qkv_psum, qkv_used = sem("zslot_ready"), sem("xkept"), sem("qkv_psum"), sem("qkv_used")
        rot_ready, xrot_ready, stats_ready, mv_ready = sem("rot_ready"), sem("xrot_ready"), sem("stats_ready"), sem("mv_ready")
        vareps_ready, rstd_ready, xn_ready, xT_psum, xT_ready = sem("vareps_ready"), sem("rstd_ready"), sem("xn_ready"), sem("xT_psum"), sem("xT_ready")
        qkc_ready, sq_ready, ssq_ready, kg_ready, hsd_ready, hrstd_ready, qkn_ready = (
            sem("qkc_ready"), sem("sq_ready"), sem("ssq_ready"), sem("kg_ready"), sem("hsd_ready"), sem("hrstd_ready"), sem("qkn_ready"))
        split_h, split_ready = sem("split_h"), sem("split_ready")
        t_psum, op_ready, s_ready, exp_done, pv_done = sem("t_psum"), sem("op_ready"), sem("s_ready"), sem("exp_done"), sem("pv_done")
        vop_set, vop_ready, oacc_ready, oT_psum, den_ready, o_ready = (
            sem("vop_set"), sem("vop_ready"), sem("oacc_ready"), sem("oT_psum"), sem("den_ready"), sem("o_ready"))
        g_step, flag_ready, row_in, row_turned, row_ops_ready, row_q_ready = (
            sem("g_step"), sem("flag_ready"), sem("row_in"), sem("row_turned"), sem("row_ops_ready"), sem("row_q_ready"))
        row_s, row_max_ready, row_shift_ready, row_exp, row_pt_psum, row_pt_ready, row_o, row_rcp_ready, row_done = (
            sem("row_s"), sem("row_max_ready"), sem("row_shift_ready"), sem("row_exp"), sem("row_pt_psum"), sem("row_pt_ready"),
            sem("row_o"), sem("row_rcp_ready"), sem("row_done"))
        orow_ready, xgb_ready, oT2_psum, oT2_ready = sem("orow_ready"), sem("xgb_ready"), sem("oT2_psum"), sem("oT2_ready")
        proj_ready, gated_ready, x2_ready, stats2_ready, mv2_ready = (
            sem("proj_ready"), sem("gated_ready"), sem("x2_ready"), sem("stats2_ready"), sem("mv2_ready"))
        vareps2_ready, rstd2_ready, xn2_ready, xT2_psum, xT2_ready = (
            sem("vareps2_ready"), sem("rstd2_ready"), sem("xn2_ready"), sem("xT2_psum"), sem("xT2_ready"))
        h_psum, h_ready, y_psum = (
            sem("h_psum"), sem("h_ready"), sem("y_psum"))
        xgb2_ready = [sem(f"xgb2_ready{j}") for j in range(2)]
        gated2_ready = [sem(f"gated2_ready{j}") for j in range(2)]
        y_ready = [sem(f"y_ready{j}") for j in range(2)]
        y_stored = [sem(f"y_stored{j}") for j in range(2)]

        block = ctx.enter_context(nc.Block())

        def wait(eng, s, value):
            if not isinstance(value, int) or value > 0:
                eng.wait_ge(s, value)

        def pairs_of(eng, body):
            half = TILES // 2
            for b in range(B):
                if b == 0:
                    body(0, 0, 0, 0)
                with eng.Fori(1 if b == 0 else 0, half - 1) as i:
                    body(half * b + i, TILES * b + 2 * i, b, b)
                body(half * (b + 1) - 1, TILES * (b + 1) - 2, b, b + 1 if b + 1 < B else None)

        def tiles_of(eng, step):
            def batches(t):
                return {d: (t + d) // TILES if 0 <= t + d < NT else None for d in range(-1, 3)}

            for b in range(B):
                for t in (0, 1):
                    step(TILES * b + t, t, batches(TILES * b + t))
                with eng.Fori(0, TILES // 2 - 2) as i:
                    for j in range(2):
                        step(TILES * b + 2 * i + (2 + j), j, batches(TILES * b + 2))
                for t in (TILES - 2, TILES - 1):
                    step(TILES * b + t, t % 2, batches(TILES * b + t))

        def where(eng, shifted, body):
            eng.wait_ge(flag_ready, 2)
            ok = eng.value_load(unshifted_ok[0:1, 0:1], min_val=0, max_val=1)
            with eng.If(ok < 1 if shifted else ok > 0):
                body()

        def where_shifted(eng, body):
            where(eng, True, body)

        def head_rows(eng, of_head, of_tile):
            with eng.Fori(0, GROUPS) as g:
                with eng.Fori(0, HG) as h:
                    of_head(g, h, HG * g + h)
                    with eng.Fori(0, TILES) as t:
                        of_tile(g, h, t, (HG * g + h) * TILES + t)

        ROW_TILES = B * NH * TILES

        @block.sync
        def _(sp):
            sp.dma_start(P_sb[:, :, :], P.rearrange("(c p) d -> p c d", p=KC)).then_inc(p_loaded, 16)
            sp.dma_start(P_top[:, :], P[0:D, :]).then_inc(p_loaded, 16)
            sp.dma_start(cond_sb[:, :, :], cond_t.rearrange("(c p) b -> p c b", p=KC)).then_inc(cond_loaded, 16)
            for b in range(B):
                sp.dma_start(xT_head[b], x_t[b].rearrange("(c p) t -> p c t", p=KC)).then_inc(xt_loaded[b], 16)
            sp.dma_start(Wf, W_fold.rearrange("(c p) n -> p c n", p=KC)).then_inc(wf_loaded, 16)
            sp.dma_start(bf[:, :], b_fold).then_inc(wf_loaded, 16)
            sp.dma_start(Pt_sb[:, :], P_t).then_inc(wf_loaded, 16)
            sp.dma_start(w_qkv_sb, w_qkv.rearrange("(c p) n -> p c n", p=KC)).then_inc(wqkv_loaded, 16)
            sp.dma_start(bias_row[:, :], b_qkv.partition_broadcast(P128)).then_inc(wqkv_loaded, 16)
            for b in range(B):
                sp.dma_start(x_sb[:, TILES * b:TILES * b + TILES, :],
                             x[b].rearrange("(t p) f -> p t f", p=P128)).then_inc(x_loaded, 16)
            sp.dma_start(w_mod_sb, w_mod.rearrange("(c p) n -> p c n", p=KC)).then_inc(mod_loaded, 16)
            sp.dma_start(bm_col, b_mod_cols).then_inc(mod_loaded, 16)
            sp.dma_start(bm_mlp, b_mlp_cols).then_inc(mod_loaded, 16)
            for row, g in ((gq_row, g_q), (gk_row, g_k)):
                sp.dma_start(row.rearrange("p (h d) -> p h d", d=HD),
                             g.partition_broadcast(NH).partition_broadcast(P128)).then_inc(row_loaded, 16)
            for r, blk in enumerate((G_MSA, G_MLP)):
                sp.dma_start(bm_row[:, r, :], b_mod[H * blk:H * blk + H].partition_broadcast(P128)).then_inc(row_loaded, 16)
            for r, bias in enumerate((b_proj, b2)):
                sp.dma_start(bo_row[:, r, :], bias.partition_broadcast(P128)).then_inc(row_loaded, 16)
            sp.dma_start(w_proj_sb[:, :, :], w_proj.rearrange("(c p) n -> p c n", p=KC)).then_inc(proj_loaded, 16)
            sp.dma_start(b1_sb[:, :], b1_cols).then_inc(proj_loaded, 16)
            sp.wait_ge(vsb_ready, 1)
            for b in range(B):
                sp.dma_start(v_dram[b], v_sb[b:b + 97:32, :]).then_inc(v_stored, 16)
            sp.wait_ge(v_stored, 16 * B)
            sp.dma_start(fold, v_dram.rearrange("b g (r j) -> (g r) b j", j=D)).then_inc(fold_loaded, 16)
            where_shifted(sp, lambda: sp.wait_ge(row_done, ROW_TILES))
            sp.wait_ge(split_ready, 4 * (GROUPS // 2))
            sp.dma_start(w1_sb[:, 0:2, :], w1[0:2 * P128, :].rearrange("(c p) n -> p c n", p=P128)).then_inc(w1_loaded, 16)
            for g in range(PARTS):
                sp.dma_start(w1_sb[REM * g:REM * g + REM, 2, :], w1[2 * P128:H, :]).then_inc(w1_loaded, 16)
            sp.wait_ge(split_ready, 4 * GROUPS)
            sp.dma_start(w2_sb, w2.rearrange("(m p) n -> p m n", p=P128)).then_inc(w2_loaded, 16)
            out_t = out.rearrange("b (c j p) f -> (b c) p j f", p=P128, j=2)
            with sp.Fori(0, CHUNKS) as c:
                for j in range(2):
                    sp.wait_ge(y_ready[j], c + 1)
                    sp.dma_start(out_t[bass.ds(c, 1), :, j, :].rearrange("c p f -> p (c f)"), y_out[:, j, :]).then_inc(y_stored[j], 16)
            for j in range(2):
                sp.wait_ge(y_stored[j], 16 * CHUNKS)

        @block.gpsimd
        def _(pool):
            n_const = 0

            def step(ins):
                nonlocal n_const
                n_const += 1
                ins.then_inc(const_step, 1)
                pool.wait_ge(const_step, n_const)

            def select(ap, op, fill, base, pattern, mult):
                return pool.affine_select(out=ap, in_=ap, compare_op=op, fill=fill, base=base, pattern=pattern,
                                          channel_multiplier=mult)

            step(pool.memset(ident[:, :], 0.0))
            select(ident[:, :], ALU.not_equal, 1.0, 0, [[-1, P128]], 1).then_inc(ident_ready, 1)
            pool.memset(neg_half[:, :], -0.5).then_inc(const_step, 1)
            n_const += 1
            pool.memset(eps_layer[:, :], EPS).then_inc(const_step, 1)
            pool.memset(eps_head[:, :], HD * EPS).then_inc(const_step, 1)
            n_const += 2
            n_rs = 0

            def diagonal_rsqrt():
                nonlocal n_rs
                n_rs += 1
                pool.wait_ge(diag_ready, n_rs)
                pool.tensor_tensor(diag_rs[:, :], diag[:, :], neg_half[0:D, 0:1], ALU.pow).then_inc(diagrs_ready, 1)

            for c in range(8):
                if c == 5:
                    diagonal_rsqrt()
                part = elim_mask[:, 8 * c:8 * c + 8, :]
                step(pool.memset(part, -1.0))
                step(select(part, ALU.is_equal, 0.0, -8 * c, [[-1, 8], [0, D]], 1))
                select(part, ALU.is_gt, 0.0, -8 * c, [[-1, 8], [1, D]], 0).then_inc(mask_ready, 1)
                if c == 0:
                    pool.memset(silu[:, :, :], 0.0).then_inc(silu_step, 1)
                    pool.wait_ge(silu_step, 2)
                    pool.tensor_scalar(ex[:, :, :], ex[:, :, :], 1.0, None, ALU.add).then_inc(silu_step, 1)
            step(pool.memset(flip[:, :], 0.0))
            step(select(flip[:, :], ALU.not_equal, 1.0, -(D - 1), [[1, D]], 1))
            step(pool.memset(neg_i[:, :], 0.0))
            step(select(neg_i[:, :], ALU.not_equal, -1.0, 0, [[-1, 32]], 1))
            for m, sign in ((fold_up, 1), (fold_low, -1)):
                step(pool.memset(m[:, :], 1.0))
                step(select(m[:, :], ALU.is_gt, 0.0, 0, [[sign, D]], -sign))
            for j in range(5):
                step(pool.memset(scaled_i[:, j, :], 0.0))
                step(select(scaled_i[:, j, :], ALU.not_equal, float(j + 2), 0, [[-1, D]], 1))
            for j in range(4):
                step(pool.memset(ident4[:, j, :], 0.0))
                step(select(ident4[:, j, :], ALU.not_equal, 1.0, 0, [[-1, D]], 1))
            step(pool.memset(ident16[:, :], 0.0))
            step(select(ident16[:, :], ALU.not_equal, 1.0, 0, [[-1, P128]], 1))
            pool.memset(lowT, 0.0).then_inc(const_ready, 1)

            diagonal_rsqrt()
            for c in range(NC + 1):
                s = w_sum[:, c, :] if c < NC else b_sum
                w = (w_qkv_sb[:, c, 0:2 * H] if c < NC else bias_row[:, 0:2 * H]).rearrange("p (h d) -> p h d", d=HD)
                pool.wait_ge(wsum_ready, c + 1)
                pool.tensor_scalar(s, s, -1.0 / HD, None, ALU.mult).then_inc(wscale, 1)
                pool.wait_ge(wscale, c + 1)
                pool.tensor_tensor(w, w, s.unsqueeze(2).broadcast_to([s.shape[0], 32, HD]), ALU.add).then_inc(wcen_ready, 1)
                if c == 1:
                    diagonal_rsqrt()
            diagonal_rsqrt()
            pool.wait_ge(fold_loaded, 16)
            pool.wait_ge(wf_loaded, 48)
            pool.tensor_tensor(fold_b, fold, bf[:, :].unsqueeze(1).broadcast_to([32, B, D]), ALU.add).then_inc(foldb_ready, 1)
            pool.wait_ge(foldb_ready, 1)
            for part, mask in ((v_up, fold_up), (v_low, fold_low)):
                pool.tensor_tensor(part, fold_b, mask[:, :].unsqueeze(1).broadcast_to([32, B, D]), ALU.mult).then_inc(vparts_ready, 1)
            pool.wait_ge(row_loaded, 16 * 6)
            pool.tensor_tensor(g_row[:, :], gq_row, gk_row, ALU.mult).then_inc(rows_ready, 1)
            pool.wait_ge(rows_ready, 1)
            pool.tensor_scalar(g_row[:, :], g_row[:, :], float(HD), None, ALU.mult).then_inc(rows_ready, 1)
            for _ in range(4):
                diagonal_rsqrt()
            pool.wait_ge(gate_ready, 4)
            for r in range(2):
                for b in range(B):
                    pool.tensor_tensor(gate_bias[:, r, b, :], gate[:, r, b, :], bo_row[:, r, :], ALU.mult).then_inc(rows_ready, 1)

            def layer_rstd(n, j):
                pool.wait_ge(mv_ready, n + 1)
                pool.tensor_tensor(var_eps[:, 0:1], mean_var[:, 0, 1:2], eps_layer[:, :], ALU.add).then_inc(vareps_ready, 1)
                pool.wait_ge(vareps_ready, n + 1)
                pool.tensor_tensor(rstd[:, 0:1], var_eps[:, 0:1], neg_half[:, 0:1], ALU.pow).then_inc(rstd_ready, 1)
                pool.tensor_copy(x_sb[:, bass.ds(n, 1), :].rearrange("p t f -> p (t f)"), x_cur[:, j, :]).then_inc(xkept, 1)

            pool.wait_ge(flag_ready, 2)
            layer_rstd(0, 0)

            def step_a(n, j, batch):
                if batch[1] is not None:
                    layer_rstd(n + 1, 1 - j)
                if isinstance(n, int) and n == TILES + 1:
                    pool.wait_ge(qkv_used, TILES)
                    for g in range(2):
                        copy_v(g, g)
                pool.wait_ge(qkc_ready, 2 * n + 2)
                wait(pool, qkn_ready, 2 * n)
                pool.tensor_tensor(k_g, qk_c[:, j, 1, :], g_row[:, :], ALU.mult).then_inc(kg_ready, 1)

            def copy_v(g, par):
                wait(pool, pv_done, 16 * g - 16)
                pool.tensor_copy(v_op[:, par, :, :, 0:HD].rearrange("p t h d -> p (t h) d"),
                                 v_all[:, bass.ds(g, 1), :, :, :].rearrange("p g t h d -> p (g t h d)")).then_inc(vop_ready, 1)

            pool.memset(v_op[:, :, :, :, HD:HD + 1], 1.0).then_inc(vop_set, 1)
            pool.memset(v_op[:, :, :, :, HD + 1:32], 0.0).then_inc(vop_set, 1)
            pool.memset(qk_split[:, :, :, :, PARTS * HD:ROWS], 0.0).then_inc(vop_set, 1)
            tiles_of(pool, step_a)

            pool.wait_ge(qkv_used, NT)
            with pool.Fori(0, GROUPS // 2 - 1) as i:
                copy_v(2 * i + 2, 0)
                copy_v(2 * i + 3, 1)

            def c_inputs(n, j, b):
                t = n - TILES * b
                wait(pool, oT2_psum, n - 1)
                pool.tensor_copy(o_row[:, j, :].rearrange("p (g f) -> p g f", g=4),
                                 o_tok[:, 4 * b:4 * b + 4, bass.ds(t, 1), :].rearrange("p g t f -> p g (t f)")).then_inc(orow_ready, 1)
                wait(pool, x2_ready, n - 1)
                pool.tensor_tensor(x_gb[:, j, :], x_sb[:, bass.ds(n, 1), :].rearrange("p t f -> p (t f)"),
                                   gate_bias[:, 0, b, :], ALU.add).then_inc(xgb_ready, 1)

            def c_rstd(n, j):
                pool.wait_ge(mv2_ready, n + 1)
                pool.tensor_tensor(var_eps[:, j:j + 1], mean_var[:, j, 1:2], eps_layer[:, :], ALU.add).then_inc(vareps2_ready, 1)
                pool.wait_ge(vareps2_ready, n + 1)
                pool.tensor_tensor(rstd[:, j:j + 1], var_eps[:, j:j + 1], neg_half[:, 0:1], ALU.pow).then_inc(rstd2_ready, 1)

            def c_out_residual(c_no, n, j, b):
                wait(pool, y_ready[j], c_no)
                pool.tensor_tensor(x_gb2[:, j, :], x_cur[:, j, :],
                                   gate_bias[:, 1, b, :], ALU.add).then_inc(xgb2_ready[j], 1)


            pool.wait_ge(o_ready, GROUPS)
            where_shifted(pool, lambda: pool.wait_ge(row_done, ROW_TILES))
            for j in range(2):
                c_inputs(j, j, 0)
            for j in range(2):
                c_rstd(j, j)

            def chunk_c(c_no, n0, b, b_next):
                if b_next is not None:
                    for j in range(2):
                        c_inputs(n0 + 2 + j, j, b_next)
                for j in range(2):
                    c_out_residual(c_no, n0 + j, j, b)
                if b_next is not None:
                    for j in range(2):
                        c_rstd(n0 + 2 + j, j)

            pairs_of(pool, chunk_c)

        @block.scalar
        def _(act):
            act.wait_ge(cond_loaded, 16)
            act.activation(ex[:, :, :], cond_sb[:, :, :], ACT.Exp, scale=-1.0).then_inc(silu_step, 1)

            def keep_z0(q):
                act.wait_ge(z0_psum, q + 1)
                act.activation(z0_all[:, 2 * q:2 * q + 2, :].rearrange("p t k -> p (t k)"), ps[0:D, 5 + q % 2, 0:256], ACT.Copy).then_inc(z0_ready, 1)

            for q in range(6):
                keep_z0(q)
            act.wait_ge(v_ready, 1)
            act.activation(v_sb, ps[:, 3, :], ACT.Copy).then_inc(vsb_ready, 1)
            for q in range(6, 8):
                keep_z0(q)
            act.wait_ge(lowT_psum, 1)
            act.wait_ge(const_ready, 1)
            low = ps[0:D, 4, 0:B * 32].rearrange("p (b r) -> p b r", b=B)
            act.activation(lowT[:, :, 32:D], low, ACT.Copy).then_inc(lowT_ready, 1)
            act.activation(neg_lowT, low, ACT.Copy, scale=-1.0).then_inc(lowT_ready, 1)
            act.wait_ge(skew_psum, 1)
            sk = ps[0:D, 3, 0:B * D].rearrange("p (b j) -> p b j", b=B)
            act.activation(skew[:, 0:2, :], sk, ACT.Copy, scale=2.0 ** -SQUARINGS).then_inc(skew_ready, 1)
            act.activation(skew[:, 2:4, :], sk, ACT.Copy, scale=-2.0 ** -SQUARINGS).then_inc(skew_ready, 1)

            def expm_round(n):
                j = TAYLOR - n
                act.wait_ge(xp_ready, n + 1)
                act.activation(X[:, n % 2, :, :], ps[0:D, 3 + (n + 1) % 2, 0:4 * D].rearrange("p (m j) -> p m j", m=4),
                               ACT.Copy, scale=1.0 / j if j > 1 else 1.0).then_inc(x_ready, 1)

            for n in range(3):
                expm_round(n)
            act.wait_ge(mod_psum, 1)
            act.activation(mod_row[:, 0, :], ps[:, 5, 0:H], ACT.Copy).then_inc(modrow_ready, 1)
            expm_round(3)
            act.wait_ge(mod_psum, 2)
            act.activation(mod_row[0:64, 1, :], ps[0:64, 6, 0:H], ACT.Copy).then_inc(modrow_ready, 1)
            for n in range(4, ROUNDS):
                expm_round(n)
            act.wait_ge(k_psum, 1)
            act.activation(FW, ps[0:D, 3, 0:B * D].rearrange("p (b j) -> p b j", b=B), ACT.Copy).then_inc(k_ready, 1)
            act.wait_ge(k_psum, 2)
            act.activation(Kt, ps[0:D, 4, 0:B * D].rearrange("p (b j) -> p b j", b=B), ACT.Copy).then_inc(k_ready, 1)
            for b in range(B):
                act.wait_ge(k_psum, 3 + b)
                act.activation(Y[:, b, :], ps[0:D, 5 + b, 0:H], ACT.Copy).then_inc(k_ready, 1)

            def fill_z(n, j):
                wait(act, rot_ready, n - 1)
                act.activation(z_slot[:, j, :], z0_all[:, bass.ds(n, 1), :].rearrange("p t k -> p (t k)"),
                               ACT.Copy).then_inc(zslot_ready, 1)

            def modulate(n, j, b):
                act.wait_ge(xT_psum, n + 1)
                wait(act, qkv_psum, 3 * n - 3)
                for c in range(NC):
                    ins = act.activation(xT[:, j, c, :], ps[0:KC, 1, P128 * c:P128 * c + P128], ACT.Identity,
                                         scale=mod_col[:, SC_MSA, c, b:b + 1], bias=mod_col[:, SH_MSA, c, b:b + 1])
                ins.then_inc(xT_ready, 1)

            def head_deviation(n):
                act.wait_ge(ssq_ready, n + 1)
                wait(act, hrstd_ready, n)
                act.activation(head_sd, head_ssq, ACT.Sqrt, bias=eps_head[:, :]).then_inc(hsd_ready, 1)

            act.wait_ge(z0_ready, NT // 2)
            for n in range(2):
                fill_z(n, n)
            act.wait_ge(modcol_ready, 3)
            modulate(0, 0, 0)

            def step_a(n, j, batch):
                if batch[-1] is not None:
                    head_deviation(n - 1)
                if batch[2] is not None:
                    fill_z(n + 2, j)
                if batch[1] is not None:
                    modulate(n + 1, 1 - j, batch[1])
                act.wait_ge(qkc_ready, 2 * n + 2)
                wait(act, ssq_ready, n)
                act.activation(qk_sq, qk_c[:, j, :, :], ACT.Square).then_inc(sq_ready, 1)

            tiles_of(act, step_a)
            head_deviation(NT - 1)

            def exp_unit(g, u):
                act.wait_ge(s_ready, 32 * g + u + 1)
                wait(act, pv_done, 16 * g + u // 2 - 3)
                act.activation(prob[:, u % 8, :], ps[:, 2 * slot_of(u):2 * slot_of(u) + 2, :].rearrange("p a q -> p (a q)"),
                               ACT.Exp, scale=HD ** -0.5).then_inc(exp_done, 1)

            def slot_of(u):
                return next(p for pair in RING_PAIRS for kind, n, p in pair if (kind, n) == ("S", u)) % 3

            def group_b(g):
                for u in range(32):
                    exp_unit(g, u)

            group_b(0)
            with act.Fori(0, GROUPS // 2 - 1) as i:
                group_b(2 * i + 1)
                group_b(2 * i + 2)
            group_b(GROUPS - 1)

            def row_tile_act(g, h, t, n):
                act.wait_ge(row_shift_ready, n + 1)
                act.activation(row_p, ps[:, 4:6, :].rearrange("p a q -> p (a q)"), ACT.Exp, scale=HD ** -0.5,
                               bias=row_shift, accum_out=row_den).then_inc(row_exp, 1)

            where_shifted(act, lambda: head_rows(act, lambda g, h, m: None, row_tile_act))

            def c_turn_o(n, j):
                act.wait_ge(oT2_psum, n + 1)
                wait(act, proj_ready, n - 1)
                act.activation(oT2[:, j, :, :], ps[0:KC, 0, 0:NC * P128].rearrange("p (c k) -> p c k", c=NC),
                               ACT.Copy).then_inc(oT2_ready, 1)

            def c_turn_x(n, j, b):
                act.wait_ge(xT2_psum, n + 1)
                for c in range(3):
                    rows = P128 if c < 2 else PARTS * REM
                    ins = act.activation(xn2T[0:rows, c, P128 * j:P128 * j + P128], ps[0:rows, 2, P128 * c:P128 * c + P128],
                                         ACT.Identity, scale=mod_mlp[0:rows, 1, c, b:b + 1], bias=mod_mlp[0:rows, 0, c, b:b + 1])
                ins.then_inc(xT2_ready, 1)

            for j in range(2):
                c_turn_o(j, j)
            for j in range(2):
                c_turn_x(j, j, 0)

            def chunk_c(c_no, n0, b, b_next):
                for m in range(FF):
                    act.wait_ge(h_psum, FF * c_no + m + 1)
                    act.activation(hid[:, m, :], ps[:, 3 + m % 3, 0:CH], ACT.Gelu_apprx_tanh,
                                   scale=1.0 / W_SCALE, bias=b1_sb[:, m:m + 1]).then_inc(h_ready, 1)
                    if b_next is not None and m in (1, 4):
                        c_turn_o(n0 + 2 + (m == 4), int(m == 4))
                if b_next is not None:
                    for j in range(2):
                        c_turn_x(n0 + 2 + j, j, b_next)

            pairs_of(act, chunk_c)

        @block.tensor
        def _(pe):
            Z, M, N = ps[:, 0, :], ps[:, 1, :], ps[:, 2, :]
            pe.wait_ge(p_loaded, 32)
            for c in range(NC):
                pe.matmul(Z[0:D, 0:D], P_sb[:, c, :], P_sb[:, c, :], start=(c == 0), stop=(c == NC - 1))
            pe.wait_ge(ident_ready, 1)
            pe.matmul(Z[0:D, D:2 * D], ident[0:D, 0:D], ident[0:D, 0:D], start=False, stop=False,
                      skip_group_check=True).then_inc(z_ready, 1)
            pe.matmul(M[0:D, 0:D], ident[0:D, 0:D], P_top[:, :], start=True, stop=False, skip_group_check=True).then_inc(m_ready, 1)
            pe.matmul(N[0:D, 0:D], P_top[:, :], ident[0:D, 0:D], start=True, stop=False, skip_group_check=True).then_inc(n_ready, 1)

            def update_z(k):
                pe.wait_ge(zrow_ready, k + 1)
                pe.wait_ge(zcol_ready, k + 1)
                pe.matmul(Z[0:D, k + 1:k + 1 + D], z_col[:, :], z_row[:, k + 1:k + 1 + D], start=False, stop=False,
                          skip_group_check=True).then_inc(z_ready, 1)

            def update_mn(k):
                pe.wait_ge(w_ready, k + 1)
                pe.wait_ge(c_ready, k + 1)
                pe.matmul(M[0:D, k + 1:D], m_col[:, k % 2, :], w_row[:, k % 2, k + 1:D], start=False, stop=False,
                          skip_group_check=True).then_inc(m_ready, 1)
                pe.matmul(N[0:D, k + 1:D], w_row[:, k % 2, :], m_col[:, k % 2, k + 1:D], start=False, stop=False,
                          skip_group_check=True).then_inc(n_ready, 1)

            def head_z0(q, c):
                if c == 0 and q % 4 == 0:
                    pe.wait_ge(xt_loaded[q // 4], 16)
                if c == 0:
                    wait(pe, z0_ready, q - 1)
                mm = pe.matmul(ps[0:D, 5 + q % 2, 0:256], P_sb[:, c, :], xT_head[q // 4][:, c, 256 * (q % 4):256 * (q % 4) + 256],
                               start=(c == 0), stop=(c == NC - 1))
                if c == NC - 1:
                    mm.then_inc(z0_psum, 1)

            def angles(c):
                if c == 0:
                    pe.wait_ge(wf_loaded, 48)
                    pe.wait_ge(silu_ready, 1)
                for g in range(4):
                    mm = pe.matmul(ps[32 * g:32 * g + 32, 3, :], silu[:, c, :], Wf[:, c, 512 * g:512 * g + 512],
                                   start=(c == 0), stop=(c == NC - 1), tile_position=(0, 32 * g))
                if c == NC - 1:
                    mm.then_inc(v_ready, 1)

            def lower_half():
                pe.wait_ge(vparts_ready, 2)
                for b in range(B):
                    mm = pe.matmul(ps[0:D, 4, 32 * b:32 * b + 32], v_low[:, b, :], flip[0:32, 32:64], start=True, stop=True)
                mm.then_inc(lowT_psum, 1)

            def skew_matrix():
                pe.wait_ge(lowT_ready, 2)
                for b in range(B):
                    a = ps[0:D, 3, D * b:D * b + D]
                    pe.matmul(a, ident[0:32, 0:D], v_up[:, b, :], start=True, stop=False, skip_group_check=True)
                    pe.matmul(a[:, 0:32], v_up[:, b, :], neg_i[:, :], start=False, stop=False, skip_group_check=True)
                    pe.matmul(a, lowT[:, b, :], flip[:, :], start=False, stop=False, skip_group_check=True)
                    mm = pe.matmul(a[:, 32:64], flip[:, :], neg_lowT[:, b, :], start=False, stop=True, skip_group_check=True)
                mm.then_inc(skew_psum, 1)

            def expm_round(n, half):
                to, j = 3 + (n + 1) % 2, TAYLOR - n
                if n == 0 and half == 0:
                    pe.wait_ge(skew_ready, 2)
                    pe.wait_ge(const_ready, 1)
                elif half == 0:
                    pe.wait_ge(x_ready, n)
                old = ident4 if n == 0 else X[:, (n - 1) % 2, :, :]
                both = ps[0:D, to, 2 * D * half:2 * D * half + 2 * D]
                if j > 1:
                    pe.matmul(both, scaled_i[:, j - 2, :], ident4[:, 0:2, :], start=True, stop=False, skip_group_check=True)
                elif j < 1:
                    pe.matmul(both, scaled_i[:, 0, :], old[:, 2 * half:2 * half + 2, :], start=True, stop=False, skip_group_check=True)
                for m in (2 * half, 2 * half + 1):
                    left = skew if j >= 1 else old
                    mm = pe.matmul(ps[0:D, to, D * m:D * m + D], left[:, m ^ 2, :], old[:, m, :], start=(j == 1), stop=True,
                                   skip_group_check=True)
                if half == 1:
                    mm.then_inc(xp_ready, 1)

            def modulation(r, c):
                if r == c == 0:
                    pe.wait_ge(mod_loaded, 48)
                for g, blk in enumerate(range(4) if r == 0 else range(4, 6)):
                    mm = pe.matmul(ps[32 * g:32 * g + 32, 5 + r, 0:H], silu[:, c, :], w_mod_sb[:, c, H * blk:H * blk + H],
                                   start=(c == 0), stop=(c == NC - 1), tile_position=(0, 32 * g))
                if c == NC - 1:
                    mm.then_inc(mod_psum, 1)

            def modulation_columns(r):
                pe.wait_ge(modrow_ready, r + 1)
                rows = 128 if r == 0 else 64
                for c in range(NC):
                    mm = pe.transpose(ps[0:KC, 7 - r, P128 * c:P128 * c + rows], mod_row[0:rows, r, KC * c:KC * c + KC],
                                      ident[0:rows, 0:rows])
                mm.then_inc(modT_psum, 1)

            def mlp_columns(r):
                pe.wait_ge(modcol_ready, 2)
                rows = 128 if r == 0 else 64
                for c in range(2):
                    pe.transpose(ps[:, 7 - r, P128 * c:P128 * c + rows], mod_row[0:rows, r, P128 * c:P128 * c + P128], ident[0:rows, 0:rows])
                for g in range(PARTS):
                    mm = pe.matmul(ps[REM * g:REM * g + REM, 7 - r, 2 * P128:2 * P128 + rows], mod_row[0:rows, r, 2 * P128:H],
                                   ident[0:rows, 0:rows], start=True, stop=True, tile_position=(0, REM * g))
                mm.then_inc(mlpT_psum, 1)

            def gate_rows(r, b):
                wait(pe, gate_ready, 2 * r + b)
                if r == 0:
                    mm = pe.matmul(ps[:, 5, 0:H], ident[:, 64 + b:65 + b].broadcast_to([P128, P128]), mod_row[:, 0, :], start=True, stop=True)
                else:
                    mm = pe.matmul(ps[:, 5, 0:H], ident[0:64, 32 + b:33 + b].broadcast_to([64, P128]), mod_row[0:64, 1, :], start=True, stop=True)
                mm.then_inc(gate_psum, 1)

            for it in range(D + LAG):
                if it < D - 1:
                    update_z(it)
                if LAG <= it < D - 1 + LAG:
                    update_mn(it - LAG)
                if 8 <= it < 8 + 8 * NC:
                    head_z0((it - 8) // NC, (it - 8) % NC)
                if 26 <= it < 26 + NC:
                    angles(it - 26)
                if it == 32:
                    lower_half()
                if it == 34:
                    skew_matrix()
                if 36 <= it < 36 + 2 * ROUNDS:
                    expm_round((it - 36) // 2, it % 2)
                if 40 <= it < 40 + 2 * NC:
                    modulation((it - 40) // NC, (it - 40) % NC)
                if it in (47, 48):
                    modulation_columns(it - 47)
                if it in (53, 54):
                    mlp_columns(it - 53)
                if it in (51, 55, 59, 63):
                    gate_rows((it - 51) // 8, (it - 51) // 4 % 2)
            E = X[:, (ROUNDS - 1) % 2, :, :]
            pe.wait_ge(x_ready, ROUNDS)
            pe.wait_ge(winv_ready, 1)
            for b in range(B):
                mm = pe.matmul(ps[0:D, 3, D * b:D * b + D], E[:, b, :], Winv[:, :], start=True, stop=True)
            mm.then_inc(k_psum, 1)
            pe.wait_ge(k_ready, 1)
            pe.matmul(ps[0:D, 4, 0:B * D], Winv[:, :], FW, start=True, stop=True).then_inc(k_psum, 1)
            pe.wait_ge(k_ready, 2)
            pe.wait_ge(gate_ready, 4)
            for b in range(B):
                pe.matmul(ps[0:D, 5 + b, 0:H], Kt[:, b, :], Pt_sb[:, :], start=True, stop=True).then_inc(k_psum, 1)
            pe.wait_ge(k_ready, 4)

            def rotate(n, j, b):
                pe.wait_ge(zslot_ready, n + 1)
                wait(pe, xrot_ready, n)
                pe.matmul(ps[:, 0, 0:H], z_slot[:, j, :], Y[:, b, :], start=True, stop=True).then_inc(rot_ready, 1)

            def turn(n):
                pe.wait_ge(xn_ready, n + 1)
                wait(pe, xT_ready, n)
                for c in range(NC):
                    mm = pe.transpose(ps[0:KC, 1, P128 * c:P128 * c + P128], xn[:, KC * c:KC * c + KC], ident[:, :])
                mm.then_inc(xT_psum, 1)

            def qkv(n, j, a):
                for c in range(NC):
                    mm = pe.matmul(ps[:, 2 + 3 * j + a, 0:H], xT[:, j, c, :], w_qkv_sb[:, c, H * a:H * a + H],
                                   start=(c == 0), stop=(c == NC - 1))
                mm.then_inc(qkv_psum, 1)

            pe.wait_ge(wcen_ready, NC)
            rotate(0, 0, 0)
            turn(0)
            rotate(1, 1, 0)

            def step_a(n, j, batch):
                pe.wait_ge(xT_ready, n + 1)
                wait(pe, qkv_used, n - 1)
                qkv(n, j, 0)
                qkv(n, j, 1)
                if batch[1] is not None:
                    turn(n + 1)
                if batch[2] is not None:
                    rotate(n + 2, j, batch[2])
                qkv(n, j, 2)

            tiles_of(pe, step_a)

            def bank(slot, a):
                return ps[:, 2 * slot + a, :]

            def slot_free(g, p, before, after):
                back = (p - 3) % RING_LEN
                while back not in RING_AT or back < p and (
                        RING_AT[back][0] == "O" and not before or RING_AT[back][0] == "T" and not after):
                    back = (back - 3) % RING_LEN
                kind, n = RING_AT[back]
                of = g if back < p else g - 1
                if kind == "S":
                    wait(pe, exp_done, 32 * of + n + 1)
                elif kind == "T":
                    wait(pe, op_ready, HP * of + HP + n + 1)
                else:
                    wait(pe, o_ready, of)

            def turn_qk(g_next, h, slot):
                pe.wait_ge(split_ready, 4 * g_next + 4)
                for a in range(2):
                    to = bank(slot, a).bitcast(F16)
                    for t in range(TILES):
                        mm = pe.transpose(to[:, P128 * t:P128 * t + P128],
                                          qk_split[:, t, a, 2 * h:2 * h + 2, :].rearrange("p e r -> p (e r)"), ident16[:, :])
                mm.then_inc(t_psum, 1)

            def scores(g, u, par, slot):
                kt, a, h = u // 4, u // 2 % 2, u % 2
                if u < 2:
                    pe.wait_ge(op_ready, HP * g + h + 1)
                for e in range(2):
                    rows = slice(ROWS * e, ROWS * e + ROWS)
                    mm = pe.matmul(bank(slot, e), qk_op[rows, par, 1, h, P128 * kt:P128 * kt + P128],
                                   qk_op[rows, par, 0, h, 512 * a:512 * a + 512], start=True, stop=True,
                                   tile_position=(ROWS * e, 0))
                mm.then_inc(s_ready, 1)

            def weigh_v(g, w, par):
                kt, a = w // 2, w % 2
                pe.wait_ge(exp_done, 32 * g + 2 * w + 2)
                if w < 2:
                    pe.wait_ge(vop_ready, g + 1)
                    wait(pe, oacc_ready, 2 * g + a - 1)
                for h in range(HG):
                    mm = pe.matmul(ps[32 * h:32 * h + 32, 6 + a, :], v_op[:, par, kt, h, :],
                                   prob[:, (2 * w + h // 2) % 8, 512 * (h % 2):512 * (h % 2) + 512], start=(kt == 0), stop=(kt == TILES - 1),
                                   tile_position=(0, 32 * h))
                mm.then_inc(pv_done, 1)

            def turn_o(g, slot):
                pe.wait_ge(oacc_ready, 2 * g + 2)
                for t in range(TILES):
                    mm = pe.transpose(bank(slot, t // 4)[:, P128 * (t % 4):P128 * (t % 4) + P128], o_acc[:, P128 * t:P128 * t + P128],
                                      ident[:, :])
                mm.then_inc(oT_psum, 1)

            def group_b(g, par, before, after):
                for v in range(16):
                    for kind, n, p in RING_PAIRS[v]:
                        if kind == "S":
                            slot_free(g, p, before, after)
                            scores(g, n, par, p % 3)
                        elif kind == "T" and after:
                            slot_free(g, p, before, after)
                            turn_qk(g + 1, n, p % 3)
                        elif kind == "O" and before:
                            slot_free(g, p, before, after)
                            turn_o(g - 1, p % 3)
                        if kind == "S" and n % 2 == 1:
                            if v >= PV_LAG:
                                weigh_v(g, v - PV_LAG, par)
                            elif before:
                                weigh_v(g - 1, 16 - PV_LAG + v, 1 - par)

            pe.wait_ge(vop_set, 3)
            pe.wait_ge(qkv_used, NT - 1)
            for h in range(HP):
                turn_qk(0, h, h)
            group_b(0, 0, False, True)
            with pe.Fori(0, GROUPS // 2 - 1) as i:
                group_b(2 * i + 1, 1, True, True)
                group_b(2 * i + 2, 0, True, True)
            group_b(GROUPS - 1, 1, True, False)
            for w in range(16 - PV_LAG, 16):
                weigh_v(GROUPS - 1, w, 1)
            pe.wait_ge(exp_done, 32 * GROUPS)
            turn_o(GROUPS - 1, 0)
            pe.wait_ge(o_ready, GROUPS)

            def row_head_pe(g, h, m):
                pe.wait_ge(row_in, 3 * m + 3)
                for a in range(2):
                    for t in range(TILES):
                        mm = pe.transpose(ps[0:HD, 2 * a + t // 4, P128 * (t % 4):P128 * (t % 4) + P128], row_qk[:, a, t, :], ident[:, :])
                mm.then_inc(row_turned, 1)

            def row_tile_pe(g, h, t, n):
                pe.wait_ge(row_q_ready, n + 1)
                for a in range(2):
                    mm = pe.matmul(ps[:, 4 + a, :], row_q, row_ops[:, 1, 512 * a:512 * a + 512], start=True, stop=True)
                mm.then_inc(row_s, 1)
                pe.wait_ge(row_exp, n + 1)
                for kt in range(TILES):
                    mm = pe.transpose(ps[:, 6 + kt // 4, P128 * (kt % 4):P128 * (kt % 4) + P128], row_p[:, P128 * kt:P128 * kt + P128], ident[:, :])
                mm.then_inc(row_pt_psum, 1)
                pe.wait_ge(row_pt_ready, n + 1)
                for kt in range(TILES):
                    mm = pe.matmul(ps[:, 0, 0:HD], row_pT[:, P128 * kt:P128 * kt + P128], row_v[:, kt, :], start=(kt == 0), stop=(kt == TILES - 1))
                mm.then_inc(row_o, 1)

            where_shifted(pe, lambda: head_rows(pe, row_head_pe, row_tile_pe))

            def c_turn_o(n, j):
                pe.wait_ge(orow_ready, n + 1)
                wait(pe, oT2_ready, n)
                for c in range(NC):
                    mm = pe.transpose(ps[0:KC, 0, P128 * c:P128 * c + P128], o_row[:, j, KC * c:KC * c + KC], ident[:, :])
                mm.then_inc(oT2_psum, 1)

            def c_project(n, j):
                pe.wait_ge(oT2_ready, n + 1)
                wait(pe, gated_ready, n)
                for c in range(NC):
                    mm = pe.matmul(ps[:, 1, 0:H], oT2[:, j, c, :], w_proj_sb[:, c, :], start=(c == 0), stop=(c == NC - 1))
                mm.then_inc(proj_ready, 1)

            def c_turn_x(n):
                pe.wait_ge(xn2_ready, n + 1)
                wait(pe, xT2_ready, n)
                for c in range(2):
                    pe.transpose(ps[:, 2, P128 * c:P128 * c + P128], xn[:, P128 * c:P128 * c + P128], ident[:, :])
                for g in range(PARTS):
                    mm = pe.matmul(ps[REM * g:REM * g + REM, 2, 2 * P128:3 * P128], xn[:, 2 * P128:H], ident[:, :],
                                   start=True, stop=True, tile_position=(0, REM * g))
                mm.then_inc(xT2_psum, 1)

            def c_up(c_no, n0, m):
                pe.wait_ge(xsplit_ready, n0 + 2)
                if m >= 3:
                    pe.wait_ge(h_ready, FF * c_no + m - 2)
                to, cols = ps[:, 3 + m % 3, 0:CH], slice(P128 * m, P128 * m + P128)
                for c in range(2):
                    for i, (w, xs) in enumerate(((w1_h, xn2_h), (w1_h, xn2_l), (w1_l, xn2_h))):
                        pe.matmul(to, w[:, c, cols], xs[:, c, :], start=(c == i == 0), stop=False)
                pe.matmul(to, w1_h[0:PARTS * REM, 2, cols], xn2_h[0:PARTS * REM, 2, :], start=False, stop=True).then_inc(h_psum, 1)

            def c_down(c_no, j, ms):
                if ms.start == 0:
                    wait(pe, gated2_ready[j], c_no)
                tokens = slice(P128 * j, P128 * j + P128)
                for m in ms:
                    if j == 0:
                        pe.wait_ge(hl_ready, FF * c_no + m + 1)
                    for i, (h, w) in enumerate(((hid_h, w2_h), (hid_h, w2_l), (hid_l, w2_h))):
                        mm = pe.matmul(ps[:, 6 + j, 0:H], h[:, m, tokens], w[:, m, :],
                                       start=(m == i == 0), stop=(m == FF - 1 and i == 2))
                if ms.stop == FF:
                    mm.then_inc(y_psum, 1)

            pe.wait_ge(proj_loaded, 32)
            c_turn_o(0, 0)
            c_project(0, 0)
            c_turn_o(1, 1)
            c_project(1, 1)
            c_turn_x(0)
            c_turn_x(1)
            pe.wait_ge(w_split, 6)

            def chunk_c(c_no, n0, b, b_next):
                for m in range(FF):
                    c_up(c_no, n0, m)
                    if b_next is not None:
                        if m == 0:
                            c_turn_o(n0 + 2, 0)
                        if m == 2:
                            c_project(n0 + 2, 0)
                        if m == 3:
                            c_turn_o(n0 + 3, 1)
                        if m == 6:
                            c_project(n0 + 3, 1)
                c_down(c_no, 0, range(FF))
                if b_next is not None:
                    c_turn_x(n0 + 2)
                c_down(c_no, 1, range(3))
                if b_next is not None:
                    c_turn_x(n0 + 3)
                c_down(c_no, 1, range(3, FF))

            pairs_of(pe, chunk_c)

        @block.vector
        def _(dve):
            Z, M, N = ps[:, 0, :], ps[:, 1, :], ps[:, 2, :]
            dve.wait_ge(silu_step, 3)
            dve.reciprocal(ex[:, :, :], ex[:, :, :]).then_inc(silu_step, 1)
            dve.wait_ge(silu_step, 4)
            dve.tensor_tensor(silu[:, :, 0:B], ex[:, :, :], cond_sb[:, :, :], ALU.mult).then_inc(silu_ready, 1)

            def read_diagonal():
                dve.tensor_tensor_reduce(out=junk[:, :], in0=Z[0:D, 0:D], in1=ident[0:D, 0:D], scale=1.0, scalar=0.0,
                                         op0=ALU.mult, op1=ALU.add, accum_out=diag[:, :]).then_inc(diag_ready, 1)

            def scale_r(j):
                dve.wait_ge(diagrs_ready, j + 1)
                wait(dve, w_ready, LAG * j)
                dve.tensor_scalar(R_half[:, :], Z[0:D, 0:D], diag_rs[:, 0:1], 0.5, ALU.mult, ALU.mult).then_inc(r_ready, 1)

            def z_step(k):
                dve.wait_ge(z_ready, k + 1)
                if k % LAG == LAG - 1:
                    read_diagonal()
                if k % LAG == 0 and k > 0:
                    scale_r(k // LAG - 1)
                if k == D - 1:
                    return
                if k % 8 == 0:
                    dve.wait_ge(mask_ready, k // 8 + 1)
                dve.reciprocal(z_rcp[:, :], Z[0:D, k:k + 1]).then_inc(zrcp_ready, 1)
                dve.tensor_copy(z_row[:, k + 1:k + 1 + D], Z[0:D, k + 1:k + 1 + D]).then_inc(zrow_ready, 1)
                dve.wait_ge(zrcp_ready, k + 1)
                dve.scalar_tensor_tensor(out=z_col[:, :], in0=Z[0:D, 0:D], scalar=z_rcp[:, 0:1], in1=elim_mask[:, k, :],
                                         op0=ALU.mult, op1=ALU.mult).then_inc(zcol_ready, 1)

            def m_step(k):
                dve.wait_ge(m_ready, k + 1)
                if k % LAG == 0:
                    dve.wait_ge(r_ready, k // LAG + 1)
                dve.tensor_scalar(signs[:, k:k + 1], M[0:D, k:k + 1], 0.0, -0.5, ALU.is_ge, ALU.add).then_inc(sign_step, 1)
                if k == D - 1:
                    return
                dve.wait_ge(sign_step, k + 1)
                dve.scalar_tensor_tensor(out=pivot_half[:, :], in0=M[0:D, k:k + 1], scalar=signs[:, k:k + 1],
                                         in1=R_half[:, k:k + 1], op0=ALU.mult, op1=ALU.add).then_inc(pivot_ready, 1)
                dve.scalar_tensor_tensor(out=w_row[:, k % 2, :], in0=M[0:D, 0:D], scalar=signs[:, k:k + 1], in1=R_half[:, :],
                                         op0=ALU.mult, op1=ALU.add).then_inc(w_ready, 1)
                dve.wait_ge(pivot_ready, k + 1)
                dve.reciprocal(pivot_rcp[:, :], pivot_half[:, :]).then_inc(prcp_ready, 1)
                dve.wait_ge(n_ready, k + 1)
                dve.wait_ge(prcp_ready, k + 1)
                dve.scalar_tensor_tensor(out=m_col[:, k % 2, :], in0=N[0:D, 0:D], scalar=pivot_rcp[:, 0:1],
                                         in1=elim_mask[:, k, :], op0=ALU.mult, op1=ALU.mult).then_inc(c_ready, 1)

            def weight_sum(c):
                if c == 0:
                    dve.wait_ge(wqkv_loaded, 32)
                w = w_qkv_sb[:, c, 0:2 * H] if c < NC else bias_row[:, 0:2 * H]
                dve.tensor_reduce(w_sum[:, c, :] if c < NC else b_sum, w.rearrange("p (h d) -> p h d", d=HD), AX.X,
                                  ALU.add).then_inc(wsum_ready, 1)

            def modulation_columns():
                dve.wait_ge(modT_psum, 2)
                for r, blocks in ((0, 4), (1, 2)):
                    src = ps[0:KC, 7 - r, 0:NC * P128].rearrange("p (c g q) -> p g c q", c=NC, g=4)[:, 0:blocks, :, 0:B]
                    for b in range(B):
                        ins = dve.tensor_tensor(mod_col[:, 4 * r:4 * r + blocks, :, b], src[:, :, :, b],
                                                bm_col[:, 4 * r:4 * r + blocks, :], ALU.add)
                    ins.then_inc(modcol_ready, 1)
                dve.wait_ge(modcol_ready, 2)
                scales = mod_col[:, SC_MSA:SC_MLP + 1:SC_MLP - SC_MSA, :, :].rearrange("p s c b -> p s (c b)")
                dve.tensor_scalar(scales, scales, 1.0, None, ALU.add).then_inc(modcol_ready, 1)

            def mlp_columns():
                dve.wait_ge(mlpT_psum, 2)
                for s, (bank, row) in enumerate(((7, 96), (6, 0))):
                    for rows, cs in ((P128, slice(0, 2)), (PARTS * REM, slice(2, 3))):
                        src = ps[0:rows, bank, 0:3 * P128].rearrange("p (c q) -> p c q", c=3)[:, cs, row:row + B]
                        ins = dve.tensor_tensor(mod_mlp[0:rows, s, cs, :], src,
                                                bm_mlp[0:rows, s, cs].unsqueeze(2).broadcast_to([rows, cs.stop - cs.start, B]), ALU.add)
                        ins.then_inc(modmlp_ready, 1)
                dve.wait_ge(modmlp_ready, 4)
                for rows, cs in ((P128, slice(0, 2)), (PARTS * REM, slice(2, 3))):
                    dve.tensor_scalar(mod_mlp[0:rows, 1, cs, :], mod_mlp[0:rows, 1, cs, :], 1.0, None, ALU.add).then_inc(modmlp_ready, 1)

            def gate_rows(r, b):
                dve.wait_ge(gate_psum, 2 * r + b + 1)
                if r == b == 0:
                    dve.wait_ge(row_loaded, 16 * 6)
                dve.tensor_tensor(gate[:, r, b, :], ps[:, 5, 0:H], bm_row[:, r, :], ALU.add).then_inc(gate_ready, 1)

            for it in range(D + LAG):
                if it < D:
                    z_step(it)
                if it == D:
                    scale_r(D // LAG - 1)
                if it >= LAG:
                    m_step(it - LAG)
                if it in (17, 19, 21, 23):
                    weight_sum((it - 17) // 2)
                if it == 50:
                    modulation_columns()
                if it == 56:
                    mlp_columns()
                if it in (52, 56, 60, 64):
                    gate_rows((it - 52) // 8, (it - 52) // 4 % 2)
            dve.wait_ge(sign_step, D)
            dve.tensor_tensor_reduce(out=junk[:, :], in0=signs[:, :], in1=ident[0:D, 0:D], scale=-2.0, scalar=0.0,
                                     op0=ALU.mult, op1=ALU.add, accum_out=sign_of[:, :]).then_inc(sign_ready, 1)
            dve.wait_ge(sign_ready, 1)
            dve.tensor_scalar(Winv[:, :], Z[0:D, D:2 * D], diag_rs[:, 0:1], sign_of[:, 0:1], ALU.mult, ALU.mult).then_inc(winv_ready, 1)

            def tile_of(n):
                return x_sb[:, bass.ds(n, 1), :].rearrange("p t f -> p (t f)")

            def split_qk(g):
                src = qkn[:, bass.ds(g, 1), :, :, :, :].rearrange("p g t a h d -> p (g t) a h d")
                part = [qk_split[:, :, :, :, HD * r:HD * r + HD] for r in range(PARTS)]
                wait(dve, t_psum, HP * g)
                for a in range(2):
                    dve.tensor_copy(part[0][:, :, a], src[:, :, a]).then_inc(split_h, 1)
                for a, low, high in ((0, 2, 1), (1, 1, 2)):
                    dve.wait_ge(split_h, 2 * g + 1 + a)
                    dve.tensor_tensor(part[low][:, :, a], src[:, :, a], part[0][:, :, a], ALU.subtract).then_inc(split_ready, 1)
                    dve.tensor_copy(part[high][:, :, a], part[0][:, :, a]).then_inc(split_ready, 1)

            def rotated(n, j):
                dve.wait_ge(rot_ready, n + 1)
                wait(dve, xkept, n - 1)
                dve.tensor_tensor(x_cur[:, j, :], ps[:, 0, 0:H], tile_of(n), ALU.add).then_inc(xrot_ready, 1)
                dve.wait_ge(xrot_ready, n + 1)
                dve.bn_stats(stats[:, :], x_cur[:, j, :]).then_inc(stats_ready, 1)

            def mean_and_variance():
                dve.bn_aggr(mean_var[:, 0, :], stats[:, :]).then_inc(mv_ready, 1)

            def normalise(n, j):
                dve.wait_ge(rstd_ready, n + 1)
                wait(dve, xT_psum, n)
                dve.tensor_scalar(xn[:, :], x_cur[:, j, :], mean_var[:, 0, 0:1], rstd[:, 0:1], ALU.subtract, ALU.mult).then_inc(xn_ready, 1)

            def bias_qk(n, j, a):
                dve.wait_ge(qkv_psum, 3 * n + a + 1)
                if a == 0:
                    wait(dve, qkn_ready, 2 * n - 2)
                dve.tensor_tensor(qk_c[:, j, a, :], ps[:, 2 + 3 * j + a, 0:H], bias_row[:, H * a:H * a + H], ALU.add).then_inc(qkc_ready, 1)

            def bias_v(n, t, j, b):
                dve.wait_ge(qkv_psum, 3 * n + 3)
                dve.tensor_tensor(v_all[:, 4 * b:4 * b + 4, bass.ds(t, 1), :, :].rearrange("p g t h d -> p g (t h d)"),
                                  ps[:, 4 + 3 * j, 0:H].rearrange("p (g f) -> p g f", g=4),
                                  bias_row[:, 2 * H:3 * H].rearrange("p (g f) -> p g f", g=4), ALU.add).then_inc(qkv_used, 1)

            def square_sums(n):
                dve.wait_ge(sq_ready, n + 1)
                dve.tensor_reduce(head_ssq, qk_sq.rearrange("p a (h d) -> p (a h) d", d=HD), AX.X, ALU.add).then_inc(ssq_ready, 1)

            def head_norms(n, t, j, b):
                dve.wait_ge(hsd_ready, n + 1)
                wait(dve, qkn_ready, 2 * n)
                dve.reciprocal(head_rstd, head_sd).then_inc(hrstd_ready, 1)
                dve.wait_ge(hrstd_ready, n + 1)
                dve.wait_ge(kg_ready, n + 1)
                for a, src in ((0, qk_c[:, j, 0, :]), (1, k_g)):
                    dve.tensor_tensor(qkn[:, 4 * b:4 * b + 4, bass.ds(t, 1), a, :, :].rearrange("p g t h d -> p g (t h) d"),
                                      src.rearrange("p (g h d) -> p g h d", g=4, h=HG),
                                      head_rstd[:, 16 * a:16 * a + 16].rearrange("p (g h) -> p g h", g=4).unsqueeze(3)
                                      .broadcast_to([P128, 4, HG, HD]), ALU.mult).then_inc(qkn_ready, 1)

            dve.wait_ge(rows_ready, 2)
            dve.tensor_tensor(xn[:, :], g_row[:, :], g_row[:, :], ALU.mult).then_inc(g_step, 1)
            dve.wait_ge(g_step, 1)
            dve.tensor_reduce(var_eps[:, 0:1], xn[:, :], AX.X, ALU.max).then_inc(g_step, 1)
            dve.wait_ge(g_step, 2)
            bound = HD * SCORE_BOUND ** 2
            dve.tensor_scalar(unshifted_ok[:, :], var_eps[0:1, 0:1], bound, None, ALU.is_le).then_inc(flag_ready, 1)
            dve.tensor_scalar(q_factor[:, :], var_eps[:, 0:1], bound, None, ALU.is_le).then_inc(flag_ready, 1)
            dve.wait_ge(flag_ready, 2)

            dve.wait_ge(x_loaded, 16 * B)
            rotated(0, 0)
            dve.wait_ge(stats_ready, 1)
            mean_and_variance()
            normalise(0, 0)
            dve.wait_ge(wcen_ready, NC + 1)

            def step_a(n, j, batch):
                before, after = batch[-1], batch[1]
                if after is not None:
                    rotated(n + 1, 1 - j)
                    dve.wait_ge(stats_ready, n + 2)
                if before is not None:
                    bias_v(n - 1, n - 1 - TILES * before, 1 - j, before)
                if after is not None:
                    mean_and_variance()
                if before is not None:
                    square_sums(n - 1)
                bias_qk(n, j, 0)
                if after is not None:
                    normalise(n + 1, 1 - j)
                if before is not None:
                    head_norms(n - 1, n - 1 - TILES * before, 1 - j, before)
                bias_qk(n, j, 1)
                if isinstance(n, int) and n == TILES + 1:
                    dve.wait_ge(qkn_ready, 2 * TILES)
                    split_qk(0)

            tiles_of(dve, step_a)
            bias_v(NT - 1, TILES - 1, 1, B - 1)
            square_sums(NT - 1)
            head_norms(NT - 1, TILES - 1, 1, B - 1)

            def read_operands(g, par, h, slot):
                dve.wait_ge(t_psum, HP * g + h + 1)
                dve.tensor_scalar(qk_op[:, par, 0, h, :], ps[:, 2 * slot, :].bitcast(F16), q_factor[:, :], None, ALU.mult)
                ins = dve.tensor_copy(qk_op[:, par, 1, h, :], ps[:, 2 * slot + 1, :].bitcast(F16))
                ins.then_inc(op_ready, 1)

            def read_output(g):
                for a in range(2):
                    dve.wait_ge(pv_done, 16 * g + 15 + a)
                    dve.tensor_copy(o_acc[:, 512 * a:512 * a + 512], ps[:, 6 + a, :]).then_inc(oacc_ready, 1)

            def divide_output(g, slot):
                dve.wait_ge(oT_psum, g + 1)
                src = ps[:, 2 * slot:2 * slot + 2, :].rearrange("p a (t h d) -> p (a t) h d", h=HG, d=32)
                dve.reciprocal(den_inv[:, :, :].unsqueeze(3), src[:, :, :, HD:HD + 1]).then_inc(den_ready, 1)
                dve.wait_ge(den_ready, g + 1)
                dve.tensor_tensor(o_tok[:, bass.ds(g, 1), :, :].rearrange("p g t (h d) -> p (g t) h d", d=HD), src[:, :, :, 0:HD],
                                  den_inv[:, :, :].unsqueeze(3).broadcast_to([P128, TILES, HG, HD]), ALU.mult).then_inc(o_ready, 1)

            units = [(kind, n, p % 3) for pair in RING_PAIRS for kind, n, p in pair if kind != "S"]

            def group_b(g, par, before, after):
                if before:
                    read_output(g - 1)
                for kind, n, slot in units:
                    if kind == "T" and after:
                        if n == 0:
                            split_qk(g + 1)
                        read_operands(g + 1, 1 - par, n, slot)
                    if kind == "O" and before:
                        divide_output(g - 1, slot)

            def split_weights():
                low = slice(REM, 2 * REM)
                dve.wait_ge(w1_loaded, 16 * (1 + PARTS))
                dve.tensor_scalar(w1_h[0:PARTS * REM, 2, :], w1_sb[0:PARTS * REM, 2, :], W_SCALE, None, ALU.mult).then_inc(w_half, 1)
                dve.tensor_scalar(w1_h[:, 0:2, :], w1_sb[:, 0:2, :], W_SCALE, None, ALU.mult).then_inc(w_half, 1)
                dve.wait_ge(w_half, 2)
                dve.scalar_tensor_tensor(out=w1_h[low, 2, :], in0=w1_sb[low, 2, :], scalar=W_SCALE, in1=w1_h[low, 2, :],
                                         op0=ALU.mult, op1=ALU.subtract).then_inc(w_split, 1)
                for c in range(2):
                    dve.scalar_tensor_tensor(out=w1_l[:, c, :], in0=w1_sb[:, c, :], scalar=W_SCALE, in1=w1_h[:, c, :],
                                             op0=ALU.mult, op1=ALU.subtract).then_inc(w_split, 1)
                dve.wait_ge(w2_loaded, 16)
                dve.tensor_scalar(w2_h, w2_sb, W_SCALE, None, ALU.mult).then_inc(w_half, 1)
                dve.wait_ge(w_half, 3)
                for ms in (slice(0, 3), slice(3, 6), slice(6, 9)):
                    dve.scalar_tensor_tensor(out=w2_l[:, ms, :], in0=w2_sb[:, ms, :], scalar=W_SCALE, in1=w2_h[:, ms, :],
                                             op0=ALU.mult, op1=ALU.subtract).then_inc(w_split, 1)

            dve.wait_ge(qkn_ready, 2 * NT)
            for h in range(HP):
                read_operands(0, 0, h, h)
            group_b(0, 0, False, True)
            with dve.Fori(0, GROUPS // 2 - 1) as i:
                group_b(2 * i + 1, 1, True, True)
                group_b(2 * i + 2, 0, True, True)
            group_b(GROUPS - 1, 1, True, False)
            dve.wait_ge(vop_ready, GROUPS)
            where(dve, False, split_weights)
            read_output(GROUPS - 1)
            divide_output(GROUPS - 1, 0)

            def row_head_dve(g, h, m):
                for a in range(2):
                    dve.tensor_copy(row_qk[:, a, :, :].unsqueeze(2),
                                    qkn[:, bass.ds(g, 1), :, a, bass.ds(h, 1), :].rearrange("p g t h d -> p (g t) h d")).then_inc(row_in, 1)
                dve.tensor_copy(row_v.unsqueeze(2), v_all[:, bass.ds(g, 1), :, bass.ds(h, 1), :].rearrange("p g t h d -> p (g t) h d")).then_inc(row_in, 1)
                dve.wait_ge(row_turned, m + 1)
                dve.tensor_copy(row_ops, ps[0:HD, 0:4, :].rearrange("p (a s) t -> p a (s t)", a=2)).then_inc(row_ops_ready, 1)

            def row_tile_dve(g, h, t, n):
                dve.wait_ge(row_ops_ready, HG * g + h + 1)
                dve.tensor_copy(row_q, row_ops[:, 0, :].rearrange("p (t q) -> p t q", q=P128)[:, bass.ds(t, 1), :].rearrange("p t q -> p (t q)")).then_inc(row_q_ready, 1)
                dve.wait_ge(row_s, n + 1)
                dve.tensor_reduce(row_max, ps[:, 4:6, :].rearrange("p a q -> p (a q)"), AX.X, ALU.max).then_inc(row_max_ready, 1)
                dve.wait_ge(row_max_ready, n + 1)
                dve.tensor_scalar(row_shift, row_max, -HD ** -0.5, None, ALU.mult).then_inc(row_shift_ready, 1)
                dve.wait_ge(row_pt_psum, n + 1)
                dve.tensor_copy(row_pT, ps[:, 6:8, :].rearrange("p a q -> p (a q)")).then_inc(row_pt_ready, 1)
                dve.wait_ge(row_exp, n + 1)
                dve.reciprocal(row_rcp, row_den).then_inc(row_rcp_ready, 1)
                dve.wait_ge(row_rcp_ready, n + 1)
                dve.wait_ge(row_o, n + 1)
                dve.tensor_scalar(o_tok[:, bass.ds(g, 1), bass.ds(t, 1), :].rearrange("p g t (h d) -> p (g t h) d", d=HD)[:, bass.ds(h, 1), :]
                                  .rearrange("p h d -> p (h d)"), ps[:, 0, 0:HD], row_rcp, None, ALU.mult).then_inc(row_done, 1)

            def row_attention():
                head_rows(dve, row_head_dve, row_tile_dve)
                split_weights()

            where_shifted(dve, row_attention)

            def c_gate(n, b, stats_of):
                dve.wait_ge(proj_ready, n + 1)
                wait(dve, x2_ready, n)
                if stats_of is not None:
                    dve.wait_ge(stats2_ready, stats_of + 1)
                dve.tensor_tensor(gated, ps[:, 1, 0:H], gate[:, 0, b, :], ALU.mult).then_inc(gated_ready, 1)

            def c_add(n, j, uses):
                dve.wait_ge(gated_ready, n + 1)
                dve.wait_ge(xgb_ready, n + 1)
                wait(dve, xgb2_ready[j], uses)
                dve.tensor_tensor(x_cur[:, j, :], gated, x_gb[:, j, :], ALU.add).then_inc(x2_ready, 1)
                dve.wait_ge(x2_ready, n + 1)
                dve.bn_stats(stats[:, :], x_cur[:, j, :]).then_inc(stats2_ready, 1)

            def c_mean_and_variance(j):
                dve.bn_aggr(mean_var[:, j, :], stats[:, :]).then_inc(mv2_ready, 1)

            def c_normalise(n, j, stats_of):
                dve.wait_ge(rstd2_ready, n + 1)
                wait(dve, xT2_psum, n)
                if stats_of is not None:
                    dve.wait_ge(stats2_ready, stats_of + 1)
                dve.tensor_scalar(xn[:, :], x_cur[:, j, :], mean_var[:, j, 0:1], rstd[:, j:j + 1], ALU.subtract, ALU.mult).then_inc(xn2_ready, 1)

            def split_x(n, j):
                dve.wait_ge(xT2_ready, n + 1)
                cols, low = slice(P128 * j, P128 * j + P128), slice(2 * REM, 3 * REM)
                dve.tensor_copy(xn2_h[0:PARTS * REM, 2, cols], xn2T[0:PARTS * REM, 2, cols]).then_inc(xh_ready, 1)
                dve.tensor_copy(xn2_h[:, 0:2, cols], xn2T[:, 0:2, cols]).then_inc(xh_ready, 1)
                dve.wait_ge(xh_ready, 2 * n + 2)
                dve.tensor_tensor(xn2_h[low, 2, cols], xn2T[low, 2, cols], xn2_h[low, 2, cols], ALU.subtract)
                dve.tensor_tensor(xn2_l[:, :, cols], xn2T[:, 0:2, cols], xn2_h[:, 0:2, cols], ALU.subtract).then_inc(xsplit_ready, 1)

            def split_hid(c_no, m):
                dve.wait_ge(h_ready, FF * c_no + m + 1)
                dve.tensor_copy(hid_h[:, m, :], hid[:, m, :]).then_inc(hh_ready, 1)
                dve.wait_ge(hh_ready, FF * c_no + m + 1)
                dve.tensor_tensor(hid_l[:, m, :], hid[:, m, :], hid_h[:, m, :], ALU.subtract).then_inc(hl_ready, 1)

            def c_first(n0, b, uses):
                c_gate(n0, b, None)
                c_add(n0, 0, uses)

            def c_second(n0, b, uses):
                c_gate(n0 + 1, b, n0)
                c_mean_and_variance(0)
                c_add(n0 + 1, 1, uses)
                c_normalise(n0, 0, n0 + 1)
                c_mean_and_variance(1)

            def c_result(n, j, b, c_no):
                dve.wait_ge(y_psum, n + 1)
                dve.scalar_tensor_tensor(out=gated2[:, j, :], in0=ps[:, 6 + j, 0:H], scalar=1.0 / W_SCALE, in1=gate[:, 1, b, :],
                                         op0=ALU.mult, op1=ALU.mult).then_inc(gated2_ready[j], 1)
                dve.wait_ge(gated2_ready[j], c_no + 1)
                dve.wait_ge(xgb2_ready[j], c_no + 1)
                wait(dve, y_stored[j], 16 * c_no)
                dve.tensor_tensor(y_out[:, j, :], gated2[:, j, :], x_gb2[:, j, :], ALU.add).then_inc(y_ready[j], 1)

            c_first(0, 0, 0)
            c_second(0, 0, 0)
            c_normalise(1, 1, None)
            for j in range(2):
                split_x(j, j)

            def chunk_c(c_no, n0, b, b_next):
                for m in range(FF):
                    split_hid(c_no, m)
                    if b_next is not None and m == 2:
                        c_first(n0 + 2, b_next, c_no + 1)
                if b_next is not None:
                    c_second(n0 + 2, b_next, c_no + 1)
                c_result(n0, 0, b, c_no)
                if b_next is not None:
                    c_normalise(n0 + 3, 1, None)
                    for j in range(2):
                        split_x(n0 + 2 + j, j)
                c_result(n0 + 1, 1, b, c_no)

            pairs_of(dve, chunk_c)


def fold_index():
    place = np.full((D, D), -1)
    rows, cols = np.triu_indices(D, 1)
    place[rows, cols] = np.arange(len(rows))
    index = np.full((D // 2, D), len(rows))
    for r in range(D // 2):
        index[r, r + 1:] = place[r, r + 1:]
        index[r, :r] = place[D - 1 - r, D - 1 - np.arange(r)]
    return index


def rows_of_128(vectors):
    full = vectors[:, :2 * P128].reshape(-1, 2, P128)
    rest = np.tile(vectors[:, 2 * P128:], (1, 4))[:, None, :]
    return np.concatenate([full, rest], axis=1).transpose(2, 0, 1)


def kernel(**inputs):
    import concourse.bacc as bacc
    from concourse.bass_utils import run_bass_kernel_spmd

    a = {k: np.asarray(v) for k, v in inputs.items()}
    index = fold_index()
    W = np.concatenate([a["L0_cond_W"], np.zeros((1, H), a["L0_cond_W"].dtype)])
    b = np.concatenate([a["L0_cond_b"], np.zeros(1, a["L0_cond_b"].dtype)])
    arrays = {
        "x": a["x"],
        "x_t": a["x"].transpose(0, 2, 1),
        "cond_t": a["cond_1152"].T,
        "P": a["L0_cond_P"],
        "P_t": a["L0_cond_P"].T,
        "W_fold": W[index.ravel()].T,
        "b_fold": b[index],
        "w_mod": a["L1_cond_w_mod"],
        "b_mod_cols": a["L1_cond_b_mod"].reshape(6, NC, KC).transpose(2, 0, 1),
        "b_mod": a["L1_cond_b_mod"],
        "w_qkv": a["L1_cond_w_qkv"],
        "b_qkv": a["L1_cond_b_qkv"],
        "g_q": a["L1_cond_g_q"],
        "g_k": a["L1_cond_g_k"],
        "w_proj": a["L1_cond_w_proj"],
        "b_proj": a["L1_cond_b_proj"],
        "w1": a["L1_cond_w1"],
        "b1_cols": a["L1_cond_b1"].reshape(FF, P128).T,
        "w2": a["L1_cond_w2"],
        "b2": a["L1_cond_b2"],
        "b_mlp_cols": rows_of_128(a["L1_cond_b_mod"].reshape(6, H)[[SH_MLP, SC_MLP]]),
    }
    arrays = {f"in_{k}": np.ascontiguousarray(v) for k, v in arrays.items()}
    nc = bacc.Bacc("TRN2", target_bir_lowering=False, num_devices=1)
    args = [nc.dram_tensor(k, v.shape, mybir.dt.from_np(v.dtype), kind="ExternalInput").ap() for k, v in arrays.items()]
    out = nc.dram_tensor("out", (B, T, H), F32, kind="ExternalOutput").ap()
    build(nc, *args, out)
    r = run_bass_kernel_spmd(nc, [arrays], core_ids=[0])
    return r.results[0]["out"]
```

```python
from contextlib import ExitStack

import numpy as np

import concourse.bass as bass
from concourse import mybir

F32 = mybir.dt.float32
F16 = mybir.dt.float16
ALU = mybir.AluOpType
ACT = mybir.ActivationFunctionType
AX = mybir.AxisListType

B, T, H = 2, 1024, 288
D = 64
NH, HD = 16, 18
MLP = 4 * H
P128 = 128
TILES = T // P128
NT = B * TILES
KC = 96
NC = H // KC
HG = 4
GROUPS = B * NH // HG
GW = HG * HD
PARTS = 3
ROWS = 64
HP = HG // 2
PV_LAG = 2
EPS = 1e-6
SCORE_BOUND = 60.0
LAG = 8
SQUARINGS = 8
TAYLOR = 6
ROUNDS = SQUARINGS + TAYLOR
FF = MLP // P128
CH = 256
REM = H - 2 * P128
BIAS = slice(PARTS * REM, PARTS * REM + 2)
REM_ROWS = BIAS.stop
W_SCALE = 64.0
CHUNKS = B * T // CH
SH_MSA, SC_MSA, G_MSA, SH_MLP, SC_MLP, G_MLP = range(6)

C_BANKS = (0, 1, 2)
C_SECOND = (0, 2, 2)
C_FIRST_BANKS = (C_BANKS, (6, 7, 3))

T_AFTER = {7: 0, 9: 1}
O_AFTER = 3


def ring_units():
    at, pairs = 0, []
    for v in range(16):
        units = [("S", 2 * v, at), ("S", 2 * v + 1, at + 1)]
        at += 2
        if v == O_AFTER:
            units.append(("O", 0, at))
            at += 1
        if v in T_AFTER:
            units.append(("T", T_AFTER[v], at))
            at += 1
        pairs.append(units)
    return pairs, -(-at // 3) * 3


RING_PAIRS, RING_LEN = ring_units()
RING_AT = {p: (kind, n) for pair in RING_PAIRS for kind, n, p in pair}


def build(nc, x, x_t, cond_t, P, P_t, W_fold, b_fold, w_mod, b_mod_cols, b_mod, w_qkv, b_qkv, g_q, g_k,
          w_proj, b_proj, w1, b1_cols, w2, b2, out):
    with ExitStack() as ctx:
        def sb(name, shape, dt=F32):
            return ctx.enter_context(nc.sbuf_tensor(name, shape, dt))

        def sem(name):
            return ctx.enter_context(nc.semaphore(name))

        ps = ctx.enter_context(nc.psum_tensor("ps", [P128, 8, 512], F32))

        ident = sb("ident", [P128, P128])
        ident16 = sb("ident16", [P128, P128], F16)
        neg_half = sb("neg_half", [P128, 1])
        x_sb = sb("x_sb", [P128, NT, H])
        o_tok = sb("o_tok", [P128, GROUPS, TILES, GW])
        w_proj_sb = sb("w_proj_sb", [P128, 3, H])
        mod_cols = sb("mod_cols", [P128, 4, 3, B])
        gate = sb("gate", [P128, 2, B, H])
        gate_bias = sb("gate_bias", [P128, 2, B, H])
        b1_sb = sb("b1_sb", [P128, FF])
        stats = sb("stats", [P128, 2, 6])
        mean_var = sb("mean_var", [P128, 2, 2])
        var_eps = sb("var_eps", [P128, 2])
        rstd = sb("rstd", [P128, 2])
        xn = sb("xn", [P128, H])
        x_cur = sb("x_cur", [P128, 2, H])
        eps_layer = sb("eps_layer", [P128, 1])
        eps_head = sb("eps_head", [P128, 1])
        wqkv_low = sb("wqkv_low", [P128, 2, 3 * H], F16)
        g_row = sb("g_row", [P128, H])
        qkn = sb("qkn", [P128, GROUPS, TILES, 2, HG, HD])
        v_all = sb("v_all", [P128, GROUPS, TILES, HG, HD])

        arena1 = sb("arena1", [P128, 8192])
        w_qkv_sb = arena1[:, 0:3 * 3 * H].rearrange("p (c n) -> p c n", c=3)
        z0_all = arena1[0:D, 2592:2592 + NT * P128].rearrange("p (t k) -> p t k", t=NT)
        xT = arena1[:, 4640:4640 + 2 * 3 * P128].rearrange("p (j c k) -> p j c k", j=2, c=3)
        xT_h = arena1[:, 5408:5792].bitcast(F16).rearrange("p (j c k) -> p j c k", j=2, c=3)
        xT_l = arena1[:, 5792:6048].bitcast(F16).rearrange("p (j c k) -> p j c k", j=2, c=2)
        qk_sq = arena1[:, 6048:6048 + 2 * H].rearrange("p (a f) -> p a f", a=2)
        head_ssq, head_sd, head_rstd = (arena1[:, 6624 + 32 * i:6656 + 32 * i] for i in range(3))
        z_slot = arena1[0:D, 6720:6720 + 2 * P128].rearrange("p (j k) -> p j k", j=2)
        Y = arena1[0:D, 6976:6976 + B * H].rearrange("p (b f) -> p b f", b=B)
        prob = arena1[:, :].rearrange("p (s q) -> p s q", s=8)

        arena2 = sb("arena2", [P128, 11328])
        Wf = arena2[0:KC, 0:NC * 2048].rearrange("p (c n) -> p c n", c=NC)
        w_mod_sb = arena2[0:KC, 6144:6144 + NC * 6 * H].rearrange("p (c n) -> p c n", c=NC)
        wqkv_high = arena2[:, 0:1296].bitcast(F16).rearrange("p (c n) -> p c n", c=3)
        bias_low = arena2[:, 1296:1728].bitcast(F16)
        qk_op = arena2[:, 0:4096].bitcast(F16).rearrange("p (s a h t) -> p s a h t", s=2, a=2, h=HP)
        qk_split = arena2[:, 4096:6144].bitcast(F16).rearrange("p (t a h r) -> p t a h r", t=TILES, a=2, h=HG)
        c_at = 0

        def c_mem(*shape):
            nonlocal c_at
            n = int(np.prod(shape))
            c_at += n
            names = "abc"[:len(shape)]
            return arena1[:, c_at - n:c_at].rearrange(
                f"p ({' '.join(names)}) -> p {' '.join(names)}", **dict(zip(names, shape)))

        hid = c_mem(FF, CH)
        xn2T = c_mem(3, CH)
        oT2 = c_mem(2, 3, P128)
        oT2_h = c_mem(3 * P128).bitcast(F16).rearrange("p (j c t) -> p j c t", j=2, c=3)
        oT2_l = c_mem(2 * P128).bitcast(F16).rearrange("p (j c t) -> p j c t", j=2, c=2)
        x_gb2, gated2, y_out = (c_mem(2, H) for _ in range(3))
        o_row, x_gb = (arena2[:, 4096 + 2 * H * i:4096 + 2 * H * (i + 1)].rearrange("p (j f) -> p j f", j=2) for i in range(2))
        gated = c_mem(H)
        hid_h = arena2[:, 0:1152].bitcast(F16).rearrange("p (m t) -> p m t", m=FF)
        hid_l = arena2[:, 1152:2304].bitcast(F16).rearrange("p (m t) -> p m t", m=FF)
        xn2_h = arena2[:, 2304:2688].bitcast(F16).rearrange("p (c t) -> p c t", c=3)
        xn2_l = arena2[:, 2688:2944].bitcast(F16).rearrange("p (c t) -> p c t", c=2)
        qk_mem = qkn[:, :, :, :, :, :].rearrange("p g t a h d -> p (g t a h d)")
        half_qk = GROUPS // 2 * TILES * 2 * GW
        w1_sb = qk_mem[:, 0:3 * MLP].rearrange("p (c n) -> p c n", c=3)
        w2_sb = qk_mem[:, half_qk:half_qk + FF * H].rearrange("p (m n) -> p m n", m=FF)
        w1_h = arena2[:, 6144:7872].bitcast(F16).rearrange("p (c n) -> p c n", c=3)
        w1_l = arena2[:, 7872:9024].bitcast(F16).rearrange("p (c n) -> p c n", c=2)
        w2_h = arena2[:, 9024:10320].bitcast(F16).rearrange("p (m n) -> p m n", m=FF)
        wp_h = arena2[:, 10320:10752].bitcast(F16).rearrange("p (c n) -> p c n", c=3)
        wp_l = arena2[:, 10752:11040].bitcast(F16).rearrange("p (c n) -> p c n", c=2)
        w2_l = v_all[:, :, :, :, :].rearrange("p g t h d -> p (g t h d)")[:, 0:1296].bitcast(F16).rearrange("p (m n) -> p m n", m=FF)

        v_op = sb("v_op", [P128, 2, TILES, HG, 32])
        o_acc = sb("o_acc", [P128, T])
        den_inv = sb("den_inv", [P128, TILES, HG])

        q_factor = sb("q_factor", [P128, 1])
        unshifted_ok = sb("unshifted_ok", [1, 1], mybir.dt.int32)
        row_p = arena1[:, 0:T]
        row_pT = arena1[:, 1024:1024 + T]
        row_ops = arena1[0:HD, 2048:2048 + 2 * T].rearrange("p (a t) -> p a t", a=2)
        row_q = arena1[0:HD, 4096:4096 + P128]
        row_qk = arena1[:, 4224:4224 + 2 * TILES * HD].rearrange("p (a t d) -> p a t d", a=2, t=TILES)
        row_v = arena1[:, 4512:4512 + TILES * HD].rearrange("p (t d) -> p t d", t=TILES)
        row_max, row_shift, row_den, row_rcp = (arena1[:, 4656 + i:4657 + i] for i in range(4))

        arena3 = o_tok[0:D, :, :, :].rearrange("p g t f -> p (g t f)")
        elim_mask = arena3[:, 0:D * D].rearrange("p (k i) -> p k i", k=D)
        flip = sb("flip", [D, D])
        neg_i = sb("neg_i", [32, 32])
        scaled_i = v_op[0:D, 0, 0:5, :, :].rearrange("p j a b -> p (j a b)")[:, 0:5 * D].rearrange("p (j i) -> p j i", j=5)
        ident4 = v_op[0:D, 1, 0:2, :, :].rearrange("p j a b -> p (j a b)").rearrange("p (j i) -> p j i", j=4)
        fold_up = sb("fold_up", [32, D])
        fold_low = sb("fold_low", [32, D])
        P_sb = sb("P_sb", [KC, NC, D])
        P_top = sb("P_top", [D, D])
        Pt_sb = sb("Pt_sb", [D, H])
        cond_sb = sb("cond_sb", [KC, NC, B])
        ex = sb("ex", [KC, NC, B])
        silu = sb("silu", [KC, NC, 32])
        bf = sb("bf", [32, D])
        z_row = sb("z_row", [D, P128])
        z_col = sb("z_col", [D, D])
        z_rcp = sb("z_rcp", [D, 1])
        diag = sb("diag", [D, 1])
        diag_rs = sb("diag_rs", [D, 1])
        junk = sb("junk", [D, D])
        R_half = sb("R_half", [D, D])
        pivot_half = sb("pivot_half", [D, 1])
        pivot_rcp = sb("pivot_rcp", [D, 1])
        signs = sb("signs", [D, D])
        w_row = sb("w_row", [D, 2, D])
        m_col = sb("m_col", [D, 2, D])
        sign_of = sb("sign_of", [D, 1])
        Winv = sb("Winv", [D, D])
        head_mem = o_acc[:, :]
        v_sb = head_mem[:, 0:512]
        fold = head_mem[0:32, 512:640].rearrange("p (b j) -> p b j", b=B)
        fold_b = head_mem[0:32, 640:768].rearrange("p (b j) -> p b j", b=B)
        v_up = head_mem[0:32, 768:896].rearrange("p (b j) -> p b j", b=B)
        v_low = head_mem[0:32, 896:1024].rearrange("p (b j) -> p b j", b=B)
        lowT = arena3[:, 4096:4224].rearrange("p (b j) -> p b j", b=B)
        neg_lowT = arena3[:, 4224:4288].rearrange("p (b j) -> p b j", b=B)
        skew = qk_mem[0:D, 0:256].rearrange("p (m j) -> p m j", m=4)
        X = qk_mem[0:D, 256:768].rearrange("p (s m j) -> p s m j", s=2, m=4)
        FW = qk_mem[0:D, 768:896].rearrange("p (b j) -> p b j", b=B)
        Kt = qk_mem[0:D, 896:1024].rearrange("p (b j) -> p b j", b=B)
        bm_cols = qk_mem[:, 4288:4300].rearrange("p (s c) -> p s c", s=4)
        mod_row = qk_mem[:, 1024:1024 + 2 * H].rearrange("p (r f) -> p r f", r=2)
        bm_row = qk_mem[:, 1632:1632 + 2 * H].rearrange("p (r f) -> p r f", r=2)
        bo_row = qk_mem[:, 2208:2208 + 2 * H].rearrange("p (r f) -> p r f", r=2)
        gq_row = qk_mem[:, 2784:2784 + H]
        gk_row = qk_mem[:, 3072:3072 + H]
        w_sum = qk_mem[:, 3360:3360 + 3 * 32].rearrange("p (c h) -> p c h", c=3)
        xT_head = [qk_mem[0:KC, 4352:4352 + NC * T].rearrange("p (c t) -> p c t", c=NC),
                   v_all[0:KC, :, :, :, :].rearrange("p g t h d -> p (g t h d)")[:, 0:NC * T].rearrange("p (c t) -> p c t", c=NC)]
        v_dram = nc.dram_tensor("v_scratch", [B, 4, 512], F32).ap()

        xt_loaded = [sem(f"xt_loaded{b}") for b in range(B)]
        p_loaded, cond_loaded, x_loaded, wf_loaded = sem("p_loaded"), sem("cond_loaded"), sem("x_loaded"), sem("wf_loaded")
        wqkv_loaded, mod_loaded, row_loaded, proj_loaded = sem("wqkv_loaded"), sem("mod_loaded"), sem("row_loaded"), sem("proj_loaded")
        w1_loaded, w2_loaded = sem("w1_loaded"), sem("w2_loaded")
        v_stored, fold_loaded = sem("v_stored"), sem("fold_loaded")
        const_step, ident_ready, mask_ready, const_ready = sem("const_step"), sem("ident_ready"), sem("mask_ready"), sem("const_ready")
        z_ready, m_ready, n_ready = sem("z_ready"), sem("m_ready"), sem("n_ready")
        zrcp_ready, zrow_ready, zcol_ready = sem("zrcp_ready"), sem("zrow_ready"), sem("zcol_ready")
        diag_ready, diagrs_ready, r_ready = sem("diag_ready"), sem("diagrs_ready"), sem("r_ready")
        sign_step, pivot_ready, prcp_ready = sem("sign_step"), sem("pivot_ready"), sem("prcp_ready")
        w_ready, c_ready, sign_ready, winv_ready = sem("w_ready"), sem("c_ready"), sem("sign_ready"), sem("winv_ready")
        silu_step, silu_ready = sem("silu_step"), sem("silu_ready")
        v_ready, vsb_ready, foldb_ready, vparts_ready = sem("v_ready"), sem("vsb_ready"), sem("foldb_ready"), sem("vparts_ready")
        lowT_psum, lowT_ready, skew_psum, skew_ready = sem("lowT_psum"), sem("lowT_ready"), sem("skew_psum"), sem("skew_ready")
        xp_ready, x_ready, k_psum, k_ready = sem("xp_ready"), sem("x_ready"), sem("k_psum"), sem("k_ready")
        z0_psum, z0_ready = sem("z0_psum"), sem("z0_ready")
        mod_psum, modrow_ready, modT_psum, modcol_ready = sem("mod_psum"), sem("modrow_ready"), sem("modT_psum"), sem("modcol_ready")
        wpart_step, wqkv_split = sem("wpart_step"), sem("wqkv_split")
        w_half, w_split, hh_ready, hl_ready, xh_ready, xsplit_ready = (
            sem("w_half"), sem("w_split"), sem("hh_ready"), sem("hl_ready"),
            sem("xh_ready"), sem("xsplit_ready"))
        gate_psum, gate_ready, wsum_ready, wscale, wcen_ready, rows_ready = (
            sem("gate_psum"), sem("gate_ready"), sem("wsum_ready"), sem("wscale"), sem("wcen_ready"), sem("rows_ready"))
        zslot_ready, xkept, qkv_psum, v_kept = sem("zslot_ready"), sem("xkept"), sem("qkv_psum"), sem("v_kept")
        low_step, ones_set, cast_ready, low_ready = sem("low_step"), sem("ones_set"), sem("cast_ready"), sem("low_ready")
        rot_ready, xrot_ready, stats_ready, mv_ready = sem("rot_ready"), sem("xrot_ready"), sem("stats_ready"), sem("mv_ready")
        vareps_ready, rstd_ready, xn_ready, xT_psum, xT_ready = sem("vareps_ready"), sem("rstd_ready"), sem("xn_ready"), sem("xT_psum"), sem("xT_ready")
        sq_ready, ssq_ready, kg_ready, hsd_ready, hrstd_ready, qkn_ready = (
            sem("sq_ready"), sem("ssq_ready"), sem("kg_ready"), sem("hsd_ready"), sem("hrstd_ready"), sem("qkn_ready"))
        split_h, split_ready = sem("split_h"), sem("split_ready")
        t_psum, op_ready, s_ready, exp_done, pv_done = sem("t_psum"), sem("op_ready"), sem("s_ready"), sem("exp_done"), sem("pv_done")
        vop_set, vop_ready, oacc_ready, oT_psum, den_ready, o_ready = (
            sem("vop_set"), sem("vop_ready"), sem("oacc_ready"), sem("oT_psum"), sem("den_ready"), sem("o_ready"))
        g_step, flag_ready, row_in, row_turned, row_ops_ready, row_q_ready = (
            sem("g_step"), sem("flag_ready"), sem("row_in"), sem("row_turned"), sem("row_ops_ready"), sem("row_q_ready"))
        row_s, row_max_ready, row_shift_ready, row_exp, row_pt_psum, row_pt_ready, row_o, row_rcp_ready, row_done = (
            sem("row_s"), sem("row_max_ready"), sem("row_shift_ready"), sem("row_exp"), sem("row_pt_psum"), sem("row_pt_ready"),
            sem("row_o"), sem("row_rcp_ready"), sem("row_done"))
        wproj_half, wproj_split = sem("wproj_half"), sem("wproj_split")
        ocast_ready, olow_step, olow_ready = sem("ocast_ready"), sem("olow_step"), sem("olow_ready")
        orow_ready, xgb_ready, oT2_psum, oT2_ready = sem("orow_ready"), sem("xgb_ready"), sem("oT2_psum"), sem("oT2_ready")
        proj_ready, gated_ready, x2_ready, stats2_ready, mv2_ready = (
            sem("proj_ready"), sem("gated_ready"), sem("x2_ready"), sem("stats2_ready"), sem("mv2_ready"))
        vareps2_ready, rstd2_ready, xn2_ready, xT2_psum, xT2_ready = (
            sem("vareps2_ready"), sem("rstd2_ready"), sem("xn2_ready"), sem("xT2_psum"), sem("xT2_ready"))
        h_psum, h_ready, y_psum = (
            sem("h_psum"), sem("h_ready"), sem("y_psum"))
        xgb2_ready = [sem(f"xgb2_ready{j}") for j in range(2)]
        gated2_ready = [sem(f"gated2_ready{j}") for j in range(2)]
        y_ready = [sem(f"y_ready{j}") for j in range(2)]
        y_stored = [sem(f"y_stored{j}") for j in range(2)]

        block = ctx.enter_context(nc.Block())

        def wait(eng, s, value):
            if not isinstance(value, int) or value > 0:
                eng.wait_ge(s, value)

        def pairs_of(eng, body):
            half = TILES // 2
            for b in range(B):
                if b == 0:
                    body(0, 0, 0, 0)
                with eng.Fori(1 if b == 0 else 0, half - 1) as i:
                    body(half * b + i, TILES * b + 2 * i, b, b)
                body(half * (b + 1) - 1, TILES * (b + 1) - 2, b, b + 1 if b + 1 < B else None)

        def tiles_of(eng, step):
            def batches(t):
                return {d: (t + d) // TILES if t + d < NT else None for d in range(4)}

            for b in range(B):
                step(TILES * b, 0, batches(TILES * b))
                with eng.Fori(0, TILES // 2 - 2) as i:
                    for j in (1, 0):
                        step(TILES * b + 2 * i + (2 - j), j, batches(TILES * b + 1))
                for t in range(TILES - 3, TILES):
                    step(TILES * b + t, t % 2, batches(TILES * b + t))

        def where(eng, shifted, body):
            eng.wait_ge(flag_ready, 2)
            ok = eng.value_load(unshifted_ok[0:1, 0:1], min_val=0, max_val=1)
            with eng.If(ok < 1 if shifted else ok > 0):
                body()

        def where_shifted(eng, body):
            where(eng, True, body)

        def head_rows(eng, of_head, of_tile):
            with eng.Fori(0, GROUPS) as g:
                with eng.Fori(0, HG) as h:
                    of_head(g, h, HG * g + h)
                    with eng.Fori(0, TILES) as t:
                        of_tile(g, h, t, (HG * g + h) * TILES + t)

        ROW_TILES = B * NH * TILES

        @block.sync
        def _(sp):
            sp.dma_start(P_sb[:, :, :], P.rearrange("(c p) d -> p c d", p=KC)).then_inc(p_loaded, 16)
            sp.dma_start(P_top[:, :], P[0:D, :]).then_inc(p_loaded, 16)
            sp.dma_start(cond_sb[:, :, :], cond_t.rearrange("(c p) b -> p c b", p=KC)).then_inc(cond_loaded, 16)
            for b in range(B):
                sp.dma_start(xT_head[b], x_t[b].rearrange("(c p) t -> p c t", p=KC)).then_inc(xt_loaded[b], 16)
            sp.dma_start(Wf, W_fold.rearrange("(c p) n -> p c n", p=KC)).then_inc(wf_loaded, 16)
            sp.dma_start(bf[:, :], b_fold).then_inc(wf_loaded, 16)
            sp.dma_start(Pt_sb[:, :], P_t).then_inc(wf_loaded, 16)
            sp.dma_start(w_qkv_sb[:, 0:2, :], w_qkv[0:2 * P128, :].rearrange("(c p) n -> p c n", p=P128)).then_inc(wqkv_loaded, 16)
            for g in range(PARTS):
                sp.dma_start(w_qkv_sb[REM * g:REM * g + REM, 2, :], w_qkv[2 * P128:H, :]).then_inc(wqkv_loaded, 16)
            sp.dma_start(w_qkv_sb[BIAS, 2, :], b_qkv.partition_broadcast(2)).then_inc(wqkv_loaded, 16)
            for b in range(B):
                sp.dma_start(x_sb[:, TILES * b:TILES * b + TILES, :],
                             x[b].rearrange("(t p) f -> p t f", p=P128)).then_inc(x_loaded, 16)
            sp.dma_start(w_mod_sb, w_mod.rearrange("(c p) n -> p c n", p=KC)).then_inc(mod_loaded, 16)
            sp.dma_start(bm_cols, b_mod_cols).then_inc(mod_loaded, 16)
            for row, g in ((gq_row, g_q), (gk_row, g_k)):
                sp.dma_start(row.rearrange("p (h d) -> p h d", d=HD),
                             g.partition_broadcast(NH).partition_broadcast(P128)).then_inc(row_loaded, 16)
            for r, blk in enumerate((G_MSA, G_MLP)):
                sp.dma_start(bm_row[:, r, :], b_mod[H * blk:H * blk + H].partition_broadcast(P128)).then_inc(row_loaded, 16)
            for r, bias in enumerate((b_proj, b2)):
                sp.dma_start(bo_row[:, r, :], bias.partition_broadcast(P128)).then_inc(row_loaded, 16)
            sp.dma_start(w_proj_sb[:, 0:2, :], w_proj[0:2 * P128, :].rearrange("(c p) n -> p c n", p=P128)).then_inc(proj_loaded, 16)
            for g in range(PARTS):
                sp.dma_start(w_proj_sb[REM * g:REM * g + REM, 2, :], w_proj[2 * P128:H, :]).then_inc(proj_loaded, 16)
            sp.dma_start(b1_sb[:, :], b1_cols).then_inc(proj_loaded, 16)
            sp.wait_ge(vsb_ready, 1)
            for b in range(B):
                sp.dma_start(v_dram[b], v_sb[b:b + 97:32, :]).then_inc(v_stored, 16)
            sp.wait_ge(v_stored, 16 * B)
            sp.dma_start(fold, v_dram.rearrange("b g (r j) -> (g r) b j", j=D)).then_inc(fold_loaded, 16)
            where_shifted(sp, lambda: sp.wait_ge(row_done, ROW_TILES))
            sp.wait_ge(split_ready, 4 * (GROUPS // 2))
            sp.dma_start(w1_sb[:, 0:2, :], w1[0:2 * P128, :].rearrange("(c p) n -> p c n", p=P128)).then_inc(w1_loaded, 16)
            for g in range(PARTS):
                sp.dma_start(w1_sb[REM * g:REM * g + REM, 2, :], w1[2 * P128:H, :]).then_inc(w1_loaded, 16)
            sp.wait_ge(split_ready, 4 * GROUPS)
            sp.dma_start(w2_sb, w2.rearrange("(m p) n -> p m n", p=P128)).then_inc(w2_loaded, 16)
            out_t = out.rearrange("b (c j p) f -> (b c) p j f", p=P128, j=2)
            with sp.Fori(0, CHUNKS) as c:
                for j in range(2):
                    sp.wait_ge(y_ready[j], c + 1)
                    sp.dma_start(out_t[bass.ds(c, 1), :, j, :].rearrange("c p f -> p (c f)"), y_out[:, j, :]).then_inc(y_stored[j], 16)
            for j in range(2):
                sp.wait_ge(y_stored[j], 16 * CHUNKS)

        @block.gpsimd
        def _(pool):
            n_const = 0

            def step(ins):
                nonlocal n_const
                n_const += 1
                ins.then_inc(const_step, 1)
                pool.wait_ge(const_step, n_const)

            def select(ap, op, fill, base, pattern, mult):
                return pool.affine_select(out=ap, in_=ap, compare_op=op, fill=fill, base=base, pattern=pattern,
                                          channel_multiplier=mult)

            step(pool.memset(ident[:, :], 0.0))
            select(ident[:, :], ALU.not_equal, 1.0, 0, [[-1, P128]], 1).then_inc(ident_ready, 1)
            pool.memset(neg_half[:, :], -0.5).then_inc(const_step, 1)
            n_const += 1
            pool.memset(eps_layer[:, :], EPS).then_inc(const_step, 1)
            pool.memset(eps_head[:, :], HD * EPS * W_SCALE ** 2).then_inc(const_step, 1)
            n_const += 2
            n_rs = 0

            def diagonal_rsqrt():
                nonlocal n_rs
                n_rs += 1
                pool.wait_ge(diag_ready, n_rs)
                pool.tensor_tensor(diag_rs[:, :], diag[:, :], neg_half[0:D, 0:1], ALU.pow).then_inc(diagrs_ready, 1)

            for c in range(8):
                if c == 5:
                    diagonal_rsqrt()
                part = elim_mask[:, 8 * c:8 * c + 8, :]
                step(pool.memset(part, -1.0))
                step(select(part, ALU.is_equal, 0.0, -8 * c, [[-1, 8], [0, D]], 1))
                select(part, ALU.is_gt, 0.0, -8 * c, [[-1, 8], [1, D]], 0).then_inc(mask_ready, 1)
                if c == 0:
                    pool.memset(silu[:, :, :], 0.0).then_inc(silu_step, 1)
                    pool.wait_ge(silu_step, 2)
                    pool.tensor_scalar(ex[:, :, :], ex[:, :, :], 1.0, None, ALU.add).then_inc(silu_step, 1)
            step(pool.memset(flip[:, :], 0.0))
            step(select(flip[:, :], ALU.not_equal, 1.0, -(D - 1), [[1, D]], 1))
            step(pool.memset(neg_i[:, :], 0.0))
            step(select(neg_i[:, :], ALU.not_equal, -1.0, 0, [[-1, 32]], 1))
            for m, sign in ((fold_up, 1), (fold_low, -1)):
                step(pool.memset(m[:, :], 1.0))
                step(select(m[:, :], ALU.is_gt, 0.0, 0, [[sign, D]], -sign))
            for j in range(5):
                step(pool.memset(scaled_i[:, j, :], 0.0))
                step(select(scaled_i[:, j, :], ALU.not_equal, float(j + 2), 0, [[-1, D]], 1))
            for j in range(4):
                step(pool.memset(ident4[:, j, :], 0.0))
                step(select(ident4[:, j, :], ALU.not_equal, 1.0, 0, [[-1, D]], 1))
            step(pool.memset(ident16[:, :], 0.0))
            step(select(ident16[:, :], ALU.not_equal, 1.0, 0, [[-1, P128]], 1))
            pool.memset(lowT, 0.0).then_inc(const_ready, 1)

            diagonal_rsqrt()
            for c in range(3):
                rows = P128 if c < 2 else REM_ROWS
                w = w_qkv_sb[0:rows, c, 0:2 * H].rearrange("p (h d) -> p h d", d=HD)
                pool.wait_ge(wsum_ready, c + 1)
                pool.tensor_scalar(w_sum[0:rows, c, :], w_sum[0:rows, c, :], -1.0 / HD, None, ALU.mult).then_inc(wscale, 1)
                pool.wait_ge(wscale, c + 1)
                pool.tensor_tensor(w, w, w_sum[0:rows, c, :].unsqueeze(2).broadcast_to([rows, 32, HD]), ALU.add).then_inc(wcen_ready, 1)
            for _ in range(2):
                diagonal_rsqrt()
            pool.wait_ge(fold_loaded, 16)
            pool.wait_ge(wf_loaded, 48)
            pool.tensor_tensor(fold_b, fold, bf[:, :].unsqueeze(1).broadcast_to([32, B, D]), ALU.add).then_inc(foldb_ready, 1)
            pool.wait_ge(foldb_ready, 1)
            for part, mask in ((v_up, fold_up), (v_low, fold_low)):
                pool.tensor_tensor(part, fold_b, mask[:, :].unsqueeze(1).broadcast_to([32, B, D]), ALU.mult).then_inc(vparts_ready, 1)
            pool.wait_ge(row_loaded, 16 * 6)
            pool.tensor_tensor(g_row[:, :], gq_row, gk_row, ALU.mult).then_inc(rows_ready, 1)
            pool.wait_ge(rows_ready, 1)
            pool.tensor_scalar(g_row[:, :], g_row[:, :], float(HD), None, ALU.mult).then_inc(rows_ready, 1)
            n_part = 0

            def part_step(ins):
                nonlocal n_part
                n_part += 1
                ins.then_inc(wpart_step, 1)
                pool.wait_ge(wpart_step, n_part)

            def split_wqkv(c):
                rows = P128 if c < 2 else REM_ROWS
                w, high = w_qkv_sb[0:rows, c, :], wqkv_high[0:rows, c, :]
                part_step(pool.tensor_scalar(high, w, W_SCALE, None, ALU.mult))
                part_step(pool.tensor_scalar(w, w, W_SCALE, None, ALU.mult))
                if c < 2:
                    pool.tensor_tensor(wqkv_low[:, c, :], w, high, ALU.subtract).then_inc(wqkv_split, 1)
                else:
                    part_step(pool.tensor_tensor(bias_low[BIAS, :], w[BIAS, :], high[BIAS, :], ALU.subtract))
                    pool.tensor_tensor(high[REM:2 * REM, :], w[REM:2 * REM, :], high[REM:2 * REM, :], ALU.subtract).then_inc(wqkv_split, 1)
                pool.wait_ge(wqkv_split, c + 1)

            def join_bias():
                high = wqkv_high[BIAS, 2, :]
                part_step(pool.tensor_scalar(high, high, ident[BIAS, BIAS.start:BIAS.start + 1], None, ALU.mult))
                part_step(pool.tensor_scalar(bias_low[BIAS, :], bias_low[BIAS, :], ident[BIAS, BIAS.start + 1:BIAS.stop], None, ALU.mult))
                pool.tensor_tensor(high, high, bias_low[BIAS, :], ALU.add).then_inc(wqkv_split, 1)
                pool.wait_ge(wqkv_split, 4)

            pool.wait_ge(v_ready, 1)
            split_wqkv(0)
            diagonal_rsqrt()
            split_wqkv(1)
            diagonal_rsqrt()
            split_wqkv(2)
            diagonal_rsqrt()
            join_bias()
            pool.memset(xT_h[BIAS, :, 2, :], 1.0).then_inc(ones_set, 1)
            pool.wait_ge(ones_set, 1)
            diagonal_rsqrt()
            pool.wait_ge(gate_ready, 4)
            for r in range(2):
                for b in range(B):
                    pool.tensor_tensor(gate_bias[:, r, b, :], gate[:, r, b, :], bo_row[:, r, :], ALU.mult).then_inc(rows_ready, 1)

            def layer_rstd(n, j):
                pool.wait_ge(mv_ready, n + 1)
                pool.tensor_tensor(var_eps[:, j:j + 1], mean_var[:, j, 1:2], eps_layer[:, :], ALU.add).then_inc(vareps_ready, 1)
                pool.wait_ge(vareps_ready, n + 1)
                pool.tensor_tensor(rstd[:, j:j + 1], var_eps[:, j:j + 1], neg_half[:, 0:1], ALU.pow).then_inc(rstd_ready, 1)
                pool.tensor_copy(x_sb[:, bass.ds(n, 1), :].rearrange("p t f -> p (t f)"), x_cur[:, j, :]).then_inc(xkept, 1)

            def low_part(n, j):
                low = slice(2 * REM, 3 * REM)
                pool.wait_ge(cast_ready, n + 1)
                pool.tensor_tensor(xT_l[:, j, :, :], xT[:, j, 0:2, :], xT_h[:, j, 0:2, :], ALU.subtract).then_inc(low_step, 1)
                pool.wait_ge(low_step, n + 1)
                pool.tensor_tensor(xT_h[low, j, 2, :], xT[low, j, 2, :], xT_h[low, j, 2, :], ALU.subtract).then_inc(low_ready, 1)
                pool.wait_ge(low_ready, n + 1)

            pool.wait_ge(flag_ready, 2)
            def step_a(n, j, batch):
                if batch[3] is not None:
                    layer_rstd(n + 3, 1 - j)
                if batch[2] is not None:
                    low_part(n + 2, j)
                t = n - TILES * batch[0]
                k = qkn[:, 4 * batch[0]:4 * batch[0] + 4, bass.ds(t, 1), 1, :, :].rearrange("p g t h d -> p g (t h d)")
                pool.wait_ge(qkn_ready, 2 * n + 2)
                pool.tensor_tensor(k, k, g_row[:, :].rearrange("p (g f) -> p g f", g=4), ALU.mult).then_inc(kg_ready, 1)
                if isinstance(n, int) and n in (NT - 2, NT - 1):
                    pool.wait_ge(v_kept, TILES)
                    copy_v(n - (NT - 2), n % 2)

            def copy_v(g, par):
                wait(pool, pv_done, 16 * g - 16)
                pool.tensor_copy(v_op[:, par, :, :, 0:HD].rearrange("p t h d -> p (t h) d"),
                                 v_all[:, bass.ds(g, 1), :, :, :].rearrange("p g t h d -> p (g t h d)")).then_inc(vop_ready, 1)

            pool.memset(v_op[:, :, :, :, HD:HD + 1], 1.0).then_inc(vop_set, 1)
            pool.memset(v_op[:, :, :, :, HD + 1:32], 0.0).then_inc(vop_set, 1)
            pool.memset(qk_split[:, :, :, :, PARTS * HD:ROWS], 0.0).then_inc(vop_set, 1)
            for n in range(3):
                layer_rstd(n, n % 2)
                if n > 0:
                    low_part(n - 1, n - 1)
            tiles_of(pool, step_a)

            pool.wait_ge(v_kept, NT)
            with pool.Fori(0, GROUPS // 2 - 1) as i:
                copy_v(2 * i + 2, 0)
                copy_v(2 * i + 3, 1)

            def c_inputs(n, j, b):
                t = n - TILES * b
                wait(pool, oT2_psum, n - 1)
                pool.tensor_copy(o_row[:, j, :].rearrange("p (g f) -> p g f", g=4),
                                 o_tok[:, 4 * b:4 * b + 4, bass.ds(t, 1), :].rearrange("p g t f -> p g (t f)")).then_inc(orow_ready, 1)
                wait(pool, x2_ready, n - 1)
                pool.tensor_tensor(x_gb[:, j, :], x_sb[:, bass.ds(n, 1), :].rearrange("p t f -> p (t f)"),
                                   gate_bias[:, 0, b, :], ALU.add).then_inc(xgb_ready, 1)

            def c_low(n, j):
                low = slice(2 * REM, 3 * REM)
                pool.wait_ge(ocast_ready, n + 1)
                pool.tensor_tensor(oT2_l[:, j, :, :], oT2[:, j, 0:2, :], oT2_h[:, j, 0:2, :], ALU.subtract).then_inc(olow_step, 1)
                pool.wait_ge(olow_step, n + 1)
                pool.tensor_tensor(oT2_h[low, j, 2, :], oT2[low, j, 2, :], oT2_h[low, j, 2, :], ALU.subtract).then_inc(olow_ready, 1)
                pool.wait_ge(olow_ready, n + 1)

            def c_rstd(n, j):
                pool.wait_ge(mv2_ready, n + 1)
                pool.tensor_tensor(var_eps[:, j:j + 1], mean_var[:, j, 1:2], eps_layer[:, :], ALU.add).then_inc(vareps2_ready, 1)
                pool.wait_ge(vareps2_ready, n + 1)
                pool.tensor_tensor(rstd[:, j:j + 1], var_eps[:, j:j + 1], neg_half[:, 0:1], ALU.pow).then_inc(rstd2_ready, 1)

            def c_out_residual(c_no, n, j, b):
                wait(pool, y_ready[j], c_no)
                pool.tensor_tensor(x_gb2[:, j, :], x_cur[:, j, :],
                                   gate_bias[:, 1, b, :], ALU.add).then_inc(xgb2_ready[j], 1)


            where(pool, False, lambda: pool.wait_ge(o_ready, GROUPS // 2))
            where_shifted(pool, lambda: pool.wait_ge(row_done, ROW_TILES))
            pool.wait_ge(t_psum, HP * GROUPS)
            for j in range(2):
                c_inputs(j, j, 0)
            for j in range(2):
                c_low(j, j)
            pool.wait_ge(o_ready, GROUPS)
            for j in range(2):
                c_rstd(j, j)

            def chunk_c(c_no, n0, b, b_next):
                if b_next is not None:
                    for j in range(2):
                        c_inputs(n0 + 2 + j, j, b_next)
                for j in range(2):
                    c_out_residual(c_no, n0 + j, j, b)
                    if b_next is not None:
                        c_low(n0 + 2 + j, j)
                if b_next is not None:
                    for j in range(2):
                        c_rstd(n0 + 2 + j, j)

            pairs_of(pool, chunk_c)

        @block.scalar
        def _(act):
            act.wait_ge(cond_loaded, 16)
            act.activation(ex[:, :, :], cond_sb[:, :, :], ACT.Exp, scale=-1.0).then_inc(silu_step, 1)

            def keep_z0(q):
                act.wait_ge(z0_psum, q + 1)
                act.activation(z0_all[:, 2 * q:2 * q + 2, :].rearrange("p t k -> p (t k)"), ps[0:D, 5 + q % 2, 0:256], ACT.Copy).then_inc(z0_ready, 1)

            for q in range(6):
                keep_z0(q)
            act.wait_ge(v_ready, 1)
            act.activation(v_sb, ps[:, 3, :], ACT.Copy).then_inc(vsb_ready, 1)
            for q in range(6, 8):
                keep_z0(q)
            act.wait_ge(lowT_psum, 1)
            act.wait_ge(const_ready, 1)
            low = ps[0:D, 4, 0:B * 32].rearrange("p (b r) -> p b r", b=B)
            act.activation(lowT[:, :, 32:D], low, ACT.Copy).then_inc(lowT_ready, 1)
            act.activation(neg_lowT, low, ACT.Copy, scale=-1.0).then_inc(lowT_ready, 1)
            act.wait_ge(skew_psum, 1)
            sk = ps[0:D, 3, 0:B * D].rearrange("p (b j) -> p b j", b=B)
            act.activation(skew[:, 0:2, :], sk, ACT.Copy, scale=2.0 ** -SQUARINGS).then_inc(skew_ready, 1)
            act.activation(skew[:, 2:4, :], sk, ACT.Copy, scale=-2.0 ** -SQUARINGS).then_inc(skew_ready, 1)

            def expm_round(n):
                j = TAYLOR - n
                act.wait_ge(xp_ready, n + 1)
                act.activation(X[:, n % 2, :, :], ps[0:D, 3 + (n + 1) % 2, 0:4 * D].rearrange("p (m j) -> p m j", m=4),
                               ACT.Copy, scale=1.0 / j if j > 1 else 1.0).then_inc(x_ready, 1)

            act.wait_ge(mod_psum, 1)
            act.activation(mod_row[:, 0, :], ps[:, 5, 0:H], ACT.Copy).then_inc(modrow_ready, 1)
            expm_round(0)
            act.wait_ge(mod_psum, 2)
            act.activation(mod_row[0:64, 1, :], ps[0:64, 6, 0:H], ACT.Copy).then_inc(modrow_ready, 1)
            for n in range(1, ROUNDS):
                expm_round(n)
            act.wait_ge(k_psum, 1)
            act.activation(FW, ps[0:D, 3, 0:B * D].rearrange("p (b j) -> p b j", b=B), ACT.Copy).then_inc(k_ready, 1)
            act.wait_ge(k_psum, 2)
            act.activation(Kt, ps[0:D, 4, 0:B * D].rearrange("p (b j) -> p b j", b=B), ACT.Copy).then_inc(k_ready, 1)
            for b in range(B):
                act.wait_ge(k_psum, 3 + b)
                act.activation(Y[:, b, :], ps[0:D, 5 + b, 0:H], ACT.Copy).then_inc(k_ready, 1)

            def fill_z(n, j):
                wait(act, rot_ready, n - 1)
                act.activation(z_slot[:, j, :], z0_all[:, bass.ds(n, 1), :].rearrange("p t k -> p (t k)"),
                               ACT.Copy).then_inc(zslot_ready, 1)

            def modulate(n, j, b):
                act.wait_ge(xT_psum, n + 1)
                wait(act, low_ready, n - 1)
                for c in range(3):
                    rows = P128 if c < 2 else PARTS * REM
                    ins = act.activation(xT[0:rows, j, c, :], ps[0:rows, 1, P128 * c:P128 * c + P128], ACT.Identity,
                                         scale=mod_cols[0:rows, 1, c, b:b + 1], bias=mod_cols[0:rows, 0, c, b:b + 1])
                ins.then_inc(xT_ready, 1)

            def cast(n, j):
                act.wait_ge(xT_ready, n + 1)
                wait(act, qkv_psum, 3 * n - 3)
                act.activation(xT_h[:, j, 0:2, :], xT[:, j, 0:2, :], ACT.Copy)
                act.activation(xT_h[0:PARTS * REM, j, 2, :], xT[0:PARTS * REM, j, 2, :], ACT.Copy).then_inc(cast_ready, 1)

            act.wait_ge(z0_ready, NT // 2)
            for n in range(2):
                fill_z(n, n)
            act.wait_ge(modcol_ready, 10)
            for n in range(2):
                modulate(n, n, 0)
                if n == 0:
                    fill_z(2, 0)
                cast(n, n)

            def step_a(n, j, batch):
                if batch[3] is not None:
                    fill_z(n + 3, 1 - j)
                act.wait_ge(qkv_psum, 3 * n + 2)
                wait(act, ssq_ready, n)
                act.activation(qk_sq, ps[:, 2 + 3 * j:4 + 3 * j, 0:H], ACT.Square).then_inc(sq_ready, 1)
                if batch[2] is not None:
                    modulate(n + 2, j, batch[2])
                act.wait_ge(ssq_ready, n + 1)
                wait(act, hrstd_ready, n)
                act.activation(head_sd, head_ssq, ACT.Sqrt, bias=eps_head[:, :]).then_inc(hsd_ready, 1)
                act.wait_ge(qkv_psum, 3 * n + 3)
                t = n - TILES * batch[0]
                act.activation(v_all[:, 4 * batch[0]:4 * batch[0] + 4, bass.ds(t, 1), :, :].rearrange("p g t h d -> p g (t h d)"),
                               ps[:, 4 + 3 * j, 0:H].rearrange("p (g f) -> p g f", g=4), ACT.Copy, scale=1.0 / W_SCALE).then_inc(v_kept, 1)
                if batch[2] is not None:
                    cast(n + 2, j)

            tiles_of(act, step_a)

            def exp_unit(g, u):
                act.wait_ge(s_ready, 32 * g + u + 1)
                wait(act, pv_done, 16 * g + u // 2 - 3)
                act.activation(prob[:, u % 8, :], ps[:, 2 * slot_of(u):2 * slot_of(u) + 2, :].rearrange("p a q -> p (a q)"),
                               ACT.Exp, scale=HD ** -0.5).then_inc(exp_done, 1)

            def slot_of(u):
                return next(p for pair in RING_PAIRS for kind, n, p in pair if (kind, n) == ("S", u)) % 3

            def group_b(g):
                for u in range(32):
                    exp_unit(g, u)

            group_b(0)
            with act.Fori(0, GROUPS // 2 - 1) as i:
                group_b(2 * i + 1)
                group_b(2 * i + 2)
            group_b(GROUPS - 1)

            def row_tile_act(g, h, t, n):
                act.wait_ge(row_shift_ready, n + 1)
                act.activation(row_p, ps[:, 4:6, :].rearrange("p a q -> p (a q)"), ACT.Exp, scale=HD ** -0.5,
                               bias=row_shift, accum_out=row_den).then_inc(row_exp, 1)

            where_shifted(act, lambda: head_rows(act, lambda g, h, m: None, row_tile_act))

            def c_turn_o(n, j, banks=C_BANKS):
                act.wait_ge(oT2_psum, n + 1)
                wait(act, proj_ready, n - 1)
                wait(act, olow_ready, n - 1)
                for rows, cs in ((P128, slice(0, 2)), (PARTS * REM, slice(2, 3))):
                    ins = act.activation(oT2[0:rows, j, cs, :], ps[0:rows, banks[0], P128 * cs.start:P128 * cs.stop]
                                         .rearrange("p (c k) -> p c k", k=P128), ACT.Copy)
                ins.then_inc(oT2_ready, 1)
                act.wait_ge(oT2_ready, n + 1)
                for rows, cs in ((P128, slice(0, 2)), (PARTS * REM, slice(2, 3))):
                    ins = act.activation(oT2_h[0:rows, j, cs, :], oT2[0:rows, j, cs, :], ACT.Copy)
                ins.then_inc(ocast_ready, 1)

            def c_turn_x(n, j, b, banks=C_BANKS):
                act.wait_ge(xT2_psum, n + 1)
                for c in range(3):
                    rows = P128 if c < 2 else PARTS * REM
                    ins = act.activation(xn2T[0:rows, c, P128 * j:P128 * j + P128], ps[0:rows, banks[2], P128 * c:P128 * c + P128],
                                         ACT.Identity, scale=mod_cols[0:rows, 3, c, b:b + 1], bias=mod_cols[0:rows, 2, c, b:b + 1])
                ins.then_inc(xT2_ready, 1)

            for j in range(2):
                c_turn_o(j, j, C_FIRST_BANKS[j])
            for j in range(2):
                c_turn_x(j, j, 0, C_FIRST_BANKS[j])

            def chunk_c(c_no, n0, b, b_next):
                for m in range(FF):
                    act.wait_ge(h_psum, FF * c_no + m + 1)
                    act.activation(hid[:, m, :], ps[:, 3 + m % 3, 0:CH], ACT.Gelu_apprx_tanh,
                                   scale=1.0 / W_SCALE, bias=b1_sb[:, m:m + 1]).then_inc(h_ready, 1)
                    if b_next is not None and m in (1, 3):
                        c_turn_o(n0 + 2 + m // 3, m // 3)
                if b_next is not None:
                    for j in range(2):
                        c_turn_x(n0 + 2 + j, j, b_next)

            pairs_of(act, chunk_c)

        @block.tensor
        def _(pe):
            Z, M, N = ps[:, 0, :], ps[:, 1, :], ps[:, 2, :]
            pe.wait_ge(p_loaded, 32)
            for c in range(NC):
                pe.matmul(Z[0:D, 0:D], P_sb[:, c, :], P_sb[:, c, :], start=(c == 0), stop=(c == NC - 1))
            pe.wait_ge(ident_ready, 1)
            pe.matmul(Z[0:D, D:2 * D], ident[0:D, 0:D], ident[0:D, 0:D], start=False, stop=False,
                      skip_group_check=True).then_inc(z_ready, 1)
            pe.matmul(M[0:D, 0:D], ident[0:D, 0:D], P_top[:, :], start=True, stop=False, skip_group_check=True).then_inc(m_ready, 1)
            pe.matmul(N[0:D, 0:D], P_top[:, :], ident[0:D, 0:D], start=True, stop=False, skip_group_check=True).then_inc(n_ready, 1)

            def update_z(k):
                pe.wait_ge(zrow_ready, k + 1)
                pe.wait_ge(zcol_ready, k + 1)
                pe.matmul(Z[0:D, k + 1:k + 1 + D], z_col[:, :], z_row[:, k + 1:k + 1 + D], start=False, stop=False,
                          skip_group_check=True).then_inc(z_ready, 1)

            def update_mn(k):
                pe.wait_ge(w_ready, k + 1)
                pe.wait_ge(c_ready, k + 1)
                pe.matmul(M[0:D, k + 1:D], m_col[:, k % 2, :], w_row[:, k % 2, k + 1:D], start=False, stop=False,
                          skip_group_check=True).then_inc(m_ready, 1)
                pe.matmul(N[0:D, k + 1:D], w_row[:, k % 2, :], m_col[:, k % 2, k + 1:D], start=False, stop=False,
                          skip_group_check=True).then_inc(n_ready, 1)

            def head_z0(q, c):
                if c == 0 and q % 4 == 0:
                    pe.wait_ge(xt_loaded[q // 4], 16)
                if c == 0:
                    wait(pe, z0_ready, q - 1)
                mm = pe.matmul(ps[0:D, 5 + q % 2, 0:256], P_sb[:, c, :], xT_head[q // 4][:, c, 256 * (q % 4):256 * (q % 4) + 256],
                               start=(c == 0), stop=(c == NC - 1))
                if c == NC - 1:
                    mm.then_inc(z0_psum, 1)

            def angles(c, half):
                if c == half == 0:
                    pe.wait_ge(wf_loaded, 48)
                    pe.wait_ge(silu_ready, 1)
                for g in range(4):
                    at = 512 * g + 256 * half
                    mm = pe.matmul(ps[32 * g:32 * g + 32, 3, 256 * half:256 * half + 256], silu[:, c, :], Wf[:, c, at:at + 256],
                                   start=(c == half == 0), stop=(c == NC - 1 and half == 1), tile_position=(0, 32 * g),
                                   skip_group_check=True)
                if c == NC - 1 and half == 1:
                    mm.then_inc(v_ready, 1)

            def lower_half():
                pe.wait_ge(vparts_ready, 2)
                for b in range(B):
                    mm = pe.matmul(ps[0:D, 4, 32 * b:32 * b + 32], v_low[:, b, :], flip[0:32, 32:64], start=True, stop=True)
                mm.then_inc(lowT_psum, 1)

            def skew_matrix():
                pe.wait_ge(lowT_ready, 2)
                for b in range(B):
                    a = ps[0:D, 3, D * b:D * b + D]
                    pe.matmul(a, ident[0:32, 0:D], v_up[:, b, :], start=True, stop=False, skip_group_check=True)
                    pe.matmul(a[:, 0:32], v_up[:, b, :], neg_i[:, :], start=False, stop=False, skip_group_check=True)
                    pe.matmul(a, lowT[:, b, :], flip[:, :], start=False, stop=False, skip_group_check=True)
                    mm = pe.matmul(a[:, 32:64], flip[:, :], neg_lowT[:, b, :], start=False, stop=True, skip_group_check=True)
                mm.then_inc(skew_psum, 1)

            def expm_round(n, half):
                to, j = 3 + (n + 1) % 2, TAYLOR - n
                if n == 0 and half == 0:
                    pe.wait_ge(skew_ready, 2)
                    pe.wait_ge(const_ready, 1)
                elif half == 0:
                    pe.wait_ge(x_ready, n)
                old = ident4 if n == 0 else X[:, (n - 1) % 2, :, :]
                both = ps[0:D, to, 2 * D * half:2 * D * half + 2 * D]
                if j > 1:
                    pe.matmul(both, scaled_i[:, j - 2, :], ident4[:, 0:2, :], start=True, stop=False, skip_group_check=True)
                elif j < 1:
                    pe.matmul(both, scaled_i[:, 0, :], old[:, 2 * half:2 * half + 2, :], start=True, stop=False, skip_group_check=True)
                for m in (2 * half, 2 * half + 1):
                    left = skew if j >= 1 else old
                    mm = pe.matmul(ps[0:D, to, D * m:D * m + D], left[:, m ^ 2, :], old[:, m, :], start=(j == 1), stop=True,
                                   skip_group_check=True)
                if half == 1:
                    mm.then_inc(xp_ready, 1)

            def modulation(r, c):
                if r == c == 0:
                    pe.wait_ge(mod_loaded, 32)
                if c == 0:
                    pe.wait_ge(z0_ready, 7 + r)
                for g, blk in enumerate(range(4) if r == 0 else range(4, 6)):
                    mm = pe.matmul(ps[32 * g:32 * g + 32, 5 + r, 0:H], silu[:, c, :], w_mod_sb[:, c, H * blk:H * blk + H],
                                   start=(c == 0), stop=(c == NC - 1), tile_position=(0, 32 * g))
                if c == NC - 1:
                    mm.then_inc(mod_psum, 1)

            def modulation_columns(r):
                pe.wait_ge(modrow_ready, r + 1)
                rows = 128 if r == 0 else 64
                for c in range(2):
                    pe.transpose(ps[:, 7 - r, P128 * c:P128 * c + rows], mod_row[0:rows, r, P128 * c:P128 * c + P128], ident[0:rows, 0:rows])
                for g in range(PARTS):
                    mm = pe.matmul(ps[REM * g:REM * g + REM, 7 - r, 2 * P128:2 * P128 + rows], mod_row[0:rows, r, 2 * P128:H],
                                   ident[0:rows, 0:rows], start=True, stop=True, tile_position=(0, REM * g))
                mm.then_inc(modT_psum, 1)

            def gate_rows(r, b):
                wait(pe, gate_ready, 2 * r + b)
                if r == 0:
                    mm = pe.matmul(ps[:, 5, 0:H], ident[:, 64 + b:65 + b].broadcast_to([P128, P128]), mod_row[:, 0, :], start=True, stop=True)
                else:
                    mm = pe.matmul(ps[:, 5, 0:H], ident[0:64, 32 + b:33 + b].broadcast_to([64, P128]), mod_row[0:64, 1, :], start=True, stop=True)
                mm.then_inc(gate_psum, 1)

            for it in range(D + LAG):
                if it < D - 1:
                    update_z(it)
                if LAG <= it < D - 1 + LAG:
                    update_mn(it - LAG)
                if 6 <= it < 24:
                    head_z0((it - 6) // NC, (it - 6) % NC)
                if 24 <= it < 30:
                    angles((it - 24) // 2, it % 2)
                if 30 <= it < 36:
                    head_z0(it // NC - 4, it % NC)
                if it == 35:
                    lower_half()
                if it == 37:
                    skew_matrix()
                if 36 <= it < 36 + 2 * NC:
                    modulation((it - 36) // NC, (it - 36) % NC)
                if 39 <= it < 39 + 2 * ROUNDS:
                    expm_round((it - 39) // 2, (it - 39) % 2)
                if it in (43, 44):
                    modulation_columns(it - 43)
                if 67 <= it < 71:
                    gate_rows((it - 67) // 2, (it - 67) % 2)
            E = X[:, (ROUNDS - 1) % 2, :, :]
            pe.wait_ge(x_ready, ROUNDS)
            pe.wait_ge(winv_ready, 1)
            for b in range(B):
                mm = pe.matmul(ps[0:D, 3, D * b:D * b + D], E[:, b, :], Winv[:, :], start=True, stop=True)
            mm.then_inc(k_psum, 1)
            pe.wait_ge(k_ready, 1)
            pe.matmul(ps[0:D, 4, 0:B * D], Winv[:, :], FW, start=True, stop=True).then_inc(k_psum, 1)
            pe.wait_ge(k_ready, 2)
            pe.wait_ge(gate_ready, 4)
            for b in range(B):
                pe.matmul(ps[0:D, 5 + b, 0:H], Kt[:, b, :], Pt_sb[:, :], start=True, stop=True).then_inc(k_psum, 1)
            pe.wait_ge(k_ready, 4)

            def rotate(n, j, b):
                pe.wait_ge(zslot_ready, n + 1)
                wait(pe, xrot_ready, n)
                pe.matmul(ps[:, 0, 0:H], z_slot[:, j, :], Y[:, b, :], start=True, stop=True).then_inc(rot_ready, 1)

            def turn(n):
                pe.wait_ge(xn_ready, n + 1)
                wait(pe, xT_ready, n)
                for c in range(2):
                    pe.transpose(ps[:, 1, P128 * c:P128 * c + P128], xn[:, P128 * c:P128 * c + P128], ident[:, :])
                for g in range(PARTS):
                    mm = pe.matmul(ps[REM * g:REM * g + REM, 1, 2 * P128:3 * P128], xn[:, 2 * P128:H], ident[:, :],
                                   start=True, stop=True, tile_position=(0, REM * g))
                mm.then_inc(xT_psum, 1)

            def qkv(n, j, a):
                to, cols = ps[:, 2 + 3 * j + a, 0:H], slice(H * a, H * a + H)
                for c in range(2):
                    for i, (xs, w) in enumerate(((xT_h, wqkv_high), (xT_h, wqkv_low), (xT_l, wqkv_high))):
                        pe.matmul(to, xs[:, j, c, :], w[:, c, cols], start=(c == i == 0), stop=False)
                pe.matmul(to, xT_h[0:REM_ROWS, j, 2, :], wqkv_high[0:REM_ROWS, 2, cols], start=False, stop=True).then_inc(qkv_psum, 1)

            def bank(slot, a):
                return ps[:, 2 * slot + a, :]

            def turn_qk(g_next, h, slot):
                pe.wait_ge(split_ready, 4 * g_next + 4)
                for a in range(2):
                    to = bank(slot, a).bitcast(F16)
                    for t in range(TILES):
                        mm = pe.transpose(to[:, P128 * t:P128 * t + P128],
                                          qk_split[:, t, a, 2 * h:2 * h + 2, :].rearrange("p e r -> p (e r)"), ident16[:, :])
                mm.then_inc(t_psum, 1)

            rotate(0, 0, 0)
            rotate(1, 1, 0)
            turn(0)
            rotate(2, 0, 0)
            turn(1)
            pe.wait_ge(wqkv_split, 4)
            pe.wait_ge(ones_set, 1)

            def step_a(n, j, batch):
                pe.wait_ge(low_ready, n + 1)
                wait(pe, qkn_ready, 2 * n - 2)
                wait(pe, v_kept, n - 1)
                qkv(n, j, 0)
                qkv(n, j, 1)
                if batch[3] is not None:
                    rotate(n + 3, 1 - j, batch[3])
                if batch[2] is not None:
                    turn(n + 2)
                if isinstance(n, int) and n == NT - 1:
                    pe.wait_ge(vop_set, 3)
                    turn_qk(0, 0, 0)
                qkv(n, j, 2)

            tiles_of(pe, step_a)

            def slot_free(g, p, before, after):
                back = (p - 3) % RING_LEN
                while back not in RING_AT or back < p and (
                        RING_AT[back][0] == "O" and not before or RING_AT[back][0] == "T" and not after):
                    back = (back - 3) % RING_LEN
                kind, n = RING_AT[back]
                of = g if back < p else g - 1
                if kind == "S":
                    wait(pe, exp_done, 32 * of + n + 1)
                elif kind == "T":
                    wait(pe, op_ready, HP * of + HP + n + 1)
                else:
                    wait(pe, o_ready, of)

            def scores(g, u, par, slot):
                kt, a, h = u // 4, u // 2 % 2, u % 2
                if u < 2:
                    pe.wait_ge(op_ready, HP * g + h + 1)
                for e in range(2):
                    rows = slice(ROWS * e, ROWS * e + ROWS)
                    mm = pe.matmul(bank(slot, e), qk_op[rows, 1 - par, 1, h, P128 * kt:P128 * kt + P128],
                                   qk_op[rows, 1 - par, 0, h, 512 * a:512 * a + 512], start=True, stop=True,
                                   tile_position=(ROWS * e, 0))
                mm.then_inc(s_ready, 1)

            def weigh_v(g, w, par):
                kt, a = w // 2, w % 2
                pe.wait_ge(exp_done, 32 * g + 2 * w + 2)
                if w < 2:
                    pe.wait_ge(vop_ready, g + 1)
                    wait(pe, oacc_ready, 2 * g + a - 1)
                for h in range(HG):
                    mm = pe.matmul(ps[32 * h:32 * h + 32, 6 + a, :], v_op[:, par, kt, h, :],
                                   prob[:, (2 * w + h // 2) % 8, 512 * (h % 2):512 * (h % 2) + 512], start=(kt == 0), stop=(kt == TILES - 1),
                                   tile_position=(0, 32 * h))
                mm.then_inc(pv_done, 1)

            def turn_o(g, slot):
                pe.wait_ge(oacc_ready, 2 * g + 2)
                for t in range(TILES):
                    mm = pe.transpose(bank(slot, t // 4)[:, P128 * (t % 4):P128 * (t % 4) + P128], o_acc[:, P128 * t:P128 * t + P128],
                                      ident[:, :])
                mm.then_inc(oT_psum, 1)

            def group_b(g, par, before, after):
                for v in range(16):
                    for kind, n, p in RING_PAIRS[v]:
                        if kind == "S":
                            slot_free(g, p, before, after)
                            if not before and n == 2:
                                pe.wait_ge(qkn_ready, 2 * NT)
                                pe.wait_ge(v_kept, NT)
                            scores(g, n, par, p % 3)
                        elif kind == "T" and after:
                            slot_free(g, p, before, after)
                            turn_qk(g + 1, n, p % 3)
                        elif kind == "O" and before:
                            slot_free(g, p, before, after)
                            turn_o(g - 1, p % 3)
                        if kind == "S" and n % 2 == 1:
                            if v >= PV_LAG:
                                weigh_v(g, v - PV_LAG, par)
                            elif before:
                                weigh_v(g - 1, 16 - PV_LAG + v, 1 - par)

            pe.wait_ge(qkn_ready, 2 * NT - 2)
            turn_qk(0, 1, 1)
            group_b(0, 0, False, True)
            with pe.Fori(0, GROUPS // 2 - 1) as i:
                group_b(2 * i + 1, 1, True, True)
                group_b(2 * i + 2, 0, True, True)
            group_b(GROUPS - 1, 1, True, False)
            for w in range(16 - PV_LAG, 16):
                weigh_v(GROUPS - 1, w, 1)
            pe.wait_ge(exp_done, 32 * GROUPS)
            turn_o(GROUPS - 1, 2)

            def row_head_pe(g, h, m):
                pe.wait_ge(row_in, 3 * m + 3)
                for a in range(2):
                    for t in range(TILES):
                        mm = pe.transpose(ps[0:HD, 2 * a + t // 4, P128 * (t % 4):P128 * (t % 4) + P128], row_qk[:, a, t, :], ident[:, :])
                mm.then_inc(row_turned, 1)

            def row_tile_pe(g, h, t, n):
                pe.wait_ge(row_q_ready, n + 1)
                for a in range(2):
                    mm = pe.matmul(ps[:, 4 + a, :], row_q, row_ops[:, 1, 512 * a:512 * a + 512], start=True, stop=True)
                mm.then_inc(row_s, 1)
                pe.wait_ge(row_exp, n + 1)
                for kt in range(TILES):
                    mm = pe.transpose(ps[:, 6 + kt // 4, P128 * (kt % 4):P128 * (kt % 4) + P128], row_p[:, P128 * kt:P128 * kt + P128], ident[:, :])
                mm.then_inc(row_pt_psum, 1)
                pe.wait_ge(row_pt_ready, n + 1)
                for kt in range(TILES):
                    mm = pe.matmul(ps[:, 0, 0:HD], row_pT[:, P128 * kt:P128 * kt + P128], row_v[:, kt, :], start=(kt == 0), stop=(kt == TILES - 1))
                mm.then_inc(row_o, 1)

            def row_attention():
                pe.wait_ge(o_ready, GROUPS)
                head_rows(pe, row_head_pe, row_tile_pe)

            where_shifted(pe, row_attention)

            def c_turn_o(n, j, banks=C_BANKS):
                pe.wait_ge(orow_ready, n + 1)
                if banks == C_BANKS:
                    wait(pe, oT2_ready, n)
                for c in range(2):
                    pe.transpose(ps[:, banks[0], P128 * c:P128 * c + P128], o_row[:, j, P128 * c:P128 * c + P128], ident[:, :])
                for g in range(PARTS):
                    mm = pe.matmul(ps[REM * g:REM * g + REM, banks[0], 2 * P128:3 * P128], o_row[:, j, 2 * P128:H], ident[:, :],
                                   start=True, stop=True, tile_position=(0, REM * g))
                mm.then_inc(oT2_psum, 1)

            def c_project(n, j, banks=C_BANKS):
                pe.wait_ge(olow_ready, n + 1)
                if banks in (C_BANKS, C_SECOND):
                    wait(pe, gated_ready, n - 1)
                to = ps[:, banks[1], 0:H]
                for c in range(2):
                    for i, (xs, w) in enumerate(((oT2_h, wp_h), (oT2_h, wp_l), (oT2_l, wp_h))):
                        pe.matmul(to, xs[:, j, c, :], w[:, c, :], start=(c == i == 0), stop=False)
                pe.matmul(to, oT2_h[0:PARTS * REM, j, 2, :], wp_h[0:PARTS * REM, 2, :], start=False, stop=True).then_inc(proj_ready, 1)

            def c_turn_x(n, banks=C_BANKS):
                pe.wait_ge(xn2_ready, n + 1)
                if banks == C_BANKS:
                    wait(pe, xT2_ready, n)
                for c in range(2):
                    pe.transpose(ps[:, banks[2], P128 * c:P128 * c + P128], xn[:, P128 * c:P128 * c + P128], ident[:, :])
                for g in range(PARTS):
                    mm = pe.matmul(ps[REM * g:REM * g + REM, banks[2], 2 * P128:3 * P128], xn[:, 2 * P128:H], ident[:, :],
                                   start=True, stop=True, tile_position=(0, REM * g))
                mm.then_inc(xT2_psum, 1)

            def c_up(c_no, n0, m):
                pe.wait_ge(xsplit_ready, n0 + 2)
                if m >= 3:
                    pe.wait_ge(h_ready, FF * c_no + m - 2)
                to, cols = ps[:, 3 + m % 3, 0:CH], slice(P128 * m, P128 * m + P128)
                for c in range(2):
                    for i, (w, xs) in enumerate(((w1_h, xn2_h), (w1_h, xn2_l), (w1_l, xn2_h))):
                        pe.matmul(to, w[:, c, cols], xs[:, c, :], start=(c == i == 0), stop=False)
                pe.matmul(to, w1_h[0:PARTS * REM, 2, cols], xn2_h[0:PARTS * REM, 2, :], start=False, stop=True).then_inc(h_psum, 1)

            def c_down(c_no, j, ms):
                if ms.start == 0:
                    wait(pe, gated2_ready[j], c_no)
                tokens = slice(P128 * j, P128 * j + P128)
                for m in ms:
                    if j == 0:
                        pe.wait_ge(hl_ready, FF * c_no + m + 1)
                    for i, (h, w) in enumerate(((hid_h, w2_h), (hid_h, w2_l), (hid_l, w2_h))):
                        mm = pe.matmul(ps[:, 6 + j, 0:H], h[:, m, tokens], w[:, m, :],
                                       start=(m == i == 0), stop=(m == FF - 1 and i == 2))
                if ms.stop == FF:
                    mm.then_inc(y_psum, 1)

            pe.wait_ge(wproj_split, 2)
            for step in (c_turn_o, c_project):
                for j in range(2):
                    step(j, j, C_FIRST_BANKS[j])
            for j in range(2):
                c_turn_x(j, C_FIRST_BANKS[j])
            pe.wait_ge(w_split, 6)

            def chunk_c(c_no, n0, b, b_next):
                for m in range(FF):
                    c_up(c_no, n0, m)
                    if b_next is not None:
                        if m == 0:
                            c_turn_o(n0 + 2, 0)
                        if m == 2:
                            c_turn_o(n0 + 3, 1)
                        if m == 5:
                            c_project(n0 + 2, 0)
                        if m == 7:
                            c_project(n0 + 3, 1, C_SECOND)
                c_down(c_no, 0, range(FF))
                if b_next is not None:
                    c_turn_x(n0 + 2)
                c_down(c_no, 1, range(3))
                if b_next is not None:
                    c_turn_x(n0 + 3)
                c_down(c_no, 1, range(3, FF))

            pairs_of(pe, chunk_c)

        @block.vector
        def _(dve):
            Z, M, N = ps[:, 0, :], ps[:, 1, :], ps[:, 2, :]
            dve.wait_ge(silu_step, 3)
            dve.reciprocal(ex[:, :, :], ex[:, :, :]).then_inc(silu_step, 1)
            dve.wait_ge(silu_step, 4)
            dve.tensor_tensor(silu[:, :, 0:B], ex[:, :, :], cond_sb[:, :, :], ALU.mult).then_inc(silu_ready, 1)

            def read_diagonal():
                dve.tensor_tensor_reduce(out=junk[:, :], in0=Z[0:D, 0:D], in1=ident[0:D, 0:D], scale=1.0, scalar=0.0,
                                         op0=ALU.mult, op1=ALU.add, accum_out=diag[:, :]).then_inc(diag_ready, 1)

            def scale_r(j):
                dve.wait_ge(diagrs_ready, j + 1)
                wait(dve, w_ready, LAG * j)
                dve.tensor_scalar(R_half[:, :], Z[0:D, 0:D], diag_rs[:, 0:1], 0.5, ALU.mult, ALU.mult).then_inc(r_ready, 1)

            def z_step(k):
                dve.wait_ge(z_ready, k + 1)
                if k % LAG == LAG - 1:
                    read_diagonal()
                if k % LAG == 0 and k > 0:
                    scale_r(k // LAG - 1)
                if k == D - 1:
                    return
                if k % 8 == 0:
                    dve.wait_ge(mask_ready, k // 8 + 1)
                dve.reciprocal(z_rcp[:, :], Z[0:D, k:k + 1]).then_inc(zrcp_ready, 1)
                dve.tensor_copy(z_row[:, k + 1:k + 1 + D], Z[0:D, k + 1:k + 1 + D]).then_inc(zrow_ready, 1)
                dve.wait_ge(zrcp_ready, k + 1)
                dve.scalar_tensor_tensor(out=z_col[:, :], in0=Z[0:D, 0:D], scalar=z_rcp[:, 0:1], in1=elim_mask[:, k, :],
                                         op0=ALU.mult, op1=ALU.mult).then_inc(zcol_ready, 1)

            def m_step(k):
                dve.wait_ge(m_ready, k + 1)
                if k % LAG == 0:
                    dve.wait_ge(r_ready, k // LAG + 1)
                dve.tensor_scalar(signs[:, k:k + 1], M[0:D, k:k + 1], 0.0, -0.5, ALU.is_ge, ALU.add).then_inc(sign_step, 1)
                if k == D - 1:
                    return
                dve.wait_ge(sign_step, k + 1)
                dve.scalar_tensor_tensor(out=pivot_half[:, :], in0=M[0:D, k:k + 1], scalar=signs[:, k:k + 1],
                                         in1=R_half[:, k:k + 1], op0=ALU.mult, op1=ALU.add).then_inc(pivot_ready, 1)
                dve.scalar_tensor_tensor(out=w_row[:, k % 2, :], in0=M[0:D, 0:D], scalar=signs[:, k:k + 1], in1=R_half[:, :],
                                         op0=ALU.mult, op1=ALU.add).then_inc(w_ready, 1)
                dve.wait_ge(pivot_ready, k + 1)
                dve.reciprocal(pivot_rcp[:, :], pivot_half[:, :]).then_inc(prcp_ready, 1)
                dve.wait_ge(n_ready, k + 1)
                dve.wait_ge(prcp_ready, k + 1)
                dve.scalar_tensor_tensor(out=m_col[:, k % 2, :], in0=N[0:D, 0:D], scalar=pivot_rcp[:, 0:1],
                                         in1=elim_mask[:, k, :], op0=ALU.mult, op1=ALU.mult).then_inc(c_ready, 1)

            def weight_sum(c):
                if c == 0:
                    dve.wait_ge(wqkv_loaded, 16 * (2 + PARTS))
                rows = P128 if c < 2 else REM_ROWS
                dve.tensor_reduce(w_sum[0:rows, c, :], w_qkv_sb[0:rows, c, 0:2 * H].rearrange("p (h d) -> p h d", d=HD), AX.X,
                                  ALU.add).then_inc(wsum_ready, 1)

            def modulation_columns():
                dve.wait_ge(modT_psum, 2)
                chunks = ((P128, slice(0, 2)), (PARTS * REM, slice(2, 3)))
                for s, (bank, row) in enumerate(((7, 0), (7, 32), (7, 96), (6, 0))):
                    for rows, cs in chunks:
                        src = ps[0:rows, bank, 0:3 * P128].rearrange("p (c q) -> p c q", c=3)[:, cs, row:row + B]
                        dve.tensor_tensor(mod_cols[0:rows, s, cs, :], src,
                                          bm_cols[0:rows, s, cs].unsqueeze(2).broadcast_to([rows, cs.stop - cs.start, B]),
                                          ALU.add).then_inc(modcol_ready, 1)
                dve.wait_ge(modcol_ready, 8)
                for rows, cs in chunks:
                    dve.tensor_scalar(mod_cols[0:rows, 1:4:2, cs, :], mod_cols[0:rows, 1:4:2, cs, :], 1.0, None, ALU.add).then_inc(modcol_ready, 1)

            def gate_rows(r, b):
                dve.wait_ge(gate_psum, 2 * r + b + 1)
                if r == b == 0:
                    dve.wait_ge(row_loaded, 16 * 6)
                dve.tensor_tensor(gate[:, r, b, :], ps[:, 5, 0:H], bm_row[:, r, :], ALU.add).then_inc(gate_ready, 1)

            for it in range(D + LAG):
                if it < D:
                    z_step(it)
                if it == D:
                    scale_r(D // LAG - 1)
                if it >= LAG:
                    m_step(it - LAG)
                if it in (17, 19, 21):
                    weight_sum((it - 17) // 2)
                if it == 46:
                    modulation_columns()
                if 68 <= it < 72:
                    gate_rows((it - 68) // 2, it % 2)
            dve.wait_ge(sign_step, D)
            dve.tensor_tensor_reduce(out=junk[:, :], in0=signs[:, :], in1=ident[0:D, 0:D], scale=-2.0, scalar=0.0,
                                     op0=ALU.mult, op1=ALU.add, accum_out=sign_of[:, :]).then_inc(sign_ready, 1)
            dve.wait_ge(sign_ready, 1)
            dve.tensor_scalar(Winv[:, :], Z[0:D, D:2 * D], diag_rs[:, 0:1], sign_of[:, 0:1], ALU.mult, ALU.mult).then_inc(winv_ready, 1)

            def tile_of(n):
                return x_sb[:, bass.ds(n, 1), :].rearrange("p t f -> p (t f)")

            def split_qk(g):
                src = qkn[:, bass.ds(g, 1), :, :, :, :].rearrange("p g t a h d -> p (g t) a h d")
                part = [qk_split[:, :, :, :, HD * r:HD * r + HD] for r in range(PARTS)]
                wait(dve, t_psum, HP * g)
                for a in range(2):
                    dve.tensor_copy(part[0][:, :, a], src[:, :, a]).then_inc(split_h, 1)
                for a, low, high in ((0, 2, 1), (1, 1, 2)):
                    dve.wait_ge(split_h, 2 * g + 1 + a)
                    dve.tensor_tensor(part[low][:, :, a], src[:, :, a], part[0][:, :, a], ALU.subtract).then_inc(split_ready, 1)
                    dve.tensor_copy(part[high][:, :, a], part[0][:, :, a]).then_inc(split_ready, 1)

            def rotated(n, j, stats_of=None):
                dve.wait_ge(rot_ready, n + 1)
                if stats_of is not None:
                    dve.wait_ge(stats_ready, stats_of + 1)
                wait(dve, xkept, n - 1)
                dve.tensor_tensor(x_cur[:, j, :], ps[:, 0, 0:H], tile_of(n), ALU.add).then_inc(xrot_ready, 1)
                if stats_of is not None:
                    mean_and_variance(1 - j)
                dve.wait_ge(xrot_ready, n + 1)
                dve.bn_stats(stats[:, j, :], x_cur[:, j, :]).then_inc(stats_ready, 1)

            def mean_and_variance(j):
                dve.bn_aggr(mean_var[:, j, :], stats[:, j, :]).then_inc(mv_ready, 1)

            def normalise(n, j, stats_of=None):
                dve.wait_ge(rstd_ready, n + 1)
                wait(dve, xT_psum, n)
                if stats_of is not None:
                    dve.wait_ge(stats_ready, stats_of + 1)
                dve.tensor_scalar(xn[:, :], x_cur[:, j, :], mean_var[:, j, 0:1], rstd[:, j:j + 1], ALU.subtract, ALU.mult).then_inc(xn_ready, 1)

            def square_sums(n):
                dve.wait_ge(sq_ready, n + 1)
                dve.tensor_reduce(head_ssq, qk_sq.rearrange("p a (h d) -> p (a h) d", d=HD), AX.X, ALU.add).then_inc(ssq_ready, 1)

            def head_norms(n, t, j, b):
                dve.wait_ge(hsd_ready, n + 1)
                wait(dve, qkn_ready, 2 * n)
                dve.reciprocal(head_rstd, head_sd).then_inc(hrstd_ready, 1)
                dve.wait_ge(hrstd_ready, n + 1)
                for a, src in enumerate((ps[:, 2 + 3 * j, 0:H], ps[:, 3 + 3 * j, 0:H])):
                    dve.tensor_tensor(qkn[:, 4 * b:4 * b + 4, bass.ds(t, 1), a, :, :].rearrange("p g t h d -> p g (t h) d"),
                                      src.rearrange("p (g h d) -> p g h d", g=4, h=HG),
                                      head_rstd[:, 16 * a:16 * a + 16].rearrange("p (g h) -> p g h", g=4).unsqueeze(3)
                                      .broadcast_to([P128, 4, HG, HD]), ALU.mult).then_inc(qkn_ready, 1)

            dve.wait_ge(rows_ready, 2)
            dve.tensor_tensor(xn[:, :], g_row[:, :], g_row[:, :], ALU.mult).then_inc(g_step, 1)
            dve.wait_ge(g_step, 1)
            dve.tensor_reduce(var_eps[:, 0:1], xn[:, :], AX.X, ALU.max).then_inc(g_step, 1)
            dve.wait_ge(g_step, 2)
            bound = HD * SCORE_BOUND ** 2
            dve.tensor_scalar(unshifted_ok[:, :], var_eps[0:1, 0:1], bound, None, ALU.is_le).then_inc(flag_ready, 1)
            dve.tensor_scalar(q_factor[:, :], var_eps[:, 0:1], bound, None, ALU.is_le).then_inc(flag_ready, 1)
            dve.wait_ge(flag_ready, 2)

            dve.wait_ge(x_loaded, 16 * B)
            def read_operands(g, par, h, slot):
                dve.wait_ge(t_psum, HP * g + h + 1)
                dve.tensor_scalar(qk_op[:, 1 - par, 0, h, :], ps[:, 2 * slot, :].bitcast(F16), q_factor[:, :], None, ALU.mult)
                ins = dve.tensor_copy(qk_op[:, 1 - par, 1, h, :], ps[:, 2 * slot + 1, :].bitcast(F16))
                ins.then_inc(op_ready, 1)

            rotated(0, 0)
            rotated(1, 1, 0)
            normalise(0, 0, 1)
            mean_and_variance(1)
            rotated(2, 0)
            normalise(1, 1, 2)
            mean_and_variance(0)
            normalise(2, 0)

            def step_a(n, j, batch):
                after = batch[3] is not None
                if after:
                    rotated(n + 3, 1 - j)
                    dve.wait_ge(stats_ready, n + 4)
                square_sums(n)
                if isinstance(n, int) and n == NT - 1:
                    for h in range(HP):
                        read_operands(0, 0, h, h)
                if after:
                    mean_and_variance(1 - j)
                head_norms(n, n - TILES * batch[0], j, batch[0])
                if after:
                    normalise(n + 3, 1 - j)
                if isinstance(n, int) and n == TILES:
                    dve.wait_ge(kg_ready, TILES)
                    split_qk(0)

            tiles_of(dve, step_a)

            def read_output(g):
                for a in range(2):
                    dve.wait_ge(pv_done, 16 * g + 15 + a)
                    dve.tensor_copy(o_acc[:, 512 * a:512 * a + 512], ps[:, 6 + a, :]).then_inc(oacc_ready, 1)

            def divide_output(g, slot):
                dve.wait_ge(oT_psum, g + 1)
                src = ps[:, 2 * slot:2 * slot + 2, :].rearrange("p a (t h d) -> p (a t) h d", h=HG, d=32)
                dve.reciprocal(den_inv[:, :, :].unsqueeze(3), src[:, :, :, HD:HD + 1]).then_inc(den_ready, 1)
                dve.wait_ge(den_ready, g + 1)
                dve.tensor_tensor(o_tok[:, bass.ds(g, 1), :, :].rearrange("p g t (h d) -> p (g t) h d", d=HD), src[:, :, :, 0:HD],
                                  den_inv[:, :, :].unsqueeze(3).broadcast_to([P128, TILES, HG, HD]), ALU.mult).then_inc(o_ready, 1)

            units = [(kind, n, p % 3) for pair in RING_PAIRS for kind, n, p in pair if kind != "S"]

            def group_b(g, par, before, after):
                if before:
                    read_output(g - 1)
                for kind, n, slot in units:
                    if kind == "T" and after:
                        if n == 0:
                            split_qk(g + 1)
                        read_operands(g + 1, 1 - par, n, slot)
                    if kind == "O" and before:
                        divide_output(g - 1, slot)

            def split_weights():
                low = slice(REM, 2 * REM)
                dve.wait_ge(proj_loaded, 16 * (2 + PARTS))
                dve.tensor_scalar(wp_h[0:PARTS * REM, 2, :], w_proj_sb[0:PARTS * REM, 2, :], W_SCALE, None, ALU.mult).then_inc(wproj_half, 1)
                dve.tensor_scalar(wp_h[:, 0:2, :], w_proj_sb[:, 0:2, :], W_SCALE, None, ALU.mult).then_inc(wproj_half, 1)
                dve.wait_ge(wproj_half, 2)
                dve.scalar_tensor_tensor(out=wp_h[low, 2, :], in0=w_proj_sb[low, 2, :], scalar=W_SCALE, in1=wp_h[low, 2, :],
                                         op0=ALU.mult, op1=ALU.subtract).then_inc(wproj_split, 1)
                dve.scalar_tensor_tensor(out=wp_l, in0=w_proj_sb[:, 0:2, :], scalar=W_SCALE, in1=wp_h[:, 0:2, :],
                                         op0=ALU.mult, op1=ALU.subtract).then_inc(wproj_split, 1)
                dve.wait_ge(w1_loaded, 16 * (1 + PARTS))
                dve.tensor_scalar(w1_h[0:PARTS * REM, 2, :], w1_sb[0:PARTS * REM, 2, :], W_SCALE, None, ALU.mult).then_inc(w_half, 1)
                dve.tensor_scalar(w1_h[:, 0:2, :], w1_sb[:, 0:2, :], W_SCALE, None, ALU.mult).then_inc(w_half, 1)
                dve.wait_ge(w_half, 2)
                dve.scalar_tensor_tensor(out=w1_h[low, 2, :], in0=w1_sb[low, 2, :], scalar=W_SCALE, in1=w1_h[low, 2, :],
                                         op0=ALU.mult, op1=ALU.subtract).then_inc(w_split, 1)
                for c in range(2):
                    dve.scalar_tensor_tensor(out=w1_l[:, c, :], in0=w1_sb[:, c, :], scalar=W_SCALE, in1=w1_h[:, c, :],
                                             op0=ALU.mult, op1=ALU.subtract).then_inc(w_split, 1)
                dve.wait_ge(w2_loaded, 16)
                dve.tensor_scalar(w2_h, w2_sb, W_SCALE, None, ALU.mult).then_inc(w_half, 1)
                dve.wait_ge(w_half, 3)
                for ms in (slice(0, 3), slice(3, 6), slice(6, 9)):
                    dve.scalar_tensor_tensor(out=w2_l[:, ms, :], in0=w2_sb[:, ms, :], scalar=W_SCALE, in1=w2_h[:, ms, :],
                                             op0=ALU.mult, op1=ALU.subtract).then_inc(w_split, 1)

            dve.wait_ge(kg_ready, NT)
            group_b(0, 0, False, True)
            with dve.Fori(0, GROUPS // 2 - 1) as i:
                group_b(2 * i + 1, 1, True, True)
                group_b(2 * i + 2, 0, True, True)
            group_b(GROUPS - 1, 1, True, False)
            dve.wait_ge(vop_ready, GROUPS)
            where(dve, False, split_weights)
            read_output(GROUPS - 1)
            divide_output(GROUPS - 1, 2)

            def row_head_dve(g, h, m):
                for a in range(2):
                    dve.tensor_copy(row_qk[:, a, :, :].unsqueeze(2),
                                    qkn[:, bass.ds(g, 1), :, a, bass.ds(h, 1), :].rearrange("p g t h d -> p (g t) h d")).then_inc(row_in, 1)
                dve.tensor_copy(row_v.unsqueeze(2), v_all[:, bass.ds(g, 1), :, bass.ds(h, 1), :].rearrange("p g t h d -> p (g t) h d")).then_inc(row_in, 1)
                dve.wait_ge(row_turned, m + 1)
                dve.tensor_copy(row_ops, ps[0:HD, 0:4, :].rearrange("p (a s) t -> p a (s t)", a=2)).then_inc(row_ops_ready, 1)

            def row_tile_dve(g, h, t, n):
                dve.wait_ge(row_ops_ready, HG * g + h + 1)
                dve.tensor_copy(row_q, row_ops[:, 0, :].rearrange("p (t q) -> p t q", q=P128)[:, bass.ds(t, 1), :].rearrange("p t q -> p (t q)")).then_inc(row_q_ready, 1)
                dve.wait_ge(row_s, n + 1)
                dve.tensor_reduce(row_max, ps[:, 4:6, :].rearrange("p a q -> p (a q)"), AX.X, ALU.max).then_inc(row_max_ready, 1)
                dve.wait_ge(row_max_ready, n + 1)
                dve.tensor_scalar(row_shift, row_max, -HD ** -0.5, None, ALU.mult).then_inc(row_shift_ready, 1)
                dve.wait_ge(row_pt_psum, n + 1)
                dve.tensor_copy(row_pT, ps[:, 6:8, :].rearrange("p a q -> p (a q)")).then_inc(row_pt_ready, 1)
                dve.wait_ge(row_exp, n + 1)
                dve.reciprocal(row_rcp, row_den).then_inc(row_rcp_ready, 1)
                dve.wait_ge(row_rcp_ready, n + 1)
                dve.wait_ge(row_o, n + 1)
                dve.tensor_scalar(o_tok[:, bass.ds(g, 1), bass.ds(t, 1), :].rearrange("p g t (h d) -> p (g t h) d", d=HD)[:, bass.ds(h, 1), :]
                                  .rearrange("p h d -> p (h d)"), ps[:, 0, 0:HD], row_rcp, None, ALU.mult).then_inc(row_done, 1)

            def row_attention():
                head_rows(dve, row_head_dve, row_tile_dve)
                split_weights()

            where_shifted(dve, row_attention)

            def c_gate(n, b, stats_of, banks=C_BANKS):
                dve.wait_ge(proj_ready, n + 1)
                wait(dve, x2_ready, n)
                if stats_of is not None:
                    dve.wait_ge(stats2_ready, stats_of + 1)
                dve.scalar_tensor_tensor(out=gated, in0=ps[:, banks[1], 0:H], scalar=1.0 / W_SCALE, in1=gate[:, 0, b, :],
                                         op0=ALU.mult, op1=ALU.mult).then_inc(gated_ready, 1)

            def c_add(n, j, uses):
                dve.wait_ge(gated_ready, n + 1)
                dve.wait_ge(xgb_ready, n + 1)
                wait(dve, xgb2_ready[j], uses)
                dve.tensor_tensor(x_cur[:, j, :], gated, x_gb[:, j, :], ALU.add).then_inc(x2_ready, 1)
                dve.wait_ge(x2_ready, n + 1)
                dve.bn_stats(stats[:, j, :], x_cur[:, j, :]).then_inc(stats2_ready, 1)

            def c_mean_and_variance(j):
                dve.bn_aggr(mean_var[:, j, :], stats[:, j, :]).then_inc(mv2_ready, 1)

            def c_normalise(n, j, stats_of):
                dve.wait_ge(rstd2_ready, n + 1)
                wait(dve, xT2_psum, n)
                if stats_of is not None:
                    dve.wait_ge(stats2_ready, stats_of + 1)
                dve.tensor_scalar(xn[:, :], x_cur[:, j, :], mean_var[:, j, 0:1], rstd[:, j:j + 1], ALU.subtract, ALU.mult).then_inc(xn2_ready, 1)

            def split_x(n, j):
                dve.wait_ge(xT2_ready, n + 1)
                cols, low = slice(P128 * j, P128 * j + P128), slice(2 * REM, 3 * REM)
                dve.tensor_copy(xn2_h[0:PARTS * REM, 2, cols], xn2T[0:PARTS * REM, 2, cols]).then_inc(xh_ready, 1)
                dve.tensor_copy(xn2_h[:, 0:2, cols], xn2T[:, 0:2, cols]).then_inc(xh_ready, 1)
                dve.wait_ge(xh_ready, 2 * n + 2)
                dve.tensor_tensor(xn2_h[low, 2, cols], xn2T[low, 2, cols], xn2_h[low, 2, cols], ALU.subtract)
                dve.tensor_tensor(xn2_l[:, :, cols], xn2T[:, 0:2, cols], xn2_h[:, 0:2, cols], ALU.subtract).then_inc(xsplit_ready, 1)

            def split_hid(c_no, m):
                dve.wait_ge(h_ready, FF * c_no + m + 1)
                dve.tensor_copy(hid_h[:, m, :], hid[:, m, :]).then_inc(hh_ready, 1)
                dve.wait_ge(hh_ready, FF * c_no + m + 1)
                dve.tensor_tensor(hid_l[:, m, :], hid[:, m, :], hid_h[:, m, :], ALU.subtract).then_inc(hl_ready, 1)

            def c_first(n0, b, uses):
                c_gate(n0, b, None)
                c_add(n0, 0, uses)

            def c_second(n0, b, uses, banks=C_BANKS):
                c_gate(n0 + 1, b, n0, banks)
                c_mean_and_variance(0)
                c_add(n0 + 1, 1, uses)
                c_normalise(n0, 0, n0 + 1)
                c_mean_and_variance(1)

            def c_result(n, j, b, c_no):
                dve.wait_ge(y_psum, n + 1)
                dve.scalar_tensor_tensor(out=gated2[:, j, :], in0=ps[:, 6 + j, 0:H], scalar=1.0 / W_SCALE, in1=gate[:, 1, b, :],
                                         op0=ALU.mult, op1=ALU.mult).then_inc(gated2_ready[j], 1)
                dve.wait_ge(gated2_ready[j], c_no + 1)
                dve.wait_ge(xgb2_ready[j], c_no + 1)
                wait(dve, y_stored[j], 16 * c_no)
                dve.tensor_tensor(y_out[:, j, :], gated2[:, j, :], x_gb2[:, j, :], ALU.add).then_inc(y_ready[j], 1)

            c_first(0, 0, 0)
            c_second(0, 0, 0, C_FIRST_BANKS[1])
            c_normalise(1, 1, None)
            for j in range(2):
                split_x(j, j)

            def chunk_c(c_no, n0, b, b_next):
                for m in range(FF):
                    split_hid(c_no, m)
                    if b_next is not None and m == 5:
                        c_first(n0 + 2, b_next, c_no + 1)
                if b_next is not None:
                    c_second(n0 + 2, b_next, c_no + 1, C_SECOND)
                c_result(n0, 0, b, c_no)
                if b_next is not None:
                    c_normalise(n0 + 3, 1, None)
                    for j in range(2):
                        split_x(n0 + 2 + j, j)
                c_result(n0 + 1, 1, b, c_no)

            pairs_of(dve, chunk_c)


def fold_index():
    place = np.full((D, D), -1)
    rows, cols = np.triu_indices(D, 1)
    place[rows, cols] = np.arange(len(rows))
    index = np.full((D // 2, D), len(rows))
    for r in range(D // 2):
        index[r, r + 1:] = place[r, r + 1:]
        index[r, :r] = place[D - 1 - r, D - 1 - np.arange(r)]
    return index


def rows_of_128(vectors):
    full = vectors[:, :2 * P128].reshape(-1, 2, P128)
    rest = np.tile(vectors[:, 2 * P128:], (1, 4))[:, None, :]
    return np.concatenate([full, rest], axis=1).transpose(2, 0, 1)


def kernel(**inputs):
    import concourse.bacc as bacc
    from concourse.bass_utils import run_bass_kernel_spmd

    a = {k: np.asarray(v) for k, v in inputs.items()}
    index = fold_index()
    W = np.concatenate([a["L0_cond_W"], np.zeros((1, H), a["L0_cond_W"].dtype)])
    b = np.concatenate([a["L0_cond_b"], np.zeros(1, a["L0_cond_b"].dtype)])
    arrays = {
        "x": a["x"],
        "x_t": a["x"].transpose(0, 2, 1),
        "cond_t": a["cond_1152"].T,
        "P": a["L0_cond_P"],
        "P_t": a["L0_cond_P"].T,
        "W_fold": W[index.ravel()].T,
        "b_fold": b[index],
        "w_mod": a["L1_cond_w_mod"],
        "b_mod_cols": rows_of_128(a["L1_cond_b_mod"].reshape(6, H)[[SH_MSA, SC_MSA, SH_MLP, SC_MLP]]),
        "b_mod": a["L1_cond_b_mod"],
        "w_qkv": a["L1_cond_w_qkv"],
        "b_qkv": a["L1_cond_b_qkv"],
        "g_q": a["L1_cond_g_q"],
        "g_k": a["L1_cond_g_k"],
        "w_proj": a["L1_cond_w_proj"],
        "b_proj": a["L1_cond_b_proj"],
        "w1": a["L1_cond_w1"],
        "b1_cols": a["L1_cond_b1"].reshape(FF, P128).T,
        "w2": a["L1_cond_w2"],
        "b2": a["L1_cond_b2"],
    }
    arrays = {f"in_{k}": np.ascontiguousarray(v) for k, v in arrays.items()}
    nc = bacc.Bacc("TRN2", target_bir_lowering=False, num_devices=1)
    args = [nc.dram_tensor(k, v.shape, mybir.dt.from_np(v.dtype), kind="ExternalInput").ap() for k, v in arrays.items()]
    out = nc.dram_tensor("out", (B, T, H), F32, kind="ExternalOutput").ap()
    build(nc, *args, out)
    r = run_bass_kernel_spmd(nc, [arrays], core_ids=[0])
    return r.results[0]["out"]
```
